# Optimizing a Trainium2 kernel written in Bass

```python
import numpy as np
import jax
import jax.numpy as jnp

def _softmax(x, axis=-1):
    return jax.nn.softmax(x, axis=axis)

def _gelu(x):
    return jax.nn.gelu(x, approximate=True)

def _silu(x):
    return jax.nn.silu(x)

def _sigmoid(x):
    return jax.nn.sigmoid(x)

def _layernorm(x, axis=-1, eps=1e-05):
    m = jnp.mean(x, axis=axis, keepdims=True)
    v = jnp.var(x, axis=axis, keepdims=True)
    return (x - m) / jnp.sqrt(v + eps)

def _scatter_add(tgt, idx, src, axis=0):
    return tgt.at[idx].add(src)

def _segment_sum(src, seg, n):
    return jax.ops.segment_sum(src, seg, n)
kernel_name = 'mk_cond_resid_d4_seqx_r4_f94809'

def setup_inputs(seed: int=0):
    np.random.seed(seed)
    _w = jnp.asarray

    def _rec_inputs():
        import jax
        import jax.numpy as jnp
        _rk = jax.random.key(seed)
        x = 7.971e-05 + 1 * jax.random.normal(jax.random.fold_in(_rk, 1), (8, 512, 256), jnp.float32)
        _lenS = 512 - jax.random.randint(jax.random.fold_in(_rk, 7), (8,), 0, max(1, 512 // 4) + 1, jnp.int32)
        _lenS2 = 512 - jax.random.randint(jax.random.fold_in(_rk, 8), (8,), 0, max(1, 512 // 4) + 1, jnp.int32)
        itok_B_0_6 = jax.random.randint(jax.random.fold_in(_rk, 11), (8,), 0, 7, jnp.int32)
        itok_B_0_2 = jax.random.randint(jax.random.fold_in(_rk, 12), (8,), 0, 3, jnp.int32)
        itok_Sx32_0_1023 = jax.random.randint(jax.random.fold_in(_rk, 14), (512, 32), 0, 256, jnp.int32)
        condB_uprev = -0.456674 + 0.753242 * jax.random.normal(jax.random.fold_in(_rk, 16), (8,), jnp.float32)
        itok_B_0_8 = jax.random.randint(jax.random.fold_in(_rk, 17), (8,), 0, 9, jnp.int32)
        _validS = jnp.arange(512)[None, :] < _lenS[:, None]
        _validS2 = jnp.arange(512)[None, :] < _lenS2[:, None]
        _causal = jnp.tril(jnp.ones((512, 512), dtype=bool))
        mask_SxS_bk0 = jnp.logical_not(jnp.broadcast_to(_validS[0:1, :], (512, 512)))
        mask_Sx32_bk1 = jnp.ones((512, 32), dtype=bool)
        return (x, itok_B_0_6, itok_B_0_2, itok_Sx32_0_1023, condB_uprev, itok_B_0_8, mask_SxS_bk0, mask_Sx32_bk1)
    x, itok_B_0_6, itok_B_0_2, itok_Sx32_0_1023, condB_uprev, itok_B_0_8, mask_SxS_bk0, mask_Sx32_bk1 = _rec_inputs()

    def _L0_cond_setup():
        import jax, jax.numpy as jnp
        import numpy as np
        N_PROFILES = 8
        HIDDEN = 256
        BOTTLENECK = 128
        EPS = 1e-05
        key = jax.random.key(seed)
        ks = jax.random.split(key, 8)
        B, S, H, K, P = (16, 512, HIDDEN, BOTTLENECK, N_PROFILES)
        down_w = jax.random.normal(ks[0], (P, H, K), dtype=jnp.float32) * (1.0 / np.sqrt(H))
        down_b = jax.random.normal(ks[1], (P, K), dtype=jnp.float32) * 0.01
        up_w = jax.random.normal(ks[2], (P, K, H), dtype=jnp.float32) * (1.0 / np.sqrt(K))
        up_b = jax.random.normal(ks[3], (P, H), dtype=jnp.float32) * 0.01
        ln_g = jnp.ones((P, H), dtype=jnp.float32)
        ln_b = jnp.zeros((P, H), dtype=jnp.float32)
        hidden = jax.random.normal(ks[4], (B, S, H), dtype=jnp.float32)
        profile_ids = jax.random.randint(ks[5], (B,), 0, P)
        return {'hidden': hidden, 'profile_ids': profile_ids, 'down_w': down_w, 'down_b': down_b, 'up_w': up_w, 'up_b': up_b, 'ln_g': ln_g, 'ln_b': ln_b}
    _L0_cond_all = _L0_cond_setup()
    _L0_cond_in = {k: v for k, v in _L0_cond_all.items() if k in ('down_w', 'down_b', 'up_w', 'up_b', 'ln_g', 'ln_b')}
    del _L0_cond_all

    def _L1_cond_setup():
        import jax, jax.numpy as jnp
        import numpy as np
        NEG_INF = -1e+30
        key = jax.random.key(seed)
        k1, k2, k3, k4, k5 = jax.random.split(key, 5)
        B, S, D, A = (16, 256, 256, 64)
        hidden = jax.random.normal(k1, (B, S, D), dtype=jnp.float32)
        W1 = jax.random.normal(k2, (D, A), dtype=jnp.float32) / np.sqrt(D)
        b1 = jax.random.normal(k3, (A,), dtype=jnp.float32) * 0.01
        v = jax.random.normal(k4, (A,), dtype=jnp.float32) / np.sqrt(A)
        prompt_type_ids = jax.random.randint(k5, (B,), 0, 3, dtype=jnp.int32)
        return {'hidden': hidden, 'W1': W1, 'b1': b1, 'v': v, 'prompt_type_ids': prompt_type_ids}
    _L1_cond_all = _L1_cond_setup()
    _L1_cond_in = {k: v for k, v in _L1_cond_all.items() if k in ('W1', 'b1', 'v')}
    del _L1_cond_all

    def _L2_cond_setup():
        import jax, jax.numpy as jnp
        import numpy as np
        B, S, D, H = (4, 256, 256, 16)
        DH = D // H
        K_SPARSE = 32
        LAMBDA_MAX, ALPHA = (10.0, 5.0)
        SPARSE_THRESHOLD = 1.0
        key = jax.random.key(seed)
        ks = jax.random.split(key, 12)
        x = jax.random.normal(ks[0], (B, S, D), dtype=jnp.float32)
        prior_mask = jax.random.bernoulli(ks[1], 0.1, (S, S))
        prior_indices = jax.random.randint(ks[2], (S, K_SPARSE), 0, S)
        prior_index_mask = jax.random.bernoulli(ks[3], 0.9, (S, K_SPARSE))
        prior_index_mask = prior_index_mask.at[:, 0].set(True)
        u_prev = jax.random.normal(ks[4], (B, 1), dtype=jnp.float32)
        sc = 1.0 / np.sqrt(D)
        Wq = jax.random.normal(ks[5], (D, D), dtype=jnp.float32) * sc
        Wk = jax.random.normal(ks[6], (D, D), dtype=jnp.float32) * sc
        Wv = jax.random.normal(ks[7], (D, D), dtype=jnp.float32) * sc
        Wo = jax.random.normal(ks[8], (D, D), dtype=jnp.float32) * sc
        bq = jnp.zeros((D,), jnp.float32)
        bk = jnp.zeros((D,), jnp.float32)
        bv = jnp.zeros((D,), jnp.float32)
        bo = jnp.zeros((D,), jnp.float32)
        return {'x': x, 'prior_mask': prior_mask, 'prior_indices': prior_indices, 'prior_index_mask': prior_index_mask, 'u_prev': u_prev, 'Wq': Wq, 'bq': bq, 'Wk': Wk, 'bk': bk, 'Wv': Wv, 'bv': bv, 'Wo': Wo, 'bo': bo}
    _L2_cond_all = _L2_cond_setup()
    _L2_cond_in = {k: v for k, v in _L2_cond_all.items() if k in ('Wq', 'bq', 'Wk', 'bk', 'Wv', 'bv', 'Wo', 'bo')}
    del _L2_cond_all

    def _L3_cond_setup():
        import jax, jax.numpy as jnp
        import numpy as np
        LN_EPS = 1e-05
        key = jax.random.key(seed)
        ks = jax.random.split(key, 8)
        B, S, H, A, L = (32, 512, 256, 64, 10)
        return {'hidden_states': jax.random.normal(ks[0], (B, S, H), dtype=jnp.float32), 'language_ids': jax.random.randint(ks[1], (B,), 0, L, dtype=jnp.int64), 'W1': jax.random.normal(ks[2], (L, H, A), dtype=jnp.float32) * (1.0 / np.sqrt(H)), 'b1': jnp.zeros((L, A), dtype=jnp.float32), 'W2': jax.random.normal(ks[3], (L, A, H), dtype=jnp.float32) * (1.0 / np.sqrt(A)), 'b2': jnp.zeros((L, H), dtype=jnp.float32), 'gamma': jnp.ones((L, H), dtype=jnp.float32), 'beta': jnp.zeros((L, H), dtype=jnp.float32)}
    _L3_cond_all = _L3_cond_setup()
    _L3_cond_in = {k: v for k, v in _L3_cond_all.items() if k in ('W1', 'b1', 'W2', 'b2', 'gamma', 'beta')}
    del _L3_cond_all
    return {'x': x, 'itok_B_0_6': itok_B_0_6, 'itok_B_0_2': itok_B_0_2, 'itok_Sx32_0_1023': itok_Sx32_0_1023, 'condB_uprev': condB_uprev, 'itok_B_0_8': itok_B_0_8, 'mask_SxS_bk0': mask_SxS_bk0, 'mask_Sx32_bk1': mask_Sx32_bk1, 'L0_cond_down_w': _L0_cond_in['down_w'], 'L0_cond_down_b': _L0_cond_in['down_b'], 'L0_cond_up_w': _L0_cond_in['up_w'], 'L0_cond_up_b': _L0_cond_in['up_b'], 'L0_cond_ln_g': _L0_cond_in['ln_g'], 'L0_cond_ln_b': _L0_cond_in['ln_b'], 'L1_cond_W1': _L1_cond_in['W1'], 'L1_cond_b1': _L1_cond_in['b1'], 'L1_cond_v': _L1_cond_in['v'], 'L2_cond_Wq': _L2_cond_in['Wq'], 'L2_cond_bq': _L2_cond_in['bq'], 'L2_cond_Wk': _L2_cond_in['Wk'], 'L2_cond_bk': _L2_cond_in['bk'], 'L2_cond_Wv': _L2_cond_in['Wv'], 'L2_cond_bv': _L2_cond_in['bv'], 'L2_cond_Wo': _L2_cond_in['Wo'], 'L2_cond_bo': _L2_cond_in['bo'], 'L3_cond_W1': _L3_cond_in['W1'], 'L3_cond_b1': _L3_cond_in['b1'], 'L3_cond_W2': _L3_cond_in['W2'], 'L3_cond_b2': _L3_cond_in['b2'], 'L3_cond_gamma': _L3_cond_in['gamma'], 'L3_cond_beta': _L3_cond_in['beta']}

def reference(x, itok_B_0_6, itok_B_0_2, itok_Sx32_0_1023, condB_uprev, itok_B_0_8, mask_SxS_bk0, mask_Sx32_bk1, L0_cond_down_w, L0_cond_down_b, L0_cond_up_w, L0_cond_up_b, L0_cond_ln_g, L0_cond_ln_b, L1_cond_W1, L1_cond_b1, L1_cond_v, L2_cond_Wq, L2_cond_bq, L2_cond_Wk, L2_cond_bk, L2_cond_Wv, L2_cond_bv, L2_cond_Wo, L2_cond_bo, L3_cond_W1, L3_cond_b1, L3_cond_W2, L3_cond_b2, L3_cond_gamma, L3_cond_beta):
    import jax
    import jax.numpy as jnp

    def _L0_cond_ref(hidden, profile_ids, down_w, down_b, up_w, up_b, ln_g, ln_b):
        import jax, jax.numpy as jnp
        import numpy as np
        N_PROFILES = 8
        HIDDEN = 256
        BOTTLENECK = 128
        EPS = 1e-05
        Wd = down_w[profile_ids]
        bd = down_b[profile_ids][:, None]
        Wu = up_w[profile_ids]
        bu = up_b[profile_ids][:, None]
        g = ln_g[profile_ids][:, None]
        b = ln_b[profile_ids][:, None]
        z = jax.nn.relu(jnp.einsum('bsh,bhk->bsk', hidden, Wd) + bd)
        y = hidden + jnp.einsum('bsk,bkh->bsh', z, Wu) + bu
        mu = jnp.mean(y, axis=-1, keepdims=True)
        var = jnp.mean(jnp.square(y - mu), axis=-1, keepdims=True)
        return (y - mu) * jax.lax.rsqrt(var + EPS) * g + b

    def _L1_cond_ref(hidden, W1, b1, v, prompt_type_ids):
        import jax, jax.numpy as jnp
        import numpy as np
        NEG_INF = -1e+30
        B, S, D = hidden.shape
        attn_in = jnp.tanh(jnp.einsum('bsd,da->bsa', hidden, W1) + b1)
        scores = jnp.einsum('bsa,a->bs', attn_in, v)
        idx = jnp.arange(S)
        j = idx[:, None]
        l = idx[None, :]
        prefix_m = l <= j
        postfix_m = l >= j
        cloze_m = l != j
        pt = prompt_type_ids[:, None, None]
        mask = jnp.where(pt == 0, prefix_m[None], jnp.where(pt == 1, postfix_m[None], cloze_m[None]))
        masked_scores = jnp.where(mask, scores[:, None, :], NEG_INF)
        p = jax.nn.softmax(masked_scores, axis=-1)
        cnt = jnp.sum(mask, axis=-1).astype(hidden.dtype)
        pooled = jnp.einsum('bjl,bld->bjd', p, hidden) / cnt[..., None]
        return pooled

    def _L2_cond_ref(x, prior_mask, prior_indices, prior_index_mask, u_prev, Wq, bq, Wk, bk, Wv, bv, Wo, bo):
        import jax, jax.numpy as jnp
        import numpy as np
        B, S, D, H = (4, 256, 256, 16)
        DH = D // H
        K_SPARSE = 32
        LAMBDA_MAX, ALPHA = (10.0, 5.0)
        SPARSE_THRESHOLD = 1.0
        Bb, Ss, Dd = x.shape
        scale = 1.0 / jnp.sqrt(jnp.asarray(DH, x.dtype))

        def proj(W, b):
            return (x @ W.T + b).reshape(Bb, Ss, H, DH).transpose(0, 2, 1, 3)
        Q, K, V = (proj(Wq, bq), proj(Wk, bk), proj(Wv, bv))
        lam = LAMBDA_MAX * jnp.exp(-ALPHA * u_prev.reshape(Bb))
        use_sparse = lam >= SPARSE_THRESHOLD
        scores = jnp.einsum('bhqd,bhkd->bhqk', Q, K) * scale
        prior_bias = jnp.where(prior_mask[:Ss, :Ss], 0.0, -1.0).astype(x.dtype)
        bias = lam[:, None, None, None] * prior_bias[None, None]
        dense_out = jnp.einsum('bhqk,bhkd->bhqd', jax.nn.softmax(scores + bias, axis=-1), V)
        idx = prior_indices[:Ss]
        Kg = K[:, :, idx]
        Vg = V[:, :, idx]
        s_scores = jnp.einsum('bhsd,bhskd->bhsk', Q, Kg) * scale
        s_scores = jnp.where(prior_index_mask[:Ss][None, None], s_scores, jnp.asarray(-jnp.inf, x.dtype))
        sparse_out = jnp.einsum('bhsk,bhskd->bhsd', jax.nn.softmax(s_scores, axis=-1), Vg)
        out = jnp.where(use_sparse[:, None, None, None], sparse_out, dense_out)
        out = out.transpose(0, 2, 1, 3).reshape(Bb, Ss, Dd)
        return out @ Wo.T + bo

    def _L3_cond_ref(hidden_states, language_ids, W1, b1, W2, b2, gamma, beta):
        import jax, jax.numpy as jnp
        import numpy as np
        LN_EPS = 1e-05
        w1 = W1[language_ids]
        w2 = W2[language_ids]
        h = jnp.einsum('bsh,bha->bsa', hidden_states, w1) + b1[language_ids][:, None, :]
        h = jax.nn.relu(h)
        adapted = jnp.einsum('bsa,bah->bsh', h, w2) + b2[language_ids][:, None, :]
        x = hidden_states + adapted
        mean = jnp.mean(x, axis=-1, keepdims=True)
        var = jnp.mean(jnp.square(x - mean), axis=-1, keepdims=True)
        normed = (x - mean) * jax.lax.rsqrt(var + LN_EPS)
        return normed * gamma[language_ids][:, None, :] + beta[language_ids][:, None, :]
    x = x + _L0_cond_ref(x, itok_B_0_6, L0_cond_down_w, L0_cond_down_b, L0_cond_up_w, L0_cond_up_b, L0_cond_ln_g, L0_cond_ln_b)
    x = x + _L1_cond_ref(x, L1_cond_W1, L1_cond_b1, L1_cond_v, itok_B_0_2)
    x = x + _L2_cond_ref(x, mask_SxS_bk0, itok_Sx32_0_1023, mask_Sx32_bk1, condB_uprev[:, None], L2_cond_Wq, L2_cond_bq, L2_cond_Wk, L2_cond_bk, L2_cond_Wv, L2_cond_bv, L2_cond_Wo, L2_cond_bo)
    x = x + _L3_cond_ref(x, itok_B_0_8, L3_cond_W1, L3_cond_b1, L3_cond_W2, L3_cond_b2, L3_cond_gamma, L3_cond_beta)
    return x

_drawn_inputs = setup_inputs


def setup_inputs(seed=0):
    import zlib

    import numpy as np

    out = dict(_drawn_inputs(seed))
    spreads = {'L0_cond_ln_g': (1.0, 0.2),
     'L0_cond_ln_b': (0.0, 0.1),
     'L2_cond_bq': (0.0, 0.1),
     'L2_cond_bk': (0.0, 0.8),
     'L2_cond_bv': (0.0, 0.1),
     'L2_cond_bo': (0.0, 0.1),
     'L3_cond_b1': (0.0, 0.8),
     'L3_cond_b2': (0.0, 0.702),
     'L3_cond_gamma': (1.0, 0.2),
     'L3_cond_beta': (0.0, 0.1)}
    factors = {'L0_cond_down_b': 8.0,
     'L0_cond_up_b': 8.0,
     'L1_cond_W1': 3.058,
     'L1_cond_b1': 8.0,
     'L1_cond_v': 2.816}
    for name, (base, spread) in spreads.items():
        noise = np.random.default_rng([zlib.crc32(name.encode()), seed]).standard_normal(out[name].shape)
        drawn = base * np.exp(spread * noise) if base else spread * noise
        out[name] = jnp.asarray(drawn.astype(out[name].dtype))
    for name, factor in factors.items():
        out[name] = (out[name] * factor).astype(out[name].dtype)
    return out
```

```python
from contextlib import ExitStack

import concourse.bass as bass
from concourse import mybir

ALU = mybir.AluOpType
ACT = mybir.ActivationFunctionType
AX_X = mybir.AxisListType.X
F32 = mybir.dt.float32
BF16 = mybir.dt.bfloat16
F16 = mybir.dt.float16
I32 = mybir.dt.int32
U8 = mybir.dt.uint8

P = 128
NEG = -1.0e30
EPS = 1.0e-5


def alone(eng, sem):
    eng.sem_inc(sem, 1)


class Count:

    def __init__(self):
        self.base, self.n, self.per = 0, 0, 0

    def enter(self, b, first, per):
        self.base, self.n, self.per = self.n + (b - first) * per, 0, per

    def leave(self, trips, start):
        assert self.n == self.per, (self.n, self.per)
        self.base, self.n = 0, start + trips * self.per

    @property
    def value(self):
        return self.base + self.n


def after(eng, sem, count):
    if not isinstance(count, int) or count > 0:
        eng.wait_ge(sem, count)


def cond_resid(nc, x, xt, profile, prompt, indices, u_prev, language, blocked, blocked_t, index_ok,
               wd, bd, wu, bu, ln0_g, ln0_b, w1, b1, v, wq_t, bq, wk_t, bk, wv_t, bv, wo_t, bo,
               lw1, lb1, lw2, lb2, lg, lb, out):
    B, S, D = x.shape
    T = S // P
    C = D // P
    H = 16
    DH = D // H
    NI = indices.shape[1]
    HP = 32
    G = H // 4
    PAIRS = [(0, 0), (0, 1), (1, 0), (0, 2), (2, 0), (1, 1)]
    NS = len(PAIRS)
    KR = NS * DH
    LAG_T, LAG_W, LAG_V = 6, 7, 8
    RING = 4
    A1 = w1.shape[1]
    A3 = lw1.shape[2]
    CONSTS = 17

    with ExitStack() as ctx:
        def sb(name, shape, dt=F32):
            return ctx.enter_context(nc.sbuf_tensor(name, shape, dt))

        def ps(name):
            return ctx.enter_context(nc.psum_tensor(name, [P, 512], F32))

        def sem(name):
            return ctx.enter_context(nc.semaphore(name))

        psS = [ps("psS0"), ps("psS1")]
        psT = [ps("psT0"), ps("psT1")]
        psO = ps("psO")
        psP = [ps("psP0"), ps("psP1")]
        psF = ps("psF")

        ident = sb("ident", [P, P])
        identb = sb("identb", [P, P], BF16)
        ones = sb("ones", [P, P])
        TW = P + T * T + T
        type_tab = sb("type_tab", [P, 3, TW])
        wq_sb, wk_sb, wv_sb, wo_sb = (sb(n, [P, C, D]) for n in ("wq_sb", "wk_sb", "wv_sb", "wo_sb"))
        bq_sb, bk_sb = sb("bq_sb", [P, C]), sb("bk_sb", [P, C])
        bqs = sb("bqs", [P, C])
        bv_sb, bo_sb = sb("bv_sb", [P, D]), sb("bo_sb", [P, D])
        w1_sb, b1_sb, v_sb, vbc = sb("w1_sb", [P, C, A1]), sb("b1_sb", [A1, 1]), sb("v_sb", [A1, 1]), sb("vbc", [A1, P])
        ids = sb("ids", [1, 2, B], I32)
        u_sb, ty_i = sb("u_sb", [P, B]), sb("ty_i", [P, B], I32)
        table = sb("table", [P, B, 8])
        tmp8 = sb("tmp8", [P, 3, B])
        idx_i, idx_ok = sb("idx_i", [P, T, NI], I32), sb("idx_ok", [P, T, NI], U8)
        idx_f, idx_m = sb("idx_f", [P, T, NI]), sb("idx_m", [P, T, NI])
        prob = sb("prob", [P, RING, T, S])
        hot = prob[:, 0].rearrange("p k s -> p (k s)").bitcast(BF16).rearrange("p (r s) -> p r s", s=S)
        blk8 = prob[:, 1, 0].bitcast(U8).rearrange("p (t s) -> p t s", t=T)
        blkt8 = prob[:, 1, 1].bitcast(U8).rearrange("p (t s) -> p t s", t=T)
        count_sb = prob[:, 2, 0:2].rearrange("p k s -> p (k s)").bitcast(BF16).rearrange("p (t s) -> p t s", t=T)
        iota_f = prob[:, 3, 0]
        iota_h = prob[:, 3, 1].bitcast(F16)[:, 0:S]
        unprior = sb("unprior", [P, T, S], BF16)
        unprior_t = sb("unprior_t", [P, T, S], BF16)
        unlisted = sb("unlisted", [P, T, S], BF16)
        count_t = sb("count_t", [P, T, S], BF16)

        x_sb = sb("x_sb", [P, T, D])
        xT = sb("xT", [P, C, S])
        wd_sb, bd_sb, wu_sb = sb("wd_sb", [P, C, P]), sb("bd_sb", [P, 1]), sb("wu_sb", [P, D])
        bu_sb, g0_sb, be0_sb = sb("bu_sb", [P, D]), sb("g0_sb", [P, D]), sb("be0_sb", [P, D])
        z_sb = sb("z_sb", [P, S])
        y_sb = sb("y_sb", [P, T, D])
        stats, mv, rstd = sb("stats", [P, T, 6]), sb("mv", [P, T, 2]), sb("rstd", [P, T])
        x1 = sb("x1", [P, T, D])
        h1 = sb("h1", [A1, S])
        typ = sb("typ", [P, TW])
        typ2 = sb("typ2", [P, TW])
        cur_m = sb("cur_m", [P, 8])
        col = sb("col", [P, T])
        bmax = sb("bmax", [P, T])
        masked = sb("masked", [P, T, P])
        m_in, m_neg = sb("m_in", [P, T]), sb("m_neg", [P, T])
        oth = sb("oth", [P, T, T])
        m_oth = sb("m_oth", [P, T])
        w_oth = sb("w_oth", [P, T, T])
        e_arg = sb("e_arg", [P, T])
        e_diag = sb("e_diag", [P, T, T])
        pin = sb("pin", [P, T, P])
        sum_in = sb("sum_in", [P, T])
        pinT = sb("pinT", [P, T, P])
        w_othT = sb("w_othT", [T, T, P])
        u_blk = sb("u_blk", [T, D])
        e_sum = sb("e_sum", [P, T])
        rec = sb("rec", [P, T])
        x2 = sb("x2", [P, T, D])
        qk = sb("qk", [P, 2 * C, S])
        parts = sb("parts", [P, 3, 2 * C, S], BF16)

        Qs = sb("Qs", [KR + 3, H, S], BF16)
        Ks = sb("Ks", [KR + 3, H, S], BF16)
        v_next = sb("v_next", [P, T, D])
        V = sb("V", [P, T, H, HP])
        cur_a, cur_w = sb("cur_a", [P, 4]), sb("cur_w", [P, 4])
        mask_a = sb("mask_a", [P, T, S], BF16)
        wgt = sb("wgt", [P, T, S])
        mx = sb("mx", [P, 2, 4, T])
        nm = sb("nm", [P, P])
        nm_parts = sb("nm_parts", [16, 3, P], BF16)
        oT_sb = sb("oT_sb", [P, S])
        orec = sb("orec", [P, T, 4])
        o_sb = sb("o_sb", [P, T, D])

        fT = sb("fT", [P, C, S])
        x3 = sb("x3", [P, T, D])
        y3 = sb("y3", [P, T, D])
        lw1_sb, lb1_sb, lw2_sb = sb("lw1_sb", [P, C, A3]), sb("lb1_sb", [A3, 1]), sb("lw2_sb", [A3, D])
        lb2_sb, lg_sb, lb_sb = sb("lb2_sb", [P, D]), sb("lg_sb", [P, D]), sb("lb_sb", [P, D])
        newt, newt3 = sb("newt", [P, T]), sb("newt3", [P, T])
        h3 = sb("h3", [A3, S])
        stats3, mv3, rstd3 = sb("stats3", [P, T, 6]), sb("mv3", [P, T, 2]), sb("rstd3", [P, T])

        x2_dram = nc.dram_tensor("x2_spill", (B, S, D), F32, kind="Internal").ap()
        st_dram = nc.dram_tensor("stacks", (2, H, NS, DH, S), BF16, kind="Internal").ap()

        s_const, s_ids = sem("s_const"), sem("s_ids")
        s_passed, s_passed_pool = sem("s_passed"), sem("s_passed_pool")
        s_ident, s_types, s_iota, s_set = sem("s_ident"), sem("s_types"), sem("s_iota"), sem("s_set")
        s_e1, s_e2 = sem("s_e1"), sem("s_e2")
        s_hot, s_hot_used, s_cnt, s_cnt_read, s_ct, s_ct_read = (sem(n) for n in (
            "s_hot", "s_hot_used", "s_cnt", "s_cnt_read", "s_ct", "s_ct_read"))
        s_loadp, s_loadf = sem("s_loadp"), sem("s_loadf")
        s_p_read = [sem("s_p0_read"), sem("s_p1_read")]
        s_f_read = sem("s_f_read")
        s_z, s_zc, s_y, s_yc, s_x1, s_x1T, s_x1Tc, s_h, s_hc = (sem(n) for n in (
            "s_z", "s_zc", "s_y", "s_yc", "s_x1", "s_x1T", "s_x1Tc", "s_h", "s_hc"))
        s_var, s_rstd, s_var3, s_rstd3 = (sem(n) for n in ("s_var", "s_rstd", "s_var3", "s_rstd3"))
        s_xbu, s_typ, s_pinT = sem("s_xbu"), sem("s_typ"), sem("s_pinT")
        s_row, s_colf, s_arg, s_exp1 = sem("s_row"), sem("s_colf"), sem("s_arg"), sem("s_exp1")
        s_pT, s_pTc, s_u, s_uc, s_pool, s_x2 = (sem(n) for n in ("s_pT", "s_pTc", "s_u", "s_uc", "s_pool", "s_x2"))
        s_x2T, s_x2Tc, s_qk, s_qkc, s_v, s_vc = (sem(n) for n in ("s_x2T", "s_x2Tc", "s_qk", "s_qkc", "s_v", "s_vc"))
        s_part, s_rest, s_split, s_stored = (sem(n) for n in ("s_part", "s_rest", "s_split", "s_stored"))
        s_stack = [sem(f"s_stack{g}") for g in range(G)]
        s_spill, s_unspill = sem("s_spill"), sem("s_unspill")
        s_wgt, s_scores, s_max, s_mT, s_negm, s_nsplit, s_mrow = (sem(n) for n in (
            "s_wgt", "s_scores", "s_max", "s_mT", "s_negm", "s_nsplit", "s_mrow"))
        s_st, s_exp, s_wmul, s_vcopy, s_pv, s_oc, s_oT, s_o = (sem(n) for n in (
            "s_st", "s_exp", "s_wmul", "s_vcopy", "s_pv", "s_oc", "s_oT", "s_o"))
        s_fT, s_fTc, s_x3p, s_x3, s_x3in, s_x3b, s_h3, s_h3c, s_y3, s_y3c, s_out_sb, s_out = (sem(n) for n in (
            "s_fT", "s_fTc", "s_x3p", "s_x3", "s_x3in", "s_x3b", "s_h3", "s_h3c", "s_y3", "s_y3c", "s_out_sb", "s_out"))
        s_dve, s_pool_seq, s_vz = sem("s_dve"), sem("s_pool_seq"), sem("s_vz")

        def bc(ap, n):
            return ap.unsqueeze(1).to_broadcast([P, n, ap.shape[1]])

        block = ctx.enter_context(nc.Block())

        LOADP, LOADF = 8, 7
        FIRST, LAST = 1, B - 1

        @block.sync
        def _(sp):
            ra, rb, rm = sp.alloc_register("ra"), sp.alloc_register("rb"), sp.alloc_register("rm")

            def times(reg, b, per, c):
                if isinstance(b, int):
                    return b * per + c
                if c >= 0:
                    sp.reg_mul(rm, b, per)
                    sp.reg_add(reg, rm, c)
                else:
                    sp.reg_add(rm, b, -1)
                    sp.reg_mul(rm, rm, per)
                    sp.reg_add(reg, rm, per + c)
                return sp.snap(reg)

            def at(ap, i):
                return ap[i] if isinstance(i, int) else ap[bass.ds(i, 1)].squeeze(0)

            sp.dma_start(ids[0:1, 0, :], profile.unsqueeze(0)).then_inc(s_ids, 16)
            sp.dma_start(ids[0:1, 1, :], language.unsqueeze(0)).then_inc(s_ids, 16)
            sp.wait_ge(s_ids, 32)

            def load_p(b, c):
                i = sp.value_load(ids[0:1, 0, b:b + 1] if isinstance(b, int) else ids[0:1, 0, bass.ds(b, 1)],
                                  min_val=0, max_val=wd.shape[0] - 1)
                src = [at(x, b).rearrange("(t p) d -> p t d", p=P), at(xt, b).rearrange("(c p) s -> p c s", p=P),
                       at(wd, i).rearrange("(c p) k -> p c k", p=P), at(bd, i).unsqueeze(1), at(wu, i),
                       at(bu, i).unsqueeze(0).to_broadcast([P, D]), at(ln0_g, i).unsqueeze(0).to_broadcast([P, D]),
                       at(ln0_b, i).unsqueeze(0).to_broadcast([P, D])]
                dst = [x_sb[:], xT[:], wd_sb[:], bd_sb[:], wu_sb[:], bu_sb[:], g0_sb[:], be0_sb[:]]
                w = times(ra, b, 1, 0)
                w2 = times(rb, b, 2 * C, 0)
                after(sp, s_v, w2)
                after(sp, s_x1, w)
                for d_, s_ in zip(dst, src):
                    sp.dma_start(d_, s_).then_inc(s_loadp, 16)

            def load_f(b):
                i = sp.value_load(ids[0:1, 1, b:b + 1] if isinstance(b, int) else ids[0:1, 1, bass.ds(b, 1)],
                                  min_val=0, max_val=lw1.shape[0] - 1)
                src = [at(lw1, i).rearrange("(c p) k -> p c k", p=P), at(lb1, i).unsqueeze(1), at(lw2, i),
                       at(lb2, i).unsqueeze(0).to_broadcast([P, D]), at(lg, i).unsqueeze(0).to_broadcast([P, D]),
                       at(lb, i).unsqueeze(0).to_broadcast([P, D])]
                dst = [lw1_sb[:], lb1_sb[:], lw2_sb[:], lb2_sb[:], lg_sb[:], lb_sb[:]]
                w = times(ra, b, 1, 0)
                after(sp, s_out_sb, w)
                for d_, s_ in zip(dst, src):
                    sp.dma_start(d_, s_).then_inc(s_loadf, 16)

            def unspill(b):
                w = times(ra, b, 16, 16)
                sp.wait_ge(s_spill, w)
                sp.dma_start(x3[:], at(x2_dram, b).rearrange("(t p) d -> p t d", p=P)).then_inc(s_loadf, 16)

            def spill(b):
                w = times(ra, b, T, T)
                sp.wait_ge(s_x2, w)
                sp.dma_start(at(x2_dram, b).rearrange("(t p) d -> p t d", p=P), x2[:]).then_inc(s_spill, 16)

            def store_stacks(b):
                w = times(ra, b, 1, 1)
                w2 = times(rb, b, 32, 0)
                sp.wait_ge(s_split, w)
                for g in range(G):
                    after(sp, s_stack[g], w2)
                for side in range(2):
                    for j, pair in enumerate(PAIRS):
                        for c in range(C):
                            sp.dma_start(st_dram[side, c * H // C:(c + 1) * H // C, j],
                                         parts[:, pair[side], side * C + c, :]).then_inc(s_stored, 16)

            def load_stack(b, g):
                w = times(ra, b, 2 * NS * C * 16, 2 * NS * C * 16)
                w2 = times(rb, b, H * T, (4 * g + 4 - H) * T)
                sp.wait_ge(s_stored, w)
                after(sp, s_st, w2)
                for side, dst in enumerate((Qs, Ks)):
                    sp.dma_start(dst[0:KR, 4 * g:4 * g + 4, :],
                                 st_dram[side, 4 * g:4 * g + 4].rearrange("h j d s -> (j d) h s")).then_inc(s_stack[g], 16)

            def load_mrow(b, g):
                w = times(ra, b, G, g + 1)
                w2 = times(rb, b, H * T, (4 * g + 4 - H) * T)
                sp.wait_ge(s_nsplit, w)
                after(sp, s_st, w2)
                for k in range(3):
                    dst = Qs[KR + k:KR + k + 1, 4 * g:4 * g + 4, :].rearrange("o h s -> o (h s)")
                    sp.dma_start(dst, nm_parts[:, k, :]).then_inc(s_mrow, 16)

            def store_out(b):
                dst = at(out, b).rearrange("(t p) d -> p t d", p=P)
                w = times(ra, b, 1, 1)
                sp.wait_ge(s_out_sb, w)
                sp.dma_start(dst, y3[:]).then_inc(s_out, 16)

            def iteration(b, is_p, is_a, is_f, more=True):
                for t in range(16):
                    if t == 0 and is_f:
                        load_mrow(b - 1, 3)
                        load_f(b - 1)
                    if t == 1 and is_f:
                        unspill(b - 1)
                    if t == 2 and is_a and b is not None and is_f:
                        load_stack(b, 2)
                    if t == 6 and is_a and is_f:
                        load_stack(b, 3)
                    if t in (5, 9, 13) and is_a:
                        load_mrow(b, t // 4 - 1)
                    if t == 10 and is_p:
                        spill(b + 1)
                    if t == 13 and is_p:
                        store_stacks(b + 1)
                        if more:
                            load_p(b + 2, 0)
                    if t == 14 and is_p:
                        load_stack(b + 1, 0)
                        load_stack(b + 1, 1)
                    if t == 15 and is_f:
                        store_out(b - 1)

            load_p(0, 0)
            n = 0
            for d_, s_ in [
                (w1_sb[:], w1.rearrange("(c p) a -> p c a", p=P)), (b1_sb[:], b1.unsqueeze(1)), (v_sb[:], v.unsqueeze(1)),
                (u_sb[:], u_prev.unsqueeze(0).to_broadcast([P, B])), (ty_i[:], prompt.unsqueeze(0).to_broadcast([P, B])),
                (idx_i[:], indices.rearrange("(t p) i -> p t i", p=P)), (idx_ok[:], index_ok.rearrange("(t p) i -> p t i", p=P)),
                (wq_sb[:], wq_t.rearrange("(c p) n -> p c n", p=P)), (wk_sb[:], wk_t.rearrange("(c p) n -> p c n", p=P)),
                (wv_sb[:], wv_t.rearrange("(c p) n -> p c n", p=P)), (wo_sb[:], wo_t.rearrange("(c p) n -> p c n", p=P)),
                (bq_sb[:], bq), (bk_sb[:], bk),
                (bv_sb[:], bv.unsqueeze(0).to_broadcast([P, D])), (bo_sb[:], bo.unsqueeze(0).to_broadcast([P, D])),
                (blk8, blocked.rearrange("(t p) k -> p t k", p=P)), (blkt8, blocked_t.rearrange("(t p) k -> p t k", p=P)),
            ]:
                sp.dma_start(d_, s_).then_inc(s_const, 16)
                n += 1
            assert n == CONSTS
            spill(0)
            store_stacks(0)
            load_p(1, 0)
            for g in range(G):
                load_stack(0, g)
            iteration(0, True, True, False)
            with sp.Fori(FIRST, LAST - 1) as b:
                iteration(b, True, True, True)
            iteration(LAST - 1, True, True, True, more=False)
            iteration(LAST, False, True, True)
            iteration(B, False, False, True)
            sp.wait_ge(s_out, 16 * B)

        @block.tensor
        def _(pe):
            P_USES = (11, 10)
            F_USES = 17
            p_used = [0, 0]
            f_used = Count()

            def bank(k, b):
                after(pe, s_p_read[k], b * P_USES[k] + p_used[k])
                p_used[k] += 1
                return psP[k]

            def fbank():
                after(pe, s_f_read, f_used.value)
                f_used.n += 1
                return psF

            def counts(t):
                for i in range(NI):
                    n = t * NI + i
                    pe.wait_ge(s_hot, n + 1)
                    if i == 0 and t >= 2:
                        pe.wait_ge(s_cnt_read, t - 1)
                    mm = pe.matmul(psS[t % 2][:], identb[:], hot[:, n % 8, :], start=(i == 0), stop=(i == NI - 1))
                    if i < NI - 1:
                        mm.then_inc(s_hot_used, 1)
                mm.then_inc(s_cnt, 1)

            def counts_t():
                for k in range(T):
                    pe.wait_ge(s_cnt_read, T)
                    if k >= 2:
                        pe.wait_ge(s_ct_read, k - 1)
                    dst = psT[k % 2][:].bitcast(BF16)
                    for t in range(T):
                        mm = pe.transpose(dst[:, t * P:(t + 1) * P], count_sb[:, t, k * P:(k + 1) * P], identb[:])
                    mm.then_inc(s_ct, 1)

            def turned(src, dst, c, sem_):
                for t in range(T):
                    mm = pe.transpose(dst[:, t * P:(t + 1) * P], src[:, t, c * P:(c + 1) * P], ident[:])
                mm.then_inc(sem_, 1)

            def first_layers(b, t):
                if t == 0:
                    p_used[:] = [0, 0]
                    pe.wait_ge(s_loadp, (b + 1) * LOADP * 16)
                    dst = bank(0, b)
                    for c in range(C):
                        mm = pe.matmul(dst[:], wd_sb[:, c, :], xT[:, c, :], start=(c == 0), stop=(c == C - 1))
                    mm.then_inc(s_z, 1)
                if t == 1:
                    pe.wait_ge(s_zc, b + 1)
                    for k in range(2):
                        dst = bank(1 - k, b)
                        for i in range(2):
                            mm = pe.matmul(dst[:, i * D:(i + 1) * D], z_sb[:, (2 * k + i) * P:(2 * k + i + 1) * P], wu_sb[:],
                                           start=True, stop=True)
                        mm.then_inc(s_y, 1)
                if t == 3:
                    pe.wait_ge(s_x1, b + 1)
                    for c in range(C):
                        turned(x1, bank(1 - c, b), c, s_x1T)
                if t == 4:
                    pe.wait_ge(s_x1Tc, (b + 1) * C)
                    dst = bank(1, b)
                    for c in range(C):
                        mm = pe.matmul(dst[0:A1, :], w1_sb[:, c, :], xT[:, c, :], start=(c == 0), stop=(c == C - 1))
                    mm.then_inc(s_h, 1)
                if t == 5:
                    pe.wait_ge(s_hc, b + 1)
                    dst = bank(0, b)
                    pe.matmul(dst[:], vbc[:], h1[:], start=True, stop=True).then_inc(s_row, 1)
                    dst = bank(1, b)
                    for i in range(T):
                        mm = pe.matmul(dst[:, i:i + 1], h1[:, i * P:(i + 1) * P], v_sb[:], start=True, stop=True)
                    mm.then_inc(s_colf, 1)
                if t == 6:
                    pe.wait_ge(s_exp1, (b + 1) * (T + 2))
                    dst = bank(0, b)
                    for i in range(T):
                        mm = pe.transpose(dst[:, i * P:(i + 1) * P], pin[:, i, :], ident[:])
                    mm.then_inc(s_pT, 1)
                    dst = bank(1, b)
                    for i in range(T):
                        mm = pe.transpose(dst[0:T, i * P:(i + 1) * P], w_oth[:, i, :], ident[:])
                    mm.then_inc(s_pT, 1)
                if t == 7:
                    dst = bank(0, b)
                    for i in range(T):
                        pe.matmul(dst[:, D:D + T], ones[:], e_diag[:, i, :], start=(i == 0), stop=(i == T - 1))
                    for i in range(T):
                        mm = pe.matmul(dst[0:T, 0:D], e_diag[:, i, :], x1[:, i, :], start=(i == 0), stop=(i == T - 1))
                    mm.then_inc(s_u, 1)
                if t == 8:
                    pe.wait_ge(s_pinT, b + 1)
                    pe.wait_ge(s_pTc, b + 1)
                    pe.wait_ge(s_uc, b + 1)
                    for k in range(2):
                        dst = bank(1 - k, b)
                        for i in range(2):
                            j = 2 * k + i
                            pe.matmul(dst[:, i * D:(i + 1) * D], pinT[:, j, :], x1[:, j, :], start=True, stop=False)
                            mm = pe.matmul(dst[:, i * D:(i + 1) * D], w_othT[:, j, :], u_blk[:], start=False, stop=True)
                        mm.then_inc(s_pool, 1)
                if t == 9:
                    pe.wait_ge(s_x2, (b + 1) * T)
                    for c in range(C):
                        turned(x2, bank(1 - c, b), c, s_x2T)
                if t == 10:
                    pe.wait_ge(s_x2Tc, (b + 1) * C)
                    for side, w_sb in enumerate((wq_sb, wk_sb)):
                        for o in range(C):
                            dst = bank(1 - o, b)
                            for c in range(C):
                                mm = pe.matmul(dst[:], w_sb[:, c, o * P:(o + 1) * P], xT[:, c, :], start=(c == 0), stop=(c == C - 1))
                            mm.then_inc(s_qk, 1)
                if t == 11:
                    for k in range(2):
                        dst = bank(1 - k, b)
                        for i in range(2):
                            j = 2 * k + i
                            for c in range(C):
                                mm = pe.matmul(dst[:, i * D:(i + 1) * D], xT[:, c, j * P:(j + 1) * P], wv_sb[:, c, :],
                                               start=(c == 0), stop=(c == C - 1))
                            mm.then_inc(s_v, 1)
                    assert tuple(p_used) == P_USES, p_used

            def scores(b, h):
                if h % 4 == 0:
                    pe.wait_ge(s_stack[h // 4], (b + 1) * 32)
                for t in range(T):
                    i = b * (H * T) + h * T + t
                    after(pe, s_max, i - 1)
                    pe.matmul(psS[t % 2][:], Qs[0:KR, h, t * P:(t + 1) * P], Ks[0:KR, h, :], start=True, stop=True)\
                        .then_inc(s_scores, 1)

            def scores_t(b, h):
                if h % 4 == 0:
                    pe.wait_ge(s_mrow, (b * G + h // 4 + 1) * 48)
                for k in range(T):
                    i = b * (H * T) + h * T + k
                    after(pe, s_exp, i - 1)
                    mm = pe.matmul(psT[k % 2][:], Ks[:, h, k * P:(k + 1) * P], Qs[:, h, :], start=True, stop=True)
                    mm.then_inc(s_st, 1)
                return mm

            def output(b, h):
                pe.wait_ge(s_wmul, b * H + h + 1)
                if h % 4 == 0:
                    pe.wait_ge(s_vcopy, b * G + h // 4 + 1)
                    after(pe, s_oc, b * G + h // 4)
                r = HP * (h % 4)
                for k in range(T):
                    mm = pe.matmul(psO[r:r + HP, :], V[:, k, h, :], prob[:, h % RING, k, :], start=(k == 0), stop=(k == T - 1))
                mm.then_inc(s_pv, 1)

            def max_turned(b, g):
                pe.wait_ge(s_max, b * (H * T) + (g + 1) * 4 * T)
                dst = fbank()
                pe.transpose(dst[0:4 * T, 0:P], mx[:, g % 2].rearrange("p h t -> p (h t)"), ident[:]).then_inc(s_mT, 1)

            def output_turned(b, g):
                pe.wait_ge(s_oc, b * G + g + 1)
                dst = fbank()
                for t in range(T):
                    mm = pe.transpose(dst[:, t * P:(t + 1) * P], oT_sb[:, t * P:(t + 1) * P], ident[:])
                mm.then_inc(s_oT, 1)

            def last_layer(b, t):
                if t == 9:
                    pe.wait_ge(s_o, (b + 1) * G)
                    for c in range(C):
                        turned(o_sb, fbank(), c, s_fT)
                if t == 10:
                    pe.wait_ge(s_fTc, 2 * C * b + C)
                    for k in range(2):
                        dst = fbank()
                        for i in range(2):
                            j = 2 * k + i
                            for c in range(C):
                                mm = pe.matmul(dst[:, i * D:(i + 1) * D], fT[:, c, j * P:(j + 1) * P], wo_sb[:, c, :],
                                               start=(c == 0), stop=(c == C - 1))
                        mm.then_inc(s_x3p, 1)
                if t == 11:
                    pe.wait_ge(s_x3, 2 * b + 2)
                    for c in range(C):
                        turned(x3, fbank(), c, s_fT)
                if t == 12:
                    pe.wait_ge(s_fTc, 2 * C * (b + 1))
                    pe.wait_ge(s_loadf, (b + 1) * LOADF * 16)
                    dst = fbank()
                    for c in range(C):
                        mm = pe.matmul(dst[0:A3, :], lw1_sb[:, c, :], fT[:, c, :], start=(c == 0), stop=(c == C - 1))
                    mm.then_inc(s_h3, 1)
                if t == 13:
                    pe.wait_ge(s_h3c, b + 1)
                    for k in range(2):
                        dst = fbank()
                        for i in range(2):
                            j = 2 * k + i
                            mm = pe.matmul(dst[:, i * D:(i + 1) * D], h3[:, j * P:(j + 1) * P], lw2_sb[:], start=True, stop=True)
                        mm.then_inc(s_y3, 1)

            def iteration(b, is_p, is_a, is_f):
                for t in range(16):
                    if is_a:
                        scores(b, t)
                    for lag, stage in ((LAG_T, scores_t), (LAG_V, output)):
                        if t >= lag and is_a:
                            stage(b, t - lag)
                        if t < lag and is_f:
                            stage(b - 1, t - lag + H)
                    if t % 4 == 0:
                        if t == 0 and is_f:
                            max_turned(b - 1, 3)
                            output_turned(b - 1, 1)
                        if t in (4, 8):
                            if is_a:
                                max_turned(b, t // 4 - 1)
                            if is_f:
                                output_turned(b - 1, t // 4 + 1)
                        if t == 12 and is_a:
                            max_turned(b, 2)
                            output_turned(b, 0)
                    if is_p:
                        first_layers(b + 1, t)
                    if is_f:
                        last_layer(b - 1, t)

            pe.wait_ge(s_ident, 3)
            pe.wait_ge(s_const, 16 * CONSTS)
            for t in range(16):
                if t == 5:
                    pe.wait_ge(s_set, 1)
                first_layers(0, t)
                if t in (1, 2, 4, 5):
                    counts((1, 2, 4, 5).index(t))
            counts_t()
            pe.wait_ge(s_ct_read, T)
            iteration(0, True, True, False)
            start = f_used.n
            with pe.Fori(FIRST, LAST) as b:
                f_used.enter(b, FIRST, F_USES)
                iteration(b, True, True, True)
            f_used.leave(LAST - FIRST, start)
            iteration(LAST, False, True, True)
            iteration(B, False, False, True)

        @block.scalar
        def _(act):
            def exps(b, h):
                after(act, s_pv, b * H + h + 1 - RING)
                for k in range(T):
                    act.wait_ge(s_st, b * (H * T) + h * T + k + 1)
                    act.activation(prob[:, h % RING, k, :], psT[k % 2][:], ACT.Exp).then_inc(s_exp, 1)

            def out_copy(b, g):
                act.wait_ge(s_pv, b * H + 4 * g + 4)
                after(act, s_oT, b * G + g)
                act.copy(oT_sb[:], psO[:]).then_inc(s_oc, 1)

            def first_layers(b, t):
                if t == 0:
                    act.wait_ge(s_z, b + 1)
                    after(act, s_y, 2 * b)
                    act.activation(z_sb[:], psP[0][:], ACT.Relu, bias=bd_sb[:]).then_inc(s_zc, 1)
                    act.wait_ge(s_zc, b + 1)
                    act.sem_inc(s_p_read[0], 1)
                if t == 3:
                    for c in range(C):
                        act.wait_ge(s_x1T, b * C + c + 1)
                        act.copy(xT[:, c, :], psP[1 - c][:]).then_inc(s_x1Tc, 1)
                        act.wait_ge(s_x1Tc, b * C + c + 1)
                        act.sem_inc(s_p_read[1 - c], 1)
                if t == 4:
                    act.wait_ge(s_h, b + 1)
                    after(act, s_colf, b)
                    act.activation(h1[:], psP[1][0:A1, :], ACT.Tanh, bias=b1_sb[:]).then_inc(s_hc, 1)
                    act.wait_ge(s_hc, b + 1)
                    act.sem_inc(s_p_read[1], 1)
                if t == 5:
                    act.wait_ge(s_arg, b + 1)
                    after(act, s_pT, 2 * b)
                    after(act, s_u, b)
                    for i in range(T):
                        act.activation(pin[:, i, :], masked[:, i, :], ACT.Exp, bias=m_neg[:, i:i + 1],
                                       accum_out=sum_in[:, i:i + 1]).then_inc(s_exp1, 1)
                    act.activation(w_oth[:], oth[:], ACT.Exp).then_inc(s_exp1, 1)
                    act.activation(e_diag[:].rearrange("p a b -> p (a b)")[:, 0:T * T:T + 1], e_arg[:], ACT.Exp)\
                       .then_inc(s_exp1, 1)
                if t == 6:
                    act.wait_ge(s_pT, 2 * b + 1)
                    act.copy(pinT[:].rearrange("p a b -> p (a b)"), psP[0][:]).then_inc(s_pinT, 1)
                    act.wait_ge(s_pinT, b + 1)
                    act.sem_inc(s_p_read[0], 1)
                if t == 9:
                    for c in range(C):
                        act.wait_ge(s_x2T, b * C + c + 1)
                        act.copy(xT[:, c, :], psP[1 - c][:]).then_inc(s_x2Tc, 1)
                        act.wait_ge(s_x2Tc, b * C + c + 1)
                        act.sem_inc(s_p_read[1 - c], 1)
                if t == 10:
                    after(act, s_split, b)
                    for side, (bias, scale) in enumerate(((bqs, DH ** -0.5), (bk_sb, 1.0))):
                        for o in range(C):
                            i = side * C + o
                            act.wait_ge(s_qk, b * 2 * C + i + 1)
                            act.activation(qk[:, i, :], psP[1 - o][:], ACT.Identity, bias=bias[:, o:o + 1], scale=scale)\
                               .then_inc(s_qkc, 1)
                            act.wait_ge(s_qkc, b * 2 * C + i + 1)
                            act.sem_inc(s_p_read[1 - o], 1)

            def last_layer(b, t):
                if t in (9, 11):
                    for c in range(C):
                        i = b * 2 * C + (C if t == 11 else 0) + c + 1
                        act.wait_ge(s_fT, i)
                        if t == 9 and c == 0:
                            after(act, s_h3, b)
                        if t == 11 and c == 0:
                            act.wait_ge(s_x3p, 2 * b + 2)
                        act.copy(fT[:, c, :], psF[:]).then_inc(s_fTc, 1)
                        act.wait_ge(s_fTc, i)
                        act.sem_inc(s_f_read, 1)
                if t == 12:
                    act.wait_ge(s_h3, b + 1)
                    after(act, s_y3, 2 * b)
                    act.activation(h3[:], psF[0:A3, :], ACT.Relu, bias=lb1_sb[:]).then_inc(s_h3c, 1)
                    act.wait_ge(s_h3c, b + 1)
                    act.sem_inc(s_f_read, 1)

            def iteration(b, is_p, is_a, is_f):
                for t in range(16):
                    if t >= LAG_T and is_a:
                        exps(b, t - LAG_T)
                    if t < LAG_T and is_f:
                        exps(b - 1, t - LAG_T + H)
                    if t == 11 and is_a:
                        out_copy(b, 0)
                    if t == 15 and is_a:
                        out_copy(b, 1)
                    if t in (3, 7) and is_f:
                        out_copy(b - 1, 2 + t // 4)
                    if is_p:
                        first_layers(b + 1, t)
                    if is_f:
                        last_layer(b - 1, t)

            act.wait_ge(s_loadp, LOADP * 16)
            act.wait_ge(s_const, 16 * CONSTS)
            act.activation(tmp8[:, 0, :], u_sb[:], ACT.Exp, scale=-5.0).then_inc(s_e1, 1)
            act.wait_ge(s_e2, 1)
            act.activation(tmp8[:, 2, :], tmp8[:, 1, :], ACT.Exp, scale=-1.0).then_inc(s_e1, 1)
            for t in range(16):
                if t == 5:
                    act.wait_ge(s_vz, 2)
                if t == 10:
                    act.wait_ge(s_set, 1)
                first_layers(0, t)
            for k in range(T):
                act.wait_ge(s_ct, k + 1)
                act.copy(count_t[:, k, :], psT[k % 2][:].bitcast(BF16)[:, 0:S]).then_inc(s_ct_read, 1)
            iteration(0, True, True, False)
            with act.Fori(FIRST, LAST) as b:
                iteration(b, True, True, True)
            iteration(LAST, False, True, True)
            iteration(B, False, False, True)

        @block.vector
        def _(dve):
            seq = Count()
            SEQ = 69

            def link(ins):
                ins.then_inc(s_dve, 1)
                seq.n += 1
                dve.wait_ge(s_dve, seq.value)

            def moments(y, st, m, r, s_var):
                for t in range(T):
                    ins = dve.bn_stats(st[:, t, :], y[:, t, :])
                    if t < T - 1:
                        ins.then_inc(s_dve, 1)
                        seq.n += 1
                link(ins)
                alone(dve, s_passed)
                for t in range(T):
                    ins = dve.bn_aggr(m[:, t, :], st[:, t, :])
                    if t < T - 1:
                        ins.then_inc(s_dve, 1)
                        seq.n += 1
                link(ins)
                link(dve.tensor_scalar(m[:, :, 1], m[:, :, 1], EPS, None, ALU.add))
                bits = r[:].bitcast(I32)
                link(dve.tensor_scalar(bits, m[:, :, 1].bitcast(I32), 1, None, ALU.logical_shift_right))
                link(dve.tensor_scalar(bits, bits, -1.0, float(0x5F3759DF), ALU.mult, ALU.add))
                dve.sem_inc(s_var, 1)

            def maxima(b, h):
                for t in range(T):
                    i = b * (H * T) + h * T + t
                    dve.wait_ge(s_scores, i + 1)
                    if h % 4 == 0 and t == 0:
                        after(dve, s_mT, b * G + h // 4 - 1)
                    alone(dve, s_passed)
                    s = psS[t % 2][:]
                    dve.tensor_tensor_reduce(s, s, mask_a[:, t, :], 1.0, NEG, ALU.add, ALU.max,
                                             mx[:, (h // 4) % 2, h % 4, t:t + 1]).then_inc(s_max, 1)

            def neg_max(b, g):
                dve.wait_ge(s_mT, b * G + g + 1)
                after(dve, s_nsplit, b * G + g)
                dve.tensor_scalar(nm[0:4 * T, :], psF[0:4 * T, 0:P], -1.0, None, ALU.mult).then_inc(s_negm, 1)
                dve.wait_ge(s_negm, b * G + g + 1)
                dve.sem_inc(s_f_read, 1)

            def weight(b, h):
                dve.wait_ge(s_exp, b * (H * T) + (h + 1) * T)
                p = prob[:, h % RING].rearrange("p k s -> p (k s)")
                dve.scalar_tensor_tensor(out=p, in0=p, scalar=-NEG, in1=wgt[:].rearrange("p k s -> p (k s)"),
                                         op0=ALU.min, op1=ALU.mult).then_inc(s_wmul, 1)

            def mask_for(b):
                after(dve, s_max, b * (H * T))
                src = table[:, b, 0:4] if isinstance(b, int) else table[:, bass.ds(b, 1), 0:4].squeeze(1)
                alone(dve, s_passed)
                link(dve.tensor_copy(cur_a[:], src))
                link(dve.tensor_scalar(mask_a[:], unprior[:], cur_a[:, 1:2], None, ALU.mult))
                link(dve.scalar_tensor_tensor(out=mask_a[:], in0=unlisted[:], scalar=cur_a[:, 0:1], in1=mask_a[:],
                                              op0=ALU.mult, op1=ALU.add))

            def weights_for(b):
                after(dve, s_wmul, b * H)
                src = table[:, b, 0:4] if isinstance(b, int) else table[:, bass.ds(b, 1), 0:4].squeeze(1)
                alone(dve, s_passed)
                link(dve.tensor_copy(cur_w[:], src))
                link(dve.tensor_scalar(wgt[:], unprior_t[:], cur_w[:, 3:4], cur_w[:, 2:3], ALU.mult, ALU.add))
                link(dve.scalar_tensor_tensor(out=wgt[:], in0=count_t[:], scalar=cur_w[:, 0:1], in1=wgt[:],
                                              op0=ALU.mult, op1=ALU.add))

            def normalize(b, g):
                dve.wait_ge(s_oT, b * G + g + 1)
                after(dve, s_fT, 2 * C * b)
                src = psF[:].rearrange("p (t h r) -> p t h r", t=T, h=4)
                link(dve.reciprocal(orec[:], src[:, :, :, DH]))
                dst = o_sb[:, :, g * 4 * DH:(g + 1) * 4 * DH].rearrange("p t (h r) -> p t h r", h=4)
                for t in range(T):
                    ins = dve.tensor_tensor(dst[:, t], src[:, t, :, 0:DH],
                                            orec[:, t].unsqueeze(2).to_broadcast([P, 4, DH]), ALU.mult)
                    if t < T - 1:
                        ins.then_inc(s_dve, 1)
                        seq.n += 1
                ins.then_inc(s_o, 1)
                dve.wait_ge(s_o, b * G + g + 1)
                dve.sem_inc(s_f_read, 1)

            def first_layers(b, t):
                if t == 1:
                    dve.wait_ge(s_xbu, 2 * b + 1)
                    for k in range(2):
                        dve.wait_ge(s_y, 2 * b + k + 1)
                        y = y_sb[:, 2 * k:2 * k + 2, :].rearrange("p t d -> p (t d)")
                        link(dve.tensor_tensor(y, psP[1 - k][:], y, ALU.add))
                        dve.sem_inc(s_p_read[1 - k], 1)
                    moments(y_sb, stats, mv, rstd, s_var)
                if t == 2:
                    dve.wait_ge(s_rstd, b + 1)
                    for t_ in range(T):
                        dve.tensor_scalar(y_sb[:, t_, :], y_sb[:, t_, :], mv[:, t_, 0:1], rstd[:, t_:t_ + 1],
                                          ALU.subtract, ALU.mult).then_inc(s_yc, 1)
                if t == 5:
                    dve.wait_ge(s_typ, b + 1)
                    dve.wait_ge(s_row, b + 1)
                    after(dve, s_exp1, b * (T + 2))
                    row = psP[0][:].rearrange("p (t l) -> p t l", t=T)
                    link(dve.tensor_reduce(bmax[:], row, AX_X, ALU.max))
                    alone(dve, s_passed)
                    for i in range(T):
                        ins = dve.tensor_tensor_reduce(masked[:, i, :], row[:, i, :], typ[:, 0:P], 1.0, NEG,
                                                       ALU.add, ALU.max, m_in[:, i:i + 1])
                        if i < T - 1:
                            ins.then_inc(s_dve, 1)
                            seq.n += 1
                    link(ins)
                    dve.sem_inc(s_p_read[0], 1)
                    dve.wait_ge(s_colf, b + 1)
                    link(dve.tensor_copy(col[:], psP[1][:, 0:T]))
                    dve.sem_inc(s_p_read[1], 1)
                    link(dve.tensor_tensor(oth[:], bmax[:].unsqueeze(1).to_broadcast([P, T, T]),
                                           typ[:, P:P + T * T].rearrange("p (a b) -> p a b", a=T), ALU.add))
                    link(dve.tensor_reduce(m_oth[:], oth[:], AX_X, ALU.max))
                    link(dve.tensor_tensor(m_in[:], m_in[:], m_oth[:], ALU.max))
                    link(dve.tensor_scalar(m_neg[:], m_in[:], -1.0, None, ALU.mult))
                    link(dve.tensor_tensor(oth[:], oth[:], m_in[:].unsqueeze(2).to_broadcast([P, T, T]), ALU.subtract))
                    dve.tensor_tensor(e_arg[:], col[:], bmax[:], ALU.subtract).then_inc(s_arg, 1)
                if t == 6:
                    dve.wait_ge(s_pT, 2 * b + 2)
                    after(dve, s_pool, 2 * b)
                    link(dve.tensor_copy(w_othT[:].rearrange("p a b -> p (a b)"), psP[1][0:T, :]))
                    dve.sem_inc(s_p_read[1], 1)
                    dve.sem_inc(s_pTc, 1)
                if t == 7:
                    dve.wait_ge(s_u, b + 1)
                    after(dve, s_pool, 2 * b)
                    link(dve.tensor_copy(u_blk[:], psP[0][0:T, 0:D]))
                    link(dve.tensor_copy(e_sum[:], psP[0][:, D:D + T]))
                    dve.sem_inc(s_p_read[0], 1)
                    dve.sem_inc(s_uc, 1)
                    link(dve.tensor_tensor(oth[:], w_oth[:], e_sum[:].unsqueeze(1).to_broadcast([P, T, T]), ALU.mult))
                    link(dve.tensor_reduce(m_oth[:], oth[:], AX_X, ALU.add))
                    link(dve.tensor_tensor(m_oth[:], m_oth[:], sum_in[:], ALU.add))
                    link(dve.tensor_tensor(m_oth[:], m_oth[:], typ[:, P + T * T:TW], ALU.mult))
                    link(dve.reciprocal(rec[:], m_oth[:]))
                if t == 8:
                    after(dve, s_x2T, C * b)
                    after(dve, s_spill, 16 * b)
                    for j in range(T):
                        dve.wait_ge(s_pool, 2 * b + j // 2 + 1)
                        dve.scalar_tensor_tensor(out=x2[:, j, :], in0=psP[1 - j // 2][:, (j % 2) * D:(j % 2 + 1) * D],
                                                 scalar=rec[:, j:j + 1], in1=x1[:, j, :], op0=ALU.mult, op1=ALU.add)\
                           .then_inc(s_x2, 1)
                        if j % 2:
                            dve.wait_ge(s_x2, b * T + j + 1)
                            dve.sem_inc(s_p_read[1 - j // 2], 1)
                if t == 11:
                    dve.wait_ge(s_qkc, (b + 1) * 2 * C)
                    after(dve, s_stored, b * 2 * NS * C * 16)
                    dve.tensor_copy(parts[:, 0], qk[:]).then_inc(s_part, 1)
                    after(dve, s_vcopy, b * G)
                    for k in range(2):
                        dve.wait_ge(s_v, 2 * C * b + 2 * k + 2)
                        link(dve.tensor_tensor(v_next[:, 2 * k:2 * k + 2, :], psP[1 - k][:].rearrange("p (t d) -> p t d", t=2),
                                               bc(bv_sb[:], 2), ALU.add))
                        dve.sem_inc(s_p_read[1 - k], 1)
                    dve.sem_inc(s_vc, 1)
                if t == 12:
                    dve.wait_ge(s_rest, b + 1)
                    dve.tensor_copy(parts[:, 1], qk[:]).then_inc(s_part, 1)

            def last_layer(b, t):
                if t == 10:
                    dve.wait_ge(s_x3in, b + 1)
                    for k in range(2):
                        dve.wait_ge(s_x3p, 2 * b + k + 1)
                        r = x3[:, 2 * k:2 * k + 2, :].rearrange("p t d -> p (t d)")
                        dve.tensor_tensor(r, psF[:], r, ALU.add).then_inc(s_x3, 1)
                        dve.wait_ge(s_x3, 2 * b + k + 1)
                        dve.sem_inc(s_f_read, 1)
                if t == 13:
                    dve.wait_ge(s_x3b, b + 1)
                    for k in range(2):
                        dve.wait_ge(s_y3, 2 * b + k + 1)
                        y = y3[:, 2 * k:2 * k + 2, :].rearrange("p t d -> p (t d)")
                        link(dve.tensor_tensor(y, psF[:], y, ALU.add))
                        dve.sem_inc(s_f_read, 1)
                    moments(y3, stats3, mv3, rstd3, s_var3)
                if t == 14:
                    dve.wait_ge(s_rstd3, b + 1)
                    for t_ in range(T):
                        dve.tensor_scalar(y3[:, t_, :], y3[:, t_, :], mv3[:, t_, 0:1], rstd3[:, t_:t_ + 1],
                                          ALU.subtract, ALU.mult).then_inc(s_y3c, 1)

            def iteration(b, is_p, is_a, is_f):
                for t in range(16):
                    if is_a:
                        if t == 0:
                            mask_for(b)
                        maxima(b, t)
                    if t >= LAG_W and is_a:
                        weight(b, t - LAG_W)
                    if t < LAG_W and is_f:
                        weight(b - 1, t - LAG_W + H)
                    if t == LAG_W - 1 and is_a:
                        weights_for(b)
                    if t == 0 and is_f:
                        neg_max(b - 1, 3)
                        normalize(b - 1, 1)
                    if t in (4, 8):
                        if is_a:
                            neg_max(b, t // 4 - 1)
                        if is_f:
                            normalize(b - 1, t // 4 + 1)
                    if t == 12 and is_a:
                        neg_max(b, 2)
                        normalize(b, 0)
                    if is_p:
                        first_layers(b + 1, t)
                    if is_f:
                        last_layer(b - 1, t)

            def hots(t):
                for i in range(NI):
                    n = t * NI + i
                    m = n - 8
                    if m >= 0:
                        if m % NI == NI - 1:
                            dve.wait_ge(s_cnt, m // NI + 1)
                        else:
                            dve.wait_ge(s_hot_used, (m // NI) * (NI - 1) + m % NI + 1)
                    dve.tensor_scalar(hot[:, n % 8, :], iota_h, idx_f[:, t, i:i + 1], None, ALU.is_equal).then_inc(s_hot, 1)
                dve.wait_ge(s_cnt, t + 1)
                link(dve.tensor_scalar(unlisted[:, t, :], psS[t % 2][:], 0.5, NEG, ALU.is_lt, ALU.mult))
                dve.tensor_copy(count_sb[:, t, :], psS[t % 2][:]).then_inc(s_cnt_read, 1)

            link(dve.memset(V[:], 0.0))
            dve.memset(V[:, :, :, DH:DH + 1], 1.0).then_inc(s_vz, 1)
            dve.wait_ge(s_vz, 1)
            link(dve.memset(e_diag[:], 0.0))
            dve.sem_inc(s_vz, 1)
            dve.wait_ge(s_const, 16 * CONSTS)
            link(dve.tensor_copy(idx_f[:], idx_i[:]))
            link(dve.tensor_copy(idx_m[:], idx_ok[:]))
            link(dve.tensor_scalar(iota_f[:, 0:T * NI], idx_f[:].rearrange("p t i -> p (t i)"), 0.0, float(S), ALU.is_lt, ALU.mult))
            link(dve.tensor_tensor(idx_f[:].rearrange("p t i -> p (t i)"), idx_f[:].rearrange("p t i -> p (t i)"),
                                   iota_f[:, 0:T * NI], ALU.add))
            link(dve.tensor_scalar(idx_f[:], idx_f[:], 0.0, float(S - 1), ALU.max, ALU.min))
            link(dve.scalar_tensor_tensor(out=idx_f[:], in0=idx_f[:], scalar=1.0, in1=idx_m[:], op0=ALU.add, op1=ALU.mult))
            link(dve.tensor_scalar(idx_f[:], idx_f[:], -1.0, None, ALU.add))
            dve.sem_inc(s_iota, 1)
            dve.wait_ge(s_iota, 2)
            link(dve.tensor_copy(iota_h, iota_f))
            dve.wait_ge(s_ident, 2)
            link(dve.tensor_copy(identb[:], ident[:]))
            dve.sem_inc(s_ident, 1)
            dve.wait_ge(s_e1, 1)
            link(dve.tensor_scalar(tmp8[:, 0, :], tmp8[:, 0, :], 10.0, None, ALU.mult))
            link(dve.tensor_scalar(table[:, :, 0], tmp8[:, 0, :], 1.0, None, ALU.is_ge))
            dve.tensor_scalar(tmp8[:, 1, :], tmp8[:, 0, :], 1.0, None, ALU.min).then_inc(s_e2, 1)
            dve.wait_ge(s_e1, 2)
            dve.wait_ge(s_e2, 1)
            link(dve.tensor_scalar(table[:, :, 2], table[:, :, 0], -1.0, 1.0, ALU.mult, ALU.add))
            link(dve.scalar_tensor_tensor(out=table[:, :, 1], in0=tmp8[:, 1, :], scalar=-1.0, in1=table[:, :, 2],
                                          op0=ALU.mult, op1=ALU.mult))
            link(dve.scalar_tensor_tensor(out=table[:, :, 3], in0=tmp8[:, 2, :], scalar=-1.0, in1=table[:, :, 2],
                                          op0=ALU.add, op1=ALU.mult))
            link(dve.tensor_copy(tmp8[:, 0, :], ty_i[:]))
            link(dve.tensor_scalar(table[:, :, 4], tmp8[:, 0, :], 0.0, None, ALU.is_equal))
            link(dve.tensor_scalar(table[:, :, 5], tmp8[:, 0, :], 1.0, None, ALU.is_equal))
            link(dve.tensor_tensor(tmp8[:, 1, :], table[:, :, 4], table[:, :, 5], ALU.add))
            link(dve.tensor_scalar(table[:, :, 6], tmp8[:, 1, :], -1.0, 1.0, ALU.mult, ALU.add))
            dve.sem_inc(s_types, 1)
            link(dve.tensor_scalar(bqs[:], bq_sb[:], DH ** -0.5, None, ALU.mult))
            link(dve.tensor_scalar(vbc[:], ones[0:A1, :], v_sb[:], None, ALU.mult))
            dve.sem_inc(s_set, 1)
            link(dve.memset(Ks[KR:KR + 3, :, :], 1.0))
            for t in range(16):
                first_layers(0, t)
                if t in (1, 2, 4, 5):
                    hots((1, 2, 4, 5).index(t))
                if t == 6:
                    link(dve.tensor_copy(unprior[:], blk8))
                    link(dve.tensor_scalar(unprior[:], unprior[:], -1.0, 1.0, ALU.mult, ALU.add))
                    link(dve.tensor_copy(unprior_t[:], blkt8))
                    link(dve.tensor_scalar(unprior_t[:], unprior_t[:], -1.0, 1.0, ALU.mult, ALU.add))
            dve.wait_ge(s_ct_read, T)
            iteration(0, True, True, False)
            start = seq.n
            with dve.Fori(FIRST, LAST) as b:
                seq.enter(b, FIRST, SEQ)
                iteration(b, True, True, True)
            seq.leave(LAST - FIRST, start)
            iteration(LAST, False, True, True)
            iteration(B, False, False, True)

        @block.gpsimd
        def _(pool):
            seq = Count()
            SEQ = 42

            def link(ins):
                ins.then_inc(s_pool_seq, 1)
                seq.n += 1
                pool.wait_ge(s_pool_seq, seq.value)

            def newton(var, r, t, s_r, b):
                for k in range(3):
                    link(pool.tensor_tensor(t[:], r[:], r[:], ALU.mult))
                    link(pool.tensor_tensor(t[:], t[:], var, ALU.mult))
                    alone(pool, s_passed_pool)
                    link(pool.tensor_scalar(t[:], t[:], -0.5, 1.5, ALU.mult, ALU.add))
                    ins = pool.tensor_tensor(r[:], r[:], t[:], ALU.mult)
                    if k < 2:
                        link(ins)
                ins.then_inc(s_r, 1)
                pool.wait_ge(s_r, b + 1)

            def types_for(b):
                after(pool, s_exp1, b * (T + 2))
                after(pool, s_x2, b * T)
                src = table[:, b, 4:7] if isinstance(b, int) else table[:, bass.ds(b, 1), 4:7].squeeze(1)
                alone(pool, s_passed_pool)
                link(pool.tensor_copy(cur_m[:, 4:7], src))
                alone(pool, s_passed_pool)
                link(pool.tensor_scalar(typ[:], type_tab[:, 0, :], cur_m[:, 4:5], None, ALU.mult))
                for k in (1, 2):
                    alone(pool, s_passed_pool)
                    link(pool.tensor_scalar(typ2[:], type_tab[:, k, :], cur_m[:, 4 + k:5 + k], None, ALU.mult))
                    ins = pool.tensor_tensor(typ[:], typ[:], typ2[:], ALU.add)
                    if k == 1:
                        link(ins)
                ins.then_inc(s_typ, 1)
                pool.wait_ge(s_typ, b + 1)

            def first_layers(b, t):
                if t == 0:
                    pool.wait_ge(s_loadp, (b + 1) * LOADP * 16)
                    pool.tensor_tensor(y_sb[:], x_sb[:], bc(bu_sb[:], T), ALU.add).then_inc(s_xbu, 1)
                    pool.wait_ge(s_xbu, 2 * b + 1)
                    pool.tensor_tensor(x_sb[:], x_sb[:], bc(be0_sb[:], T), ALU.add).then_inc(s_xbu, 1)
                    pool.wait_ge(s_xbu, 2 * b + 2)
                    types_for(b)
                if t == 2:
                    pool.wait_ge(s_var, b + 1)
                    newton(mv[:, :, 1], rstd, newt, s_rstd, b)
                    pool.wait_ge(s_yc, (b + 1) * T)
                    link(pool.tensor_tensor(y_sb[:], y_sb[:], bc(g0_sb[:], T), ALU.mult))
                    after(pool, s_pool, 2 * b)
                    after(pool, s_x2, T * b)
                    pool.tensor_tensor(x1[:], y_sb[:], x_sb[:], ALU.add).then_inc(s_x1, 1)
                    pool.wait_ge(s_x1, b + 1)
                if t == 11:
                    pool.wait_ge(s_part, 2 * b + 1)
                    pool.tensor_tensor(qk[:], qk[:], parts[:, 0], ALU.subtract).then_inc(s_rest, 1)
                    pool.wait_ge(s_rest, b + 1)
                if t == 12:
                    pool.wait_ge(s_part, 2 * b + 2)
                    pool.tensor_tensor(parts[:, 2], qk[:], parts[:, 1], ALU.subtract).then_inc(s_split, 1)
                    pool.wait_ge(s_split, b + 1)

            def split_max(b, g):
                pool.wait_ge(s_negm, b * G + g + 1)
                after(pool, s_mrow, (b * G + g) * 48)
                a = nm[0:4 * T, :]
                alone(pool, s_passed_pool)
                link(pool.tensor_copy(nm_parts[:, 0, :], a))
                link(pool.tensor_tensor(a, a, nm_parts[:, 0, :], ALU.subtract))
                alone(pool, s_passed_pool)
                link(pool.tensor_copy(nm_parts[:, 1, :], a))
                pool.tensor_tensor(nm_parts[:, 2, :], a, nm_parts[:, 1, :], ALU.subtract).then_inc(s_nsplit, 1)
                pool.wait_ge(s_nsplit, b * G + g + 1)

            def v_copy(b, g):
                if g == 0:
                    pool.wait_ge(s_vc, b + 1)
                after(pool, s_pv, b * H + 4 * g + 4 - H)
                src = v_next[:, :, g * 4 * DH:(g + 1) * 4 * DH].rearrange("p t (h r) -> p t h r", h=4)
                alone(pool, s_passed_pool)
                pool.tensor_copy(V[:, :, 4 * g:4 * g + 4, 0:DH], src).then_inc(s_vcopy, 1)
                pool.wait_ge(s_vcopy, b * G + g + 1)

            def last_layer(b, t):
                if t == 9:
                    pool.wait_ge(s_loadf, (b + 1) * LOADF * 16)
                    pool.tensor_tensor(x3[:], x3[:], bc(bo_sb[:], T), ALU.add).then_inc(s_x3in, 1)
                if t == 11:
                    pool.wait_ge(s_x3, 2 * b + 2)
                    after(pool, s_out, 16 * b)
                    pool.tensor_tensor(y3[:], x3[:], bc(lb2_sb[:], T), ALU.add).then_inc(s_x3b, 1)
                    pool.wait_ge(s_x3b, b + 1)
                    pool.wait_ge(s_fT, 2 * C * (b + 1))
                    link(pool.tensor_tensor(x3[:], x3[:], bc(lb_sb[:], T), ALU.add))
                if t == 14:
                    pool.wait_ge(s_var3, b + 1)
                    newton(mv3[:, :, 1], rstd3, newt3, s_rstd3, b)
                    pool.wait_ge(s_y3c, (b + 1) * T)
                    link(pool.tensor_tensor(y3[:], y3[:], bc(lg_sb[:], T), ALU.mult))
                    pool.tensor_tensor(y3[:], y3[:], x3[:], ALU.add).then_inc(s_out_sb, 1)
                    pool.wait_ge(s_out_sb, b + 1)

            def iteration(b, is_p, is_a, is_f):
                for t in range(16):
                    if t == 0 and is_f:
                        split_max(b - 1, 3)
                    if t in (4, 8, 12) and is_a:
                        split_max(b, t // 4 - 1)
                    if t == 1 and is_a:
                        v_copy(b, 0)
                        v_copy(b, 1)
                    if t in (4, 8) and is_a:
                        v_copy(b, 1 + t // 4)
                    if is_p:
                        first_layers(b + 1, t)
                    if is_f:
                        last_layer(b - 1, t)

            link(pool.memset(ident[:], 0.0))
            pool.affine_select(out=ident[:], in_=ident[:], compare_op=ALU.not_equal, fill=1.0, base=0,
                               pattern=[[-1, P]], channel_multiplier=1).then_inc(s_ident, 1)
            pool.memset(ones[:], 1.0).then_inc(s_ident, 1)
            link(pool.memset(type_tab[:], 0.0))
            for k, (op, sign, off) in enumerate(((ALU.is_ge, 1, 0), (ALU.is_ge, -1, 0), (ALU.not_equal, 1, 0))):
                link(pool.affine_select(out=type_tab[:, k, 0:P], in_=type_tab[:, k, 0:P], compare_op=op, fill=NEG,
                                        base=0, pattern=[[-sign, P]], channel_multiplier=sign))
                m = type_tab[:, k, P:P + T * T].rearrange("p (a b) -> p a b", a=T)
                link(pool.affine_select(out=m, in_=m, compare_op=op, fill=NEG, base=0 if k == 2 else -1,
                                        pattern=[[sign, T], [-sign, T]], channel_multiplier=0))
            for k, (base, step) in enumerate(((1, 1), (S, -1))):
                link(pool.iota(type_tab[:, k, P + T * T:TW], [[step * P, T]], base=base, channel_multiplier=step,
                               allow_small_or_imprecise_dtypes=True))
            link(pool.memset(type_tab[:, 2, P + T * T:TW], float(S - 1)))
            pool.wait_ge(s_iota, 1)
            pool.iota(iota_f, [[1, S]], base=0, channel_multiplier=0,
                      allow_small_or_imprecise_dtypes=True).then_inc(s_iota, 1)
            pool.wait_ge(s_types, 1)
            for t in range(16):
                first_layers(0, t)
            iteration(0, True, True, False)
            start = seq.n
            with pool.Fori(FIRST, LAST) as b:
                seq.enter(b, FIRST, SEQ)
                iteration(b, True, True, True)
            seq.leave(LAST - FIRST, start)
            iteration(LAST, False, True, True)
            iteration(B, False, False, True)


_INS = ['x', 'xt', 'profile', 'prompt', 'indices', 'u_prev', 'language', 'blocked', 'blocked_t', 'index_ok',
        'wd', 'bd', 'wu', 'bu', 'ln0_g', 'ln0_b', 'w1', 'b1', 'v', 'wq_t', 'bq', 'wk_t', 'bk', 'wv_t', 'bv', 'wo_t', 'bo',
        'lw1', 'lb1', 'lw2', 'lb2', 'lg', 'lb']


def kernel(x, itok_B_0_6, itok_B_0_2, itok_Sx32_0_1023, condB_uprev, itok_B_0_8, mask_SxS_bk0, mask_Sx32_bk1,
           L0_cond_down_w, L0_cond_down_b, L0_cond_up_w, L0_cond_up_b, L0_cond_ln_g, L0_cond_ln_b,
           L1_cond_W1, L1_cond_b1, L1_cond_v, L2_cond_Wq, L2_cond_bq, L2_cond_Wk, L2_cond_bk, L2_cond_Wv, L2_cond_bv,
           L2_cond_Wo, L2_cond_bo, L3_cond_W1, L3_cond_b1, L3_cond_W2, L3_cond_b2, L3_cond_gamma, L3_cond_beta):
    import numpy as np
    import concourse.bacc as bacc
    from concourse import mybir as mb
    from concourse.bass_utils import run_bass_kernel_spmd as run

    x = np.asarray(x)
    mask = np.asarray(mask_SxS_bk0)
    data = dict(zip(_INS, [
        x, x.transpose(0, 2, 1), itok_B_0_6, itok_B_0_2, itok_Sx32_0_1023, condB_uprev, itok_B_0_8,
        mask, mask.T, mask_Sx32_bk1,
        L0_cond_down_w, L0_cond_down_b, L0_cond_up_w, L0_cond_up_b, L0_cond_ln_g, L0_cond_ln_b,
        L1_cond_W1, L1_cond_b1, L1_cond_v, np.asarray(L2_cond_Wq).T, np.asarray(L2_cond_bq).reshape(-1, P).T, np.asarray(L2_cond_Wk).T,
        np.asarray(L2_cond_bk).reshape(-1, P).T,
        np.asarray(L2_cond_Wv).T, L2_cond_bv, np.asarray(L2_cond_Wo).T, L2_cond_bo,
        L3_cond_W1, L3_cond_b1, L3_cond_W2, L3_cond_b2, L3_cond_gamma, L3_cond_beta]))
    nc = bacc.Bacc("TRN2", target_bir_lowering=False, num_devices=1)
    arrays, args = {}, []
    for name in _INS:
        a = np.ascontiguousarray(data[name])
        arrays[f"in_{name}"] = a
        args.append(nc.dram_tensor(f"in_{name}", a.shape, mb.dt.from_np(a.dtype), kind="ExternalInput").ap())
    o = nc.dram_tensor("out_0", x.shape, mb.dt.from_np(x.dtype), kind="ExternalOutput").ap()
    cond_resid(nc, *args, o)
    r = run(nc, [arrays], core_ids=[0])
    return r.results[0]["out_0"]
```

```python
from contextlib import ExitStack

import concourse.bass as bass
from concourse import mybir

ALU = mybir.AluOpType
ACT = mybir.ActivationFunctionType
AX_X = mybir.AxisListType.X
F32 = mybir.dt.float32
BF16 = mybir.dt.bfloat16
F16 = mybir.dt.float16
I32 = mybir.dt.int32
U8 = mybir.dt.uint8

P = 128
NEG = -1.0e30
EPS = 1.0e-5


def alone(eng, sem):
    eng.sem_inc(sem, 1)


class Count:

    def __init__(self):
        self.base, self.n, self.per = 0, 0, 0

    def enter(self, b, first, per):
        self.base, self.n, self.per = self.n + (b - first) * per, 0, per

    def leave(self, trips, start):
        assert self.n == self.per, (self.n, self.per)
        self.base, self.n = 0, start + trips * self.per

    @property
    def value(self):
        return self.base + self.n


def either(eng, live, counts, body):
    start = [c.n for c in counts]
    with eng.If(live > 0):
        body(True)
    end = [c.n for c in counts]
    for c, n in zip(counts, start):
        c.n = n
    with eng.Else():
        body(False)
    assert [c.n for c in counts] == end


def in_slots(eng, live, b, is_a, is_f, counts, slots):
    def reg(i):
        return eng.value_load(live[0:1, i:i + 1] if isinstance(i, int) else live[0:1, bass.ds(i, 1)],
                              min_val=0, max_val=1)
    if is_a and is_f:
        new, old = reg(b), reg(b - 1)
        either(eng, old, counts, lambda o: either(eng, new, counts, lambda n: slots(range(0, 8), n, o)))
        either(eng, new, counts, lambda n: slots(range(8, 16), n, n))
    elif is_a:
        either(eng, reg(b), counts, lambda n: slots(range(16), n, n))
    else:
        either(eng, reg(b - 1), counts, lambda o: slots(range(0, 8), o, o))
        slots(range(8, 16), False, False)


def after(eng, sem, count):
    if not isinstance(count, int) or count > 0:
        eng.wait_ge(sem, count)


def cond_resid(nc, x, xt, profile, prompt, indices, u_prev, language, blocked, blocked_t, index_ok,
               wd, bd, wu, bu, ln0_g, ln0_b, w1, b1, v, wq_t, bq, wk_t, bk, wv_t, bv, wo_t, bo,
               lw1, lb1, lw2, lb2, lg, lb, out):
    B, S, D = x.shape
    T = S // P
    C = D // P
    TN, SN = T // 2, S // 2
    H = 16
    DH = D // H
    NI = indices.shape[1]
    HP = 32
    G = H // 4
    PAIRS = [(0, 0), (0, 1), (1, 0), (0, 2), (2, 0), (1, 1)]
    NS = len(PAIRS)
    KR = NS * DH
    LAG_T, LAG_W, LAG_V = 6, 7, 8
    RING = 4
    A1 = w1.shape[1]
    A3 = lw1.shape[2]
    CONSTS = 17

    with ExitStack() as ctx:
        def sb(name, shape, dt=F32):
            return ctx.enter_context(nc.sbuf_tensor(name, shape, dt))

        def ps(name):
            return ctx.enter_context(nc.psum_tensor(name, [P, 512], F32))

        def sem(name):
            return ctx.enter_context(nc.semaphore(name))

        psS = [ps("psS0"), ps("psS1")]
        psT = [ps("psT0"), ps("psT1")]
        psO = ps("psO")
        psP = [ps("psP0"), ps("psP1")]
        psF = ps("psF")

        ident = sb("ident", [P, P])
        identb = sb("identb", [P, P], BF16)
        ones = sb("ones", [P, P])
        TW = P + T * T + T
        type_tab = sb("type_tab", [P, 3, TW])
        wq_sb, wk_sb, wv_sb, wo_sb = (sb(n, [P, C, D]) for n in ("wq_sb", "wk_sb", "wv_sb", "wo_sb"))
        bq_sb, bk_sb = sb("bq_sb", [P, C]), sb("bk_sb", [P, C])
        bqs = sb("bqs", [P, C])
        bv_sb, bo_sb = sb("bv_sb", [P, D]), sb("bo_sb", [P, D])
        w1_sb, b1_sb, v_sb, vbc = sb("w1_sb", [P, C, A1]), sb("b1_sb", [A1, 1]), sb("v_sb", [A1, 1]), sb("vbc", [A1, P])
        ids = sb("ids", [1, 2, B], I32)
        u_sb, ty_i = sb("u_sb", [P, B]), sb("ty_i", [P, B], I32)
        live_i = sb("live_i", [1, B], I32)
        far = sb("far", [P, 1])
        table = sb("table", [P, B, 8])
        tmp8 = sb("tmp8", [P, 3, B])
        idx_i, idx_ok = sb("idx_i", [P, T, NI], I32), sb("idx_ok", [P, T, NI], U8)
        idx_f, idx_m = sb("idx_f", [P, T, NI]), sb("idx_m", [P, T, NI])
        prob = sb("prob", [P, RING, T, S])
        hot = prob[:, 0].rearrange("p k s -> p (k s)").bitcast(BF16).rearrange("p (r s) -> p r s", s=S)
        blk8 = prob[:, 1, 0].bitcast(U8).rearrange("p (t s) -> p t s", t=T)
        blkt8 = prob[:, 1, 1].bitcast(U8).rearrange("p (t s) -> p t s", t=T)
        count_sb = prob[:, 2, 0:2].rearrange("p k s -> p (k s)").bitcast(BF16).rearrange("p (t s) -> p t s", t=T)
        iota_f = prob[:, 3, 0]
        iota_h = prob[:, 3, 1].bitcast(F16)[:, 0:S]
        unprior = sb("unprior", [P, T, S], BF16)
        unprior_t = sb("unprior_t", [P, T, S], BF16)
        unlisted = sb("unlisted", [P, T, S], BF16)
        count_t = sb("count_t", [P, T, S], BF16)

        x_sb = sb("x_sb", [P, T, D])
        xT = sb("xT", [P, C, S])
        wd_sb, bd_sb, wu_sb = sb("wd_sb", [P, C, P]), sb("bd_sb", [P, 1]), sb("wu_sb", [P, D])
        bu_sb, g0_sb, be0_sb = sb("bu_sb", [P, D]), sb("g0_sb", [P, D]), sb("be0_sb", [P, D])
        z_sb = sb("z_sb", [P, S])
        y_sb = sb("y_sb", [P, T, D])
        stats, mv, rstd = sb("stats", [P, T, 6]), sb("mv", [P, T, 2]), sb("rstd", [P, T])
        x1 = sb("x1", [P, T, D])
        h1 = sb("h1", [A1, S])
        typ = sb("typ", [P, TW])
        typ2 = sb("typ2", [P, TW])
        cur_m = sb("cur_m", [P, 8])
        col = sb("col", [P, T])
        bmax = sb("bmax", [P, T])
        masked = sb("masked", [P, T, P])
        m_in, m_neg = sb("m_in", [P, T]), sb("m_neg", [P, T])
        oth = sb("oth", [P, T, T])
        m_oth = sb("m_oth", [P, T])
        w_oth = sb("w_oth", [P, T, T])
        e_arg = sb("e_arg", [P, T])
        e_diag = sb("e_diag", [P, T, T])
        pin = sb("pin", [P, T, P])
        sum_in = sb("sum_in", [P, T])
        pinT = sb("pinT", [P, T, P])
        w_othT = sb("w_othT", [T, T, P])
        u_blk = sb("u_blk", [T, D])
        e_sum = sb("e_sum", [P, T])
        rec = sb("rec", [P, T])
        x2 = sb("x2", [P, T, D])
        qk = sb("qk", [P, 2 * C, S])
        parts = sb("parts", [P, 3, 2 * C, S], BF16)

        Qs = sb("Qs", [KR + 3, H, S], BF16)
        Ks = sb("Ks", [KR + 3, H, S], BF16)
        v_next = sb("v_next", [P, T, D])
        V = sb("V", [P, T, H, HP])
        cur_a, cur_w = sb("cur_a", [P, 4]), sb("cur_w", [P, 4])
        mask_a = sb("mask_a", [P, T, S], BF16)
        wgt = sb("wgt", [P, T, S])
        mx = sb("mx", [P, 2, 4, T])
        nm = sb("nm", [P, P])
        nm_parts = sb("nm_parts", [16, 3, P], BF16)
        oT_sb = sb("oT_sb", [P, S])
        orec = sb("orec", [P, T, 4])
        o_sb = sb("o_sb", [P, T, D])

        fT = sb("fT", [P, C, S])
        x3 = sb("x3", [P, T, D])
        y3 = sb("y3", [P, T, D])
        lw1_sb, lb1_sb, lw2_sb = sb("lw1_sb", [P, C, A3]), sb("lb1_sb", [A3, 1]), sb("lw2_sb", [A3, D])
        lb2_sb, lg_sb, lb_sb = sb("lb2_sb", [P, D]), sb("lg_sb", [P, D]), sb("lb_sb", [P, D])
        newt, newt3 = sb("newt", [P, T]), sb("newt3", [P, T])
        h3 = sb("h3", [A3, S])
        stats3, mv3, rstd3 = sb("stats3", [P, T, 6]), sb("mv3", [P, T, 2]), sb("rstd3", [P, T])

        x2_dram = nc.dram_tensor("x2_spill", (B, S, D), F32, kind="Internal").ap()
        st_dram = nc.dram_tensor("stacks", (2, H, NS, DH, S), BF16, kind="Internal").ap()

        s_const, s_ids = sem("s_const"), sem("s_ids")
        s_far, s_far_row, s_live = sem("s_far"), sem("s_far_row"), sem("s_live")
        s_passed, s_passed_pool = sem("s_passed"), sem("s_passed_pool")
        s_ident, s_types, s_iota, s_set = sem("s_ident"), sem("s_types"), sem("s_iota"), sem("s_set")
        s_e1, s_e2 = sem("s_e1"), sem("s_e2")
        s_hot, s_hot_used, s_cnt, s_cnt_read, s_ct, s_ct_read = (sem(n) for n in (
            "s_hot", "s_hot_used", "s_cnt", "s_cnt_read", "s_ct", "s_ct_read"))
        s_loadp, s_loadf = sem("s_loadp"), sem("s_loadf")
        s_p_read = [sem("s_p0_read"), sem("s_p1_read")]
        s_f_read = sem("s_f_read")
        s_z, s_zc, s_y, s_yc, s_x1, s_x1T, s_x1Tc, s_h, s_hc = (sem(n) for n in (
            "s_z", "s_zc", "s_y", "s_yc", "s_x1", "s_x1T", "s_x1Tc", "s_h", "s_hc"))
        s_var, s_rstd, s_var3, s_rstd3 = (sem(n) for n in ("s_var", "s_rstd", "s_var3", "s_rstd3"))
        s_xbu, s_typ, s_pinT = sem("s_xbu"), sem("s_typ"), sem("s_pinT")
        s_row, s_colf, s_colc, s_arg, s_exp1 = (sem(n) for n in ("s_row", "s_colf", "s_colc", "s_arg", "s_exp1"))
        s_pT, s_pTc, s_u, s_uc, s_pool, s_x2 = (sem(n) for n in ("s_pT", "s_pTc", "s_u", "s_uc", "s_pool", "s_x2"))
        s_x2T, s_x2Tc, s_qk, s_qkc, s_v, s_vc = (sem(n) for n in ("s_x2T", "s_x2Tc", "s_qk", "s_qkc", "s_v", "s_vc"))
        s_hi, s_rest, s_mid, s_lo = (sem(n) for n in ("s_hi", "s_rest", "s_mid", "s_lo"))
        s_stored = [sem(f"s_stored{c}") for c in range(C)]
        s_stack = [sem(f"s_stack{g}") for g in range(G)]
        s_spill, s_unspill = sem("s_spill"), sem("s_unspill")
        s_wgt, s_scores, s_max, s_mT, s_negm, s_nsplit, s_mrow = (sem(n) for n in (
            "s_wgt", "s_scores", "s_max", "s_mT", "s_negm", "s_nsplit", "s_mrow"))
        s_st, s_exp, s_wmul, s_vcopy, s_pv, s_oc, s_oT, s_o = (sem(n) for n in (
            "s_st", "s_exp", "s_wmul", "s_vcopy", "s_pv", "s_oc", "s_oT", "s_o"))
        s_fT, s_fTc, s_x3p, s_x3, s_x3in, s_x3b, s_h3, s_h3c, s_y3, s_y3c, s_out_sb, s_out = (sem(n) for n in (
            "s_fT", "s_fTc", "s_x3p", "s_x3", "s_x3in", "s_x3b", "s_h3", "s_h3c", "s_y3", "s_y3c", "s_out_sb", "s_out"))
        s_dve, s_pool_seq, s_vz = sem("s_dve"), sem("s_pool_seq"), sem("s_vz")

        def bc(ap, n):
            return ap.unsqueeze(1).to_broadcast([P, n, ap.shape[1]])

        block = ctx.enter_context(nc.Block())

        LOADP, LOADF = 8, 7
        FIRST, LAST = 1, B - 1

        @block.sync
        def _(sp):
            ra, rb, rm = sp.alloc_register("ra"), sp.alloc_register("rb"), sp.alloc_register("rm")

            def times(reg, b, per, c):
                if isinstance(b, int):
                    return b * per + c
                if c >= 0:
                    sp.reg_mul(rm, b, per)
                    sp.reg_add(reg, rm, c)
                else:
                    sp.reg_add(rm, b, -1)
                    sp.reg_mul(rm, rm, per)
                    sp.reg_add(reg, rm, per + c)
                return sp.snap(reg)

            def at(ap, i):
                return ap[i] if isinstance(i, int) else ap[bass.ds(i, 1)].squeeze(0)

            sp.dma_start(ids[0:1, 0, :], profile.unsqueeze(0)).then_inc(s_ids, 16)
            sp.dma_start(ids[0:1, 1, :], language.unsqueeze(0)).then_inc(s_ids, 16)
            sp.wait_ge(s_ids, 32)

            def load_xt(b):
                src = at(xt, b).rearrange("(c p) s -> p c s", p=P)
                w = times(ra, b, 2 * C, 0)
                after(sp, s_v, w)
                sp.dma_start(xT[:], src).then_inc(s_loadp, 16)

            def load_p(b):
                i = sp.value_load(ids[0:1, 0, b:b + 1] if isinstance(b, int) else ids[0:1, 0, bass.ds(b, 1)],
                                  min_val=0, max_val=wd.shape[0] - 1)
                src = [at(x, b).rearrange("(t p) d -> p t d", p=P),
                       at(wd, i).rearrange("(c p) k -> p c k", p=P), at(bd, i).unsqueeze(1), at(wu, i),
                       at(bu, i).unsqueeze(0).to_broadcast([P, D]), at(ln0_g, i).unsqueeze(0).to_broadcast([P, D]),
                       at(ln0_b, i).unsqueeze(0).to_broadcast([P, D])]
                dst = [x_sb[:], wd_sb[:], bd_sb[:], wu_sb[:], bu_sb[:], g0_sb[:], be0_sb[:]]
                w = times(ra, b, 1, 0)
                after(sp, s_x1, w)
                for d_, s_ in zip(dst, src):
                    sp.dma_start(d_, s_).then_inc(s_loadp, 16)

            def load_f(b):
                i = sp.value_load(ids[0:1, 1, b:b + 1] if isinstance(b, int) else ids[0:1, 1, bass.ds(b, 1)],
                                  min_val=0, max_val=lw1.shape[0] - 1)
                src = [at(lw1, i).rearrange("(c p) k -> p c k", p=P), at(lb1, i).unsqueeze(1), at(lw2, i),
                       at(lb2, i).unsqueeze(0).to_broadcast([P, D]), at(lg, i).unsqueeze(0).to_broadcast([P, D]),
                       at(lb, i).unsqueeze(0).to_broadcast([P, D])]
                dst = [lw1_sb[:], lb1_sb[:], lw2_sb[:], lb2_sb[:], lg_sb[:], lb_sb[:]]
                w = times(ra, b, 1, 0)
                after(sp, s_out_sb, w)
                for d_, s_ in zip(dst, src):
                    sp.dma_start(d_, s_).then_inc(s_loadf, 16)

            def unspill(b):
                w = times(ra, b, 16, 16)
                sp.wait_ge(s_spill, w)
                sp.dma_start(x3[:], at(x2_dram, b).rearrange("(t p) d -> p t d", p=P)).then_inc(s_loadf, 16)

            def spill(b):
                w = times(ra, b, T, T)
                sp.wait_ge(s_x2, w)
                sp.dma_start(at(x2_dram, b).rearrange("(t p) d -> p t d", p=P), x2[:]).then_inc(s_spill, 16)

            def store_stacks(b, c, part):
                made, per, n = ((s_hi, C, c + 1), (s_mid, C, c + 1), (s_lo, C, c + 1))[part]
                w = times(ra, b, per, n)
                sp.wait_ge(made, w)
                if part == 0 and c == 0:
                    w2 = times(rb, b, 32, 0)
                    for g in range(G):
                        after(sp, s_stack[g], w2)
                for side in range(2):
                    for j, pair in enumerate(PAIRS):
                        if pair[side] == part:
                            sp.dma_start(st_dram[side, c * H // C:(c + 1) * H // C, j],
                                         parts[:, part, side * C + c, :]).then_inc(s_stored[c], 16)

            def load_stack(b, g):
                w = times(ra, b, 2 * NS * 16, 2 * NS * 16)
                w2 = times(rb, b, H * T, (4 * g + 4 - H) * T)
                sp.wait_ge(s_stored[g * C // G], w)
                after(sp, s_st, w2)
                for side, dst in enumerate((Qs, Ks)):
                    sp.dma_start(dst[0:KR, 4 * g:4 * g + 4, :],
                                 st_dram[side, 4 * g:4 * g + 4].rearrange("h j d s -> (j d) h s")).then_inc(s_stack[g], 16)

            def load_mrow(b, g):
                w = times(ra, b, G, g + 1)
                w2 = times(rb, b, H * T, (4 * g + 4 - H) * T)
                sp.wait_ge(s_nsplit, w)
                after(sp, s_st, w2)
                for k in range(3):
                    dst = Qs[KR + k:KR + k + 1, 4 * g:4 * g + 4, :].rearrange("o h s -> o (h s)")
                    sp.dma_start(dst, nm_parts[:, k, :]).then_inc(s_mrow, 16)

            def store_out(b):
                dst = at(out, b).rearrange("(t p) d -> p t d", p=P)
                w = times(ra, b, 1, 1)
                sp.wait_ge(s_out_sb, w)
                sp.dma_start(dst, y3[:]).then_inc(s_out, 16)

            def iteration(b, is_p, is_a, is_f, more=True):
                for t in range(16):
                    if t == 0 and is_f:
                        load_mrow(b - 1, 3)
                        load_f(b - 1)
                    if t == 1 and is_f:
                        unspill(b - 1)
                    if t == 2 and is_a and b is not None and is_f:
                        load_stack(b, 2)
                    if t == 6 and is_a and is_f:
                        load_stack(b, 3)
                    if t in (5, 9, 13) and is_a:
                        load_mrow(b, t // 4 - 1)
                    if t == 8 and is_p and more:
                        load_p(b + 2)
                    if t == 10 and is_p:
                        spill(b + 1)
                    if t == 12 and is_p:
                        store_stacks(b + 1, 0, 0)
                    if t == 13 and is_p:
                        store_stacks(b + 1, 0, 1)
                        store_stacks(b + 1, 0, 2)
                        load_stack(b + 1, 0)
                        if more:
                            load_xt(b + 2)
                    if t == 14 and is_p:
                        load_stack(b + 1, 1)
                        for part in range(3):
                            store_stacks(b + 1, 1, part)
                    if t == 15 and is_f:
                        store_out(b - 1)

            load_xt(0)
            load_p(0)
            n = 0
            for d_, s_ in [
                (w1_sb[:], w1.rearrange("(c p) a -> p c a", p=P)), (b1_sb[:], b1.unsqueeze(1)), (v_sb[:], v.unsqueeze(1)),
                (u_sb[:], u_prev.unsqueeze(0).to_broadcast([P, B])), (ty_i[:], prompt.unsqueeze(0).to_broadcast([P, B])),
                (idx_i[:], indices.rearrange("(t p) i -> p t i", p=P)), (idx_ok[:], index_ok.rearrange("(t p) i -> p t i", p=P)),
                (wq_sb[:], wq_t.rearrange("(c p) n -> p c n", p=P)), (wk_sb[:], wk_t.rearrange("(c p) n -> p c n", p=P)),
                (wv_sb[:], wv_t.rearrange("(c p) n -> p c n", p=P)), (wo_sb[:], wo_t.rearrange("(c p) n -> p c n", p=P)),
                (bq_sb[:], bq), (bk_sb[:], bk),
                (bv_sb[:], bv.unsqueeze(0).to_broadcast([P, D])), (bo_sb[:], bo.unsqueeze(0).to_broadcast([P, D])),
                (blk8, blocked.rearrange("(t p) k -> p t k", p=P)), (blkt8, blocked_t.rearrange("(t p) k -> p t k", p=P)),
            ]:
                sp.dma_start(d_, s_).then_inc(s_const, 16)
                n += 1
            assert n == CONSTS
            load_p(1)
            spill(0)
            for c in range(C):
                for part in range(3):
                    store_stacks(0, c, part)
            load_xt(1)
            for g in range(G):
                load_stack(0, g)
            iteration(0, True, True, False)
            with sp.Fori(FIRST, LAST - 1) as b:
                iteration(b, True, True, True)
            iteration(LAST - 1, True, True, True, more=False)
            iteration(LAST, False, True, True)
            iteration(B, False, False, True)
            sp.wait_ge(s_out, 16 * B)

        @block.tensor
        def _(pe):
            P_USES = (11, 10)
            F_USES = 17
            p_used = [Count(), Count()]
            f_used = Count()

            def bank(k, b):
                after(pe, s_p_read[k], b * P_USES[k] + p_used[k].n)
                p_used[k].n += 1
                return psP[k]

            def fbank():
                after(pe, s_f_read, f_used.value)
                f_used.n += 1
                return psF

            def counts(t):
                for i in range(NI):
                    n = t * NI + i
                    pe.wait_ge(s_hot, n + 1)
                    if i == 0 and t >= 2:
                        pe.wait_ge(s_cnt_read, t - 1)
                    mm = pe.matmul(psS[t % 2][:], identb[:], hot[:, n % 8, :], start=(i == 0), stop=(i == NI - 1))
                    if i < NI - 1:
                        mm.then_inc(s_hot_used, 1)
                mm.then_inc(s_cnt, 1)

            def counts_t():
                for k in range(T):
                    pe.wait_ge(s_cnt_read, T)
                    if k >= 2:
                        pe.wait_ge(s_ct_read, k - 1)
                    dst = psT[k % 2][:].bitcast(BF16)
                    for t in range(T):
                        mm = pe.transpose(dst[:, t * P:(t + 1) * P], count_sb[:, t, k * P:(k + 1) * P], identb[:])
                    mm.then_inc(s_ct, 1)

            def turned(src, dst, c, sem_):
                for t in range(T):
                    mm = pe.transpose(dst[:, t * P:(t + 1) * P], src[:, t, c * P:(c + 1) * P], ident[:])
                mm.then_inc(sem_, 1)

            def first_layers(b, t):
                if t == 0:
                    p_used[0].n = p_used[1].n = 0
                    pe.wait_ge(s_loadp, (b + 1) * LOADP * 16)
                    dst = bank(0, b)
                    for c in range(C):
                        mm = pe.matmul(dst[:], wd_sb[:, c, :], xT[:, c, :], start=(c == 0), stop=(c == C - 1))
                    mm.then_inc(s_z, 1)
                if t == 1:
                    pe.wait_ge(s_zc, b + 1)
                    for k in range(2):
                        dst = bank(1 - k, b)
                        for i in range(2):
                            mm = pe.matmul(dst[:, i * D:(i + 1) * D], z_sb[:, (2 * k + i) * P:(2 * k + i + 1) * P], wu_sb[:],
                                           start=True, stop=True)
                        mm.then_inc(s_y, 1)
                if t == 4:
                    pe.wait_ge(s_x1, b + 1)
                    for c in range(C):
                        turned(x1, bank(1 - c, b), c, s_x1T)
                if t == 5:
                    pe.wait_ge(s_x1Tc, (b + 1) * C)
                    dst = bank(1, b)
                    for c in range(C):
                        mm = pe.matmul(dst[0:A1, :], w1_sb[:, c, :], xT[:, c, :], start=(c == 0), stop=(c == C - 1))
                    mm.then_inc(s_h, 1)
                if t == 6:
                    pe.wait_ge(s_hc, b + 1)
                    dst = bank(0, b)
                    pe.matmul(dst[:], vbc[:], h1[:], start=True, stop=True).then_inc(s_row, 1)
                    dst = bank(1, b)
                    for i in range(T):
                        mm = pe.matmul(dst[:, i:i + 1], h1[:, i * P:(i + 1) * P], v_sb[:], start=True, stop=True)
                    mm.then_inc(s_colf, 1)
                if t == 7.5:
                    pe.wait_ge(s_exp1, (b + 1) * (T + 2))
                    dst = bank(0, b)
                    for i in range(T):
                        mm = pe.transpose(dst[:, i * P:(i + 1) * P], pin[:, i, :], ident[:])
                    mm.then_inc(s_pT, 1)
                    dst = bank(1, b)
                    for i in range(T):
                        mm = pe.transpose(dst[0:T, i * P:(i + 1) * P], w_oth[:, i, :], ident[:])
                    mm.then_inc(s_pT, 1)
                if t == 8:
                    dst = bank(0, b)
                    for i in range(T):
                        pe.matmul(dst[:, D:D + T], ones[:], e_diag[:, i, :], start=(i == 0), stop=(i == T - 1))
                    for i in range(T):
                        mm = pe.matmul(dst[0:T, 0:D], e_diag[:, i, :], x1[:, i, :], start=(i == 0), stop=(i == T - 1))
                    mm.then_inc(s_u, 1)
                if t == 9:
                    pe.wait_ge(s_pinT, b + 1)
                    pe.wait_ge(s_pTc, b + 1)
                    pe.wait_ge(s_uc, 2 * b + 2)
                    for k in range(2):
                        dst = bank(1 - k, b)
                        for i in range(2):
                            j = 2 * k + i
                            pe.matmul(dst[:, i * D:(i + 1) * D], pinT[:, j, :], x1[:, j, :], start=True, stop=False)
                            mm = pe.matmul(dst[:, i * D:(i + 1) * D], w_othT[:, j, :], u_blk[:], start=False, stop=True)
                        mm.then_inc(s_pool, 1)
                if t == 10:
                    pe.wait_ge(s_x2, (b + 1) * T)
                    for c in range(C):
                        turned(x2, bank(1 - c, b), c, s_x2T)
                if t in (11, 12):
                    o = t - 11
                    pe.wait_ge(s_x2Tc, (b + 1) * C)
                    for side, w_sb in enumerate((wq_sb, wk_sb)):
                        dst = bank(1 - side, b)
                        for c in range(C):
                            mm = pe.matmul(dst[:], w_sb[:, c, o * P:(o + 1) * P], xT[:, c, :], start=(c == 0), stop=(c == C - 1))
                        mm.then_inc(s_qk, 1)
                if t == 13:
                    for k in range(2):
                        dst = bank(1 - k, b)
                        for i in range(2):
                            j = 2 * k + i
                            for c in range(C):
                                mm = pe.matmul(dst[:, i * D:(i + 1) * D], xT[:, c, j * P:(j + 1) * P], wv_sb[:, c, :],
                                               start=(c == 0), stop=(c == C - 1))
                            mm.then_inc(s_v, 1)
                    assert (p_used[0].n, p_used[1].n) == P_USES, p_used

            def scores(b, h, t, wide):
                if h % 4 == 0 and t == 0:
                    pe.wait_ge(s_stack[h // 4], (b + 1) * 32)
                i = b * (H * T) + h * T + t
                after(pe, s_max, i - 1)
                n = S if wide else SN
                pe.matmul(psS[t % 2][:, 0:n], Qs[0:KR, h, t * P:(t + 1) * P], Ks[0:KR, h, 0:n], start=True, stop=True)\
                    .then_inc(s_scores, 1)

            def scores_t(b, h, k, wide):
                if h % 4 == 0 and k == 0:
                    pe.wait_ge(s_mrow, (b * G + h // 4 + 1) * 48)
                i = b * (H * T) + h * T + k
                after(pe, s_exp, i - 1)
                pe.matmul(psT[k % 2][:], Ks[:, h, k * P:(k + 1) * P], Qs[:, h, :], start=True, stop=True)\
                    .then_inc(s_st, 1 if wide else 2)

            def output(b, h, k, wide):
                n = T if wide else TN
                if k in (0, n // 2):
                    pe.wait_ge(s_wmul, 2 * (b * H + h) + (1 if k == 0 else 2))
                if h % 4 == 0 and k == 0:
                    pe.wait_ge(s_vcopy, b * G + h // 4 + 1)
                    after(pe, s_oc, b * G + h // 4)
                r = HP * (h % 4)
                mm = pe.matmul(psO[r:r + HP, :], V[:, k, h, :], prob[:, h % RING, k, :], start=(k == 0), stop=(k == n - 1))
                if k == n - 1:
                    mm.then_inc(s_pv, 1)

            def max_turned(b, g):
                pe.wait_ge(s_max, b * (H * T) + (g + 1) * 4 * T)
                dst = fbank()
                pe.transpose(dst[0:4 * T, 0:P], mx[:, g % 2].rearrange("p h t -> p (h t)"), ident[:]).then_inc(s_mT, 1)

            def output_turned(b, g):
                pe.wait_ge(s_oc, b * G + g + 1)
                dst = fbank()
                for t in range(T):
                    mm = pe.transpose(dst[:, t * P:(t + 1) * P], oT_sb[:, t * P:(t + 1) * P], ident[:])
                mm.then_inc(s_oT, 1)

            def last_layer(b, t):
                if t == 9:
                    pe.wait_ge(s_o, (b + 1) * G)
                    for c in range(C):
                        turned(o_sb, fbank(), c, s_fT)
                if t in (10, 10.5):
                    k = int(t > 10)
                    if k == 0:
                        pe.wait_ge(s_fTc, 2 * C * b + C)
                    dst = fbank()
                    for i in range(2):
                        j = 2 * k + i
                        for c in range(C):
                            mm = pe.matmul(dst[:, i * D:(i + 1) * D], fT[:, c, j * P:(j + 1) * P], wo_sb[:, c, :],
                                           start=(c == 0), stop=(c == C - 1))
                    mm.then_inc(s_x3p, 1)
                if t == 11.5:
                    pe.wait_ge(s_x3, 2 * b + 2)
                    for c in range(C):
                        turned(x3, fbank(), c, s_fT)
                if t == 12:
                    pe.wait_ge(s_fTc, 2 * C * (b + 1))
                    pe.wait_ge(s_loadf, (b + 1) * LOADF * 16)
                    dst = fbank()
                    for c in range(C):
                        mm = pe.matmul(dst[0:A3, :], lw1_sb[:, c, :], fT[:, c, :], start=(c == 0), stop=(c == C - 1))
                    mm.then_inc(s_h3, 1)
                if t in (13, 13.5):
                    k = int(t > 13)
                    if k == 0:
                        pe.wait_ge(s_h3c, b + 1)
                    dst = fbank()
                    for i in range(2):
                        j = 2 * k + i
                        mm = pe.matmul(dst[:, i * D:(i + 1) * D], h3[:, j * P:(j + 1) * P], lw2_sb[:], start=True, stop=True)
                    mm.then_inc(s_y3, 1)

            WIDE = "S0 S1 T0 T1 V0 S2 T2 V1 S3 T3 V2 V3".split()
            NARROW = "S0 S1 T0 T1 V0 S2 V1 S3".split()

            def slots(b, is_p, is_a, is_f, span, new, old):
                for t in span:
                    for step in WIDE if new or old else NARROW:
                        stage, k = step[0], int(step[1])
                        lag, run = {"S": (0, scores), "T": (LAG_T, scores_t), "V": (LAG_V, output)}[stage]
                        if t >= lag and is_a and (stage == "S" or new or k < TN):
                            run(b, t - lag, k, new)
                        if t < lag and is_f and (old or k < TN):
                            run(b - 1, t - lag + H, k, old)
                        if step == "V0":
                            if t == 0 and is_f:
                                max_turned(b - 1, 3)
                            if t in (4, 8, 12) and is_a:
                                max_turned(b, t // 4 - 1)
                            if is_p:
                                first_layers(b + 1, t - 0.5)
                            if is_f:
                                last_layer(b - 1, t - 0.5)
                    if t in (0, 4, 8) and is_f:
                        output_turned(b - 1, t // 4 + 1)
                    if t == 12 and is_a:
                        output_turned(b, 0)
                    if is_p:
                        first_layers(b + 1, t)
                    if is_f:
                        last_layer(b - 1, t)

            def iteration(b, is_p, is_a, is_f):
                in_slots(pe, live_i, b, is_a, is_f, [*p_used, f_used],
                         lambda span, new, old: slots(b, is_p, is_a, is_f, span, new, old))

            pe.wait_ge(s_ident, 3)
            pe.wait_ge(s_const, 16 * CONSTS)
            for t in range(16):
                if t == 5:
                    pe.wait_ge(s_set, 1)
                first_layers(0, t - 0.5)
                first_layers(0, t)
                if t in (1, 4, 5, 6):
                    counts((1, 4, 5, 6).index(t))
            counts_t()
            pe.wait_ge(s_far, 1)
            pe.matmul(psO[0:1, 0:P], far[:], ident[:], start=True, stop=True).then_inc(s_far_row, 1)
            pe.wait_ge(s_ct_read, T)
            pe.wait_ge(s_live, 1)
            iteration(0, True, True, False)
            start = f_used.n
            with pe.Fori(FIRST, LAST) as b:
                f_used.enter(b, FIRST, F_USES)
                iteration(b, True, True, True)
            f_used.leave(LAST - FIRST, start)
            iteration(LAST, False, True, True)
            iteration(B, False, False, True)

        @block.scalar
        def _(act):
            def exps(b, h, tiles, wide):
                if tiles[0] == 0:
                    after(act, s_pv, b * H + h + 1 - RING)
                each = 1 if wide else 2
                for k in tiles:
                    act.wait_ge(s_st, b * (H * T) + h * T + each * (k + 1))
                    act.activation(prob[:, h % RING, k, :], psT[k % 2][:], ACT.Exp).then_inc(s_exp, each)

            def out_copy(b, g):
                act.wait_ge(s_pv, b * H + 4 * g + 4)
                after(act, s_oT, b * G + g)
                act.copy(oT_sb[:], psO[:]).then_inc(s_oc, 1)

            def first_layers(b, t):
                if t == 0:
                    act.wait_ge(s_z, b + 1)
                    after(act, s_y, 2 * b)
                    act.activation(z_sb[:], psP[0][:], ACT.Relu, bias=bd_sb[:]).then_inc(s_zc, 1)
                    act.wait_ge(s_zc, b + 1)
                    act.sem_inc(s_p_read[0], 1)
                if t == 4:
                    for c in range(C):
                        act.wait_ge(s_x1T, b * C + c + 1)
                        act.copy(xT[:, c, :], psP[1 - c][:]).then_inc(s_x1Tc, 1)
                        act.wait_ge(s_x1Tc, b * C + c + 1)
                        act.sem_inc(s_p_read[1 - c], 1)
                if t == 5:
                    act.wait_ge(s_h, b + 1)
                    after(act, s_colf, b)
                    act.activation(h1[:], psP[1][0:A1, :], ACT.Tanh, bias=b1_sb[:]).then_inc(s_hc, 1)
                    act.wait_ge(s_hc, b + 1)
                    act.sem_inc(s_p_read[1], 1)
                if t == 6:
                    act.wait_ge(s_colf, b + 1)
                    after(act, s_arg, b)
                    act.copy(col[:], psP[1][:, 0:T]).then_inc(s_colc, 1)
                    act.wait_ge(s_colc, b + 1)
                    act.sem_inc(s_p_read[1], 1)
                if t == 7:
                    act.wait_ge(s_arg, b + 1)
                    after(act, s_pT, 2 * b)
                    after(act, s_u, b)
                    for i in range(T):
                        act.activation(pin[:, i, :], masked[:, i, :], ACT.Exp, bias=m_neg[:, i:i + 1],
                                       accum_out=sum_in[:, i:i + 1]).then_inc(s_exp1, 1)
                    act.activation(w_oth[:], oth[:], ACT.Exp).then_inc(s_exp1, 1)
                    act.activation(e_diag[:].rearrange("p a b -> p (a b)")[:, 0:T * T:T + 1], e_arg[:], ACT.Exp)\
                       .then_inc(s_exp1, 1)
                if t == 8:
                    act.wait_ge(s_pT, 2 * b + 1)
                    act.copy(pinT[:].rearrange("p a b -> p (a b)"), psP[0][:]).then_inc(s_pinT, 1)
                    act.wait_ge(s_pinT, b + 1)
                    act.sem_inc(s_p_read[0], 1)
                    act.wait_ge(s_pT, 2 * b + 2)
                    after(act, s_pool, 2 * b)
                    act.copy(w_othT[:].rearrange("p a b -> p (a b)"), psP[1][0:T, :]).then_inc(s_pTc, 1)
                    act.wait_ge(s_pTc, b + 1)
                    act.sem_inc(s_p_read[1], 1)
                    act.wait_ge(s_u, b + 1)
                    after(act, s_x2, T * b)
                    act.copy(u_blk[:], psP[0][0:T, 0:D]).then_inc(s_uc, 1)
                    act.copy(e_sum[:], psP[0][:, D:D + T]).then_inc(s_uc, 1)
                    act.wait_ge(s_uc, 2 * b + 2)
                    act.sem_inc(s_p_read[0], 1)
                if t == 10:
                    for c in range(C):
                        act.wait_ge(s_x2T, b * C + c + 1)
                        act.copy(xT[:, c, :], psP[1 - c][:]).then_inc(s_x2Tc, 1)
                        act.wait_ge(s_x2Tc, b * C + c + 1)
                        act.sem_inc(s_p_read[1 - c], 1)
                if t in (11, 12):
                    o = t - 11
                    after(act, s_lo, b * C)
                    after(act, s_stored[o], b * 2 * NS * 16)
                    for side, (bias, scale) in enumerate(((bqs, DH ** -0.5), (bk_sb, 1.0))):
                        i = side * C + o
                        act.wait_ge(s_qk, b * 2 * C + 2 * o + side + 1)
                        act.activation(qk[:, i, :], psP[1 - side][:], ACT.Identity, bias=bias[:, o:o + 1], scale=scale)\
                           .then_inc(s_qkc, 1)
                        act.activation(parts[:, 0, i, :], psP[1 - side][:], ACT.Identity, bias=bias[:, o:o + 1],
                                       scale=scale).then_inc(s_qkc, 1)
                        act.wait_ge(s_qkc, 2 * (b * 2 * C + 2 * o + side + 1))
                        act.sem_inc(s_p_read[1 - side], 1)
                    act.sem_inc(s_hi, 1)

            def neg_max(b, g):
                act.wait_ge(s_mT, b * G + g + 1)
                after(act, s_nsplit, b * G + g)
                act.mul(nm[0:4 * T, :], psF[0:4 * T, 0:P], -1.0).then_inc(s_negm, 1)
                act.wait_ge(s_negm, b * G + g + 1)
                act.sem_inc(s_f_read, 1)

            def last_layer(b, t):
                if t in (9, 11.5):
                    for c in range(C):
                        i = b * 2 * C + (C if t > 9 else 0) + c + 1
                        act.wait_ge(s_fT, i)
                        if t == 9 and c == 0:
                            after(act, s_h3, b)
                        if t > 9 and c == 0:
                            act.wait_ge(s_x3p, 2 * b + 2)
                        act.copy(fT[:, c, :], psF[:]).then_inc(s_fTc, 1)
                        act.wait_ge(s_fTc, i)
                        act.sem_inc(s_f_read, 1)
                if t == 12:
                    act.wait_ge(s_h3, b + 1)
                    after(act, s_y3, 2 * b)
                    act.activation(h3[:], psF[0:A3, :], ACT.Relu, bias=lb1_sb[:]).then_inc(s_h3c, 1)
                    act.wait_ge(s_h3c, b + 1)
                    act.sem_inc(s_f_read, 1)

            def slots(b, is_p, is_a, is_f, span, new, old):
                for t in span:
                    for tiles in (range(0, 2), range(2, T)):
                        if t >= LAG_T and is_a and (new or tiles[0] < TN):
                            exps(b, t - LAG_T, tiles, new)
                        if t < LAG_T and is_f and (old or tiles[0] < TN):
                            exps(b - 1, t - LAG_T + H, tiles, old)
                        if tiles[0] > 0:
                            break
                        if t == 0 and is_f:
                            neg_max(b - 1, 3)
                        if t in (4, 8, 12) and is_a:
                            neg_max(b, t // 4 - 1)
                        if is_f:
                            last_layer(b - 1, t - 0.5)
                    if t == 11 and is_a:
                        out_copy(b, 0)
                    if t == 15 and is_a:
                        out_copy(b, 1)
                    if t in (3, 7) and is_f:
                        out_copy(b - 1, 2 + t // 4)
                    if is_p:
                        first_layers(b + 1, t)
                    if is_f:
                        last_layer(b - 1, t)

            def iteration(b, is_p, is_a, is_f):
                in_slots(act, live_i, b, is_a, is_f, [],
                         lambda span, new, old: slots(b, is_p, is_a, is_f, span, new, old))

            act.wait_ge(s_loadp, LOADP * 16)
            act.wait_ge(s_const, 16 * CONSTS)
            act.activation(tmp8[:, 0, :], u_sb[:], ACT.Exp, scale=-5.0).then_inc(s_e1, 1)
            act.wait_ge(s_e2, 1)
            act.activation(tmp8[:, 2, :], tmp8[:, 1, :], ACT.Exp, scale=-1.0).then_inc(s_e1, 1)
            for t in range(16):
                if t == 5:
                    act.wait_ge(s_vz, 2)
                if t == 10:
                    act.wait_ge(s_set, 1)
                first_layers(0, t)
            for k in range(T):
                act.wait_ge(s_ct, k + 1)
                act.copy(count_t[:, k, :], psT[k % 2][:].bitcast(BF16)[:, 0:S]).then_inc(s_ct_read, 1)
            act.wait_ge(s_live, 1)
            iteration(0, True, True, False)
            with act.Fori(FIRST, LAST) as b:
                iteration(b, True, True, True)
            iteration(LAST, False, True, True)
            iteration(B, False, False, True)

        @block.vector
        def _(dve):
            seq = Count()
            SEQ = 65

            def link(ins):
                ins.then_inc(s_dve, 1)
                seq.n += 1
                dve.wait_ge(s_dve, seq.value)

            def skip(n):
                dve.sem_inc(s_dve, n)
                seq.n += n

            def moments(y, st, m, r, s_var):
                for t in range(T):
                    ins = dve.bn_stats(st[:, t, :], y[:, t, :])
                    if t < T - 1:
                        ins.then_inc(s_dve, 1)
                        seq.n += 1
                link(ins)
                alone(dve, s_passed)
                for t in range(T):
                    ins = dve.bn_aggr(m[:, t, :], st[:, t, :])
                    if t < T - 1:
                        ins.then_inc(s_dve, 1)
                        seq.n += 1
                link(ins)
                link(dve.tensor_scalar(m[:, :, 1], m[:, :, 1], EPS, None, ALU.add))
                bits = r[:].bitcast(I32)
                link(dve.tensor_scalar(bits, m[:, :, 1].bitcast(I32), 1, None, ALU.logical_shift_right))
                link(dve.tensor_scalar(bits, bits, -1.0, float(0x5F3759DF), ALU.mult, ALU.add))
                dve.sem_inc(s_var, 1)

            def maxima(b, h, tiles, wide):
                n, mask = (S, mask_a) if wide else (SN, unlisted)
                for t in tiles:
                    i = b * (H * T) + h * T + t
                    dve.wait_ge(s_scores, i + 1)
                    if h % 4 == 0 and t == 0:
                        after(dve, s_mT, b * G + h // 4 - 1)
                    alone(dve, s_passed)
                    s = psS[t % 2][:, 0:n]
                    dve.tensor_tensor_reduce(s, s, mask[:, t, 0:n], 1.0, NEG, ALU.add, ALU.max,
                                             mx[:, (h // 4) % 2, h % 4, t:t + 1]).then_inc(s_max, 1)

            def weight(b, h, half, wide):
                n = (T if wide else TN) // 2
                if half == 0:
                    dve.wait_ge(s_exp, b * (H * T) + (h + 1) * T)
                k = slice(half * n, (half + 1) * n)
                p = prob[:, h % RING, k].rearrange("p k s -> p (k s)")
                by = (wgt if wide else count_t)[:, k].rearrange("p k s -> p (k s)")
                dve.scalar_tensor_tensor(out=p, in0=p, scalar=-NEG, in1=by, op0=ALU.min, op1=ALU.mult).then_inc(s_wmul, 1)

            def mask_for(b):
                after(dve, s_max, b * (H * T))
                src = table[:, b, 0:4] if isinstance(b, int) else table[:, bass.ds(b, 1), 0:4].squeeze(1)
                alone(dve, s_passed)
                link(dve.tensor_copy(cur_a[:], src))
                link(dve.tensor_scalar(mask_a[:], unprior[:], cur_a[:, 1:2], None, ALU.mult))
                link(dve.scalar_tensor_tensor(out=mask_a[:], in0=unlisted[:], scalar=cur_a[:, 0:1], in1=mask_a[:],
                                              op0=ALU.mult, op1=ALU.add))

            def weights_for(b):
                after(dve, s_wmul, 2 * b * H)
                src = table[:, b, 0:4] if isinstance(b, int) else table[:, bass.ds(b, 1), 0:4].squeeze(1)
                alone(dve, s_passed)
                link(dve.tensor_copy(cur_w[:], src))
                link(dve.tensor_scalar(wgt[:], unprior_t[:], cur_w[:, 3:4], cur_w[:, 2:3], ALU.mult, ALU.add))
                link(dve.scalar_tensor_tensor(out=wgt[:], in0=count_t[:], scalar=cur_w[:, 0:1], in1=wgt[:],
                                              op0=ALU.mult, op1=ALU.add))

            def normalize(b, g):
                dve.wait_ge(s_oT, b * G + g + 1)
                after(dve, s_fT, 2 * C * b)
                src = psF[:].rearrange("p (t h r) -> p t h r", t=T, h=4)
                link(dve.reciprocal(orec[:], src[:, :, :, DH]))
                dst = o_sb[:, :, g * 4 * DH:(g + 1) * 4 * DH].rearrange("p t (h r) -> p t h r", h=4)
                for t in range(T):
                    ins = dve.tensor_tensor(dst[:, t], src[:, t, :, 0:DH],
                                            orec[:, t].unsqueeze(2).to_broadcast([P, 4, DH]), ALU.mult)
                    if t < T - 1:
                        ins.then_inc(s_dve, 1)
                        seq.n += 1
                ins.then_inc(s_o, 1)
                dve.wait_ge(s_o, b * G + g + 1)
                dve.sem_inc(s_f_read, 1)

            def first_layers(b, t):
                if t == 1:
                    dve.wait_ge(s_xbu, 2 * b + 1)
                    for k in range(2):
                        dve.wait_ge(s_y, 2 * b + k + 1)
                        y = y_sb[:, 2 * k:2 * k + 2, :].rearrange("p t d -> p (t d)")
                        link(dve.tensor_tensor(y, psP[1 - k][:], y, ALU.add))
                        dve.sem_inc(s_p_read[1 - k], 1)
                    moments(y_sb, stats, mv, rstd, s_var)
                if t == 2:
                    dve.wait_ge(s_rstd, b + 1)
                    for t_ in range(T):
                        dve.tensor_scalar(y_sb[:, t_, :], y_sb[:, t_, :], mv[:, t_, 0:1], rstd[:, t_:t_ + 1],
                                          ALU.subtract, ALU.mult).then_inc(s_yc, 1)
                if t == 6:
                    dve.wait_ge(s_typ, b + 1)
                    dve.wait_ge(s_row, b + 1)
                    after(dve, s_exp1, b * (T + 2))
                    row = psP[0][:].rearrange("p (t l) -> p t l", t=T)
                    link(dve.tensor_reduce(bmax[:], row, AX_X, ALU.max))
                    alone(dve, s_passed)
                    for i in range(T):
                        ins = dve.tensor_tensor_reduce(masked[:, i, :], row[:, i, :], typ[:, 0:P], 1.0, NEG,
                                                       ALU.add, ALU.max, m_in[:, i:i + 1])
                        if i < T - 1:
                            ins.then_inc(s_dve, 1)
                            seq.n += 1
                    link(ins)
                    dve.sem_inc(s_p_read[0], 1)
                    dve.wait_ge(s_colc, b + 1)
                    link(dve.tensor_tensor(oth[:], bmax[:].unsqueeze(1).to_broadcast([P, T, T]),
                                           typ[:, P:P + T * T].rearrange("p (a b) -> p a b", a=T), ALU.add))
                    link(dve.tensor_reduce(m_oth[:], oth[:], AX_X, ALU.max))
                    link(dve.tensor_tensor(m_in[:], m_in[:], m_oth[:], ALU.max))
                    link(dve.tensor_scalar(m_neg[:], m_in[:], -1.0, None, ALU.mult))
                    link(dve.tensor_tensor(oth[:], oth[:], m_in[:].unsqueeze(2).to_broadcast([P, T, T]), ALU.subtract))
                    dve.tensor_tensor(e_arg[:], col[:], bmax[:], ALU.subtract).then_inc(s_arg, 1)
                if t == 8:
                    dve.wait_ge(s_uc, 2 * b + 2)
                    link(dve.tensor_tensor(oth[:], w_oth[:], e_sum[:].unsqueeze(1).to_broadcast([P, T, T]), ALU.mult))
                    link(dve.tensor_reduce(m_oth[:], oth[:], AX_X, ALU.add))
                    link(dve.tensor_tensor(m_oth[:], m_oth[:], sum_in[:], ALU.add))
                    link(dve.tensor_tensor(m_oth[:], m_oth[:], typ[:, P + T * T:TW], ALU.mult))
                    link(dve.reciprocal(rec[:], m_oth[:]))
                if t == 9:
                    after(dve, s_x2T, C * b)
                    after(dve, s_spill, 16 * b)
                    for j in range(T):
                        dve.wait_ge(s_pool, 2 * b + j // 2 + 1)
                        dve.scalar_tensor_tensor(out=x2[:, j, :], in0=psP[1 - j // 2][:, (j % 2) * D:(j % 2 + 1) * D],
                                                 scalar=rec[:, j:j + 1], in1=x1[:, j, :], op0=ALU.mult, op1=ALU.add)\
                           .then_inc(s_x2, 1)
                        if j % 2:
                            dve.wait_ge(s_x2, b * T + j + 1)
                            dve.sem_inc(s_p_read[1 - j // 2], 1)
                if t in (11, 12):
                    o = t - 11
                    dve.wait_ge(s_rest, b * C + o + 1)
                    dve.tensor_copy(parts[:, 1, o::C], qk[:, o::C]).then_inc(s_mid, 1)
                if t == 13:
                    after(dve, s_vcopy, b * G)
                    for k in range(2):
                        dve.wait_ge(s_v, 2 * C * b + 2 * k + 2)
                        link(dve.tensor_tensor(v_next[:, 2 * k:2 * k + 2, :], psP[1 - k][:].rearrange("p (t d) -> p t d", t=2),
                                               bc(bv_sb[:], 2), ALU.add))
                        dve.sem_inc(s_p_read[1 - k], 1)
                    dve.sem_inc(s_vc, 1)

            def last_layer(b, t):
                if t in (10, 10.5):
                    k = int(t > 10)
                    dve.wait_ge(s_x3in, b + 1)
                    dve.wait_ge(s_x3p, 2 * b + k + 1)
                    r = x3[:, 2 * k:2 * k + 2, :].rearrange("p t d -> p (t d)")
                    dve.tensor_tensor(r, psF[:], r, ALU.add).then_inc(s_x3, 1)
                    dve.wait_ge(s_x3, 2 * b + k + 1)
                    dve.sem_inc(s_f_read, 1)
                if t in (13, 13.5):
                    k = int(t > 13)
                    dve.wait_ge(s_x3b, b + 1)
                    dve.wait_ge(s_y3, 2 * b + k + 1)
                    y = y3[:, 2 * k:2 * k + 2, :].rearrange("p t d -> p (t d)")
                    link(dve.tensor_tensor(y, psF[:], y, ALU.add))
                    dve.sem_inc(s_f_read, 1)
                    if k:
                        moments(y3, stats3, mv3, rstd3, s_var3)
                if t == 14.5:
                    dve.wait_ge(s_rstd3, b + 1)
                    for t_ in range(T):
                        dve.tensor_scalar(y3[:, t_, :], y3[:, t_, :], mv3[:, t_, 0:1], rstd3[:, t_:t_ + 1],
                                          ALU.subtract, ALU.mult).then_inc(s_y3c, 1)

            def slots(b, is_p, is_a, is_f, span, new, old):
                for t in span:
                    if is_a and t == 0:
                        if new:
                            mask_for(b)
                        else:
                            skip(3)
                    for half in range(2):
                        if is_a:
                            maxima(b, t, range(2 * half, 2 * half + 2), new)
                        if half == 0:
                            if is_p:
                                first_layers(b + 1, t - 1)
                            if is_f:
                                last_layer(b - 1, t - 1)
                        elif is_f:
                            last_layer(b - 1, t - 0.5)
                        if t >= LAG_W and is_a:
                            weight(b, t - LAG_W, half, new)
                        if t < LAG_W and is_f:
                            weight(b - 1, t - LAG_W + H, half, old)
                    if t == LAG_W - 1 and is_a:
                        if new:
                            weights_for(b)
                        else:
                            skip(3)
                    if t in (0, 4, 8) and is_f:
                        normalize(b - 1, t // 4 + 1)
                    if t == 12 and is_a:
                        normalize(b, 0)
                alone(dve, s_passed)

            def iteration(b, is_p, is_a, is_f):
                in_slots(dve, live_i, b, is_a, is_f, [seq],
                         lambda span, new, old: slots(b, is_p, is_a, is_f, span, new, old))

            def hots(t):
                for i in range(NI):
                    n = t * NI + i
                    m = n - 8
                    if m >= 0:
                        if m % NI == NI - 1:
                            dve.wait_ge(s_cnt, m // NI + 1)
                        else:
                            dve.wait_ge(s_hot_used, (m // NI) * (NI - 1) + m % NI + 1)
                    dve.tensor_scalar(hot[:, n % 8, :], iota_h, idx_f[:, t, i:i + 1], None, ALU.is_equal).then_inc(s_hot, 1)
                dve.wait_ge(s_cnt, t + 1)
                link(dve.tensor_scalar(unlisted[:, t, :], psS[t % 2][:], 0.5, NEG, ALU.is_lt, ALU.mult))
                dve.tensor_copy(count_sb[:, t, :], psS[t % 2][:]).then_inc(s_cnt_read, 1)

            link(dve.memset(V[:], 0.0))
            dve.memset(V[:, :, :, DH:DH + 1], 1.0).then_inc(s_vz, 1)
            dve.wait_ge(s_vz, 1)
            link(dve.memset(e_diag[:], 0.0))
            dve.sem_inc(s_vz, 1)
            dve.wait_ge(s_const, 16 * CONSTS)
            link(dve.tensor_copy(idx_f[:], idx_i[:]))
            link(dve.tensor_copy(idx_m[:], idx_ok[:]))
            link(dve.tensor_scalar(iota_f[:, 0:T * NI], idx_f[:].rearrange("p t i -> p (t i)"), 0.0, float(S), ALU.is_lt, ALU.mult))
            link(dve.tensor_tensor(idx_f[:].rearrange("p t i -> p (t i)"), idx_f[:].rearrange("p t i -> p (t i)"),
                                   iota_f[:, 0:T * NI], ALU.add))
            link(dve.tensor_scalar(idx_f[:], idx_f[:], 0.0, float(S - 1), ALU.max, ALU.min))
            link(dve.scalar_tensor_tensor(out=idx_f[:], in0=idx_f[:], scalar=1.0, in1=idx_m[:], op0=ALU.add, op1=ALU.mult))
            link(dve.tensor_scalar(idx_f[:], idx_f[:], -1.0, None, ALU.add))
            dve.sem_inc(s_iota, 1)
            dve.tensor_reduce(far[:], idx_f[:].rearrange("p t i -> p (t i)"), AX_X, ALU.max).then_inc(s_far, 1)
            dve.wait_ge(s_iota, 2)
            link(dve.tensor_copy(iota_h, iota_f))
            dve.wait_ge(s_ident, 2)
            link(dve.tensor_copy(identb[:], ident[:]))
            dve.sem_inc(s_ident, 1)
            dve.wait_ge(s_e1, 1)
            link(dve.tensor_scalar(tmp8[:, 0, :], tmp8[:, 0, :], 10.0, None, ALU.mult))
            link(dve.tensor_scalar(table[:, :, 0], tmp8[:, 0, :], 1.0, None, ALU.is_ge))
            dve.tensor_scalar(tmp8[:, 1, :], tmp8[:, 0, :], 1.0, None, ALU.min).then_inc(s_e2, 1)
            dve.wait_ge(s_e1, 2)
            dve.wait_ge(s_e2, 1)
            link(dve.tensor_scalar(table[:, :, 2], table[:, :, 0], -1.0, 1.0, ALU.mult, ALU.add))
            link(dve.scalar_tensor_tensor(out=table[:, :, 1], in0=tmp8[:, 1, :], scalar=-1.0, in1=table[:, :, 2],
                                          op0=ALU.mult, op1=ALU.mult))
            link(dve.scalar_tensor_tensor(out=table[:, :, 3], in0=tmp8[:, 2, :], scalar=-1.0, in1=table[:, :, 2],
                                          op0=ALU.add, op1=ALU.mult))
            link(dve.tensor_copy(tmp8[:, 0, :], ty_i[:]))
            link(dve.tensor_scalar(table[:, :, 4], tmp8[:, 0, :], 0.0, None, ALU.is_equal))
            link(dve.tensor_scalar(table[:, :, 5], tmp8[:, 0, :], 1.0, None, ALU.is_equal))
            link(dve.tensor_tensor(tmp8[:, 1, :], table[:, :, 4], table[:, :, 5], ALU.add))
            link(dve.tensor_scalar(table[:, :, 6], tmp8[:, 1, :], -1.0, 1.0, ALU.mult, ALU.add))
            dve.sem_inc(s_types, 1)
            link(dve.tensor_scalar(bqs[:], bq_sb[:], DH ** -0.5, None, ALU.mult))
            link(dve.tensor_scalar(vbc[:], ones[0:A1, :], v_sb[:], None, ALU.mult))
            dve.sem_inc(s_set, 1)
            link(dve.memset(Ks[KR:KR + 3, :, :], 1.0))
            for t in range(16):
                first_layers(0, t)
                if t in (1, 4, 5, 6):
                    hots((1, 4, 5, 6).index(t))
                if t == 7:
                    link(dve.tensor_copy(unprior[:], blk8))
                    link(dve.tensor_scalar(unprior[:], unprior[:], -1.0, 1.0, ALU.mult, ALU.add))
                    link(dve.tensor_copy(unprior_t[:], blkt8))
                    link(dve.tensor_scalar(unprior_t[:], unprior_t[:], -1.0, 1.0, ALU.mult, ALU.add))
            dve.wait_ge(s_far_row, 1)
            link(dve.tensor_reduce(far[0:1, :], psO[0:1, 0:P], AX_X, ALU.max))
            link(dve.tensor_scalar(far[0:1, :], far[0:1, :], float(SN), None, ALU.is_ge))
            link(dve.tensor_scalar(live_i[:], table[0:1, :, 2], far[0:1, :], None, ALU.max))
            dve.sem_inc(s_live, 1)
            dve.wait_ge(s_ct_read, T)
            iteration(0, True, True, False)
            start = seq.n
            with dve.Fori(FIRST, LAST) as b:
                seq.enter(b, FIRST, SEQ)
                iteration(b, True, True, True)
            seq.leave(LAST - FIRST, start)
            iteration(LAST, False, True, True)
            iteration(B, False, False, True)

        @block.gpsimd
        def _(pool):
            seq = Count()
            SEQ = 42

            def link(ins):
                ins.then_inc(s_pool_seq, 1)
                seq.n += 1
                pool.wait_ge(s_pool_seq, seq.value)

            def newton(var, r, t, s_r, b):
                for k in range(3):
                    link(pool.tensor_tensor(t[:], r[:], r[:], ALU.mult))
                    link(pool.tensor_tensor(t[:], t[:], var, ALU.mult))
                    alone(pool, s_passed_pool)
                    link(pool.tensor_scalar(t[:], t[:], -0.5, 1.5, ALU.mult, ALU.add))
                    ins = pool.tensor_tensor(r[:], r[:], t[:], ALU.mult)
                    if k < 2:
                        link(ins)
                ins.then_inc(s_r, 1)
                pool.wait_ge(s_r, b + 1)

            def types_for(b):
                after(pool, s_exp1, b * (T + 2))
                after(pool, s_x2, b * T)
                src = table[:, b, 4:7] if isinstance(b, int) else table[:, bass.ds(b, 1), 4:7].squeeze(1)
                alone(pool, s_passed_pool)
                link(pool.tensor_copy(cur_m[:, 4:7], src))
                alone(pool, s_passed_pool)
                link(pool.tensor_scalar(typ[:], type_tab[:, 0, :], cur_m[:, 4:5], None, ALU.mult))
                for k in (1, 2):
                    alone(pool, s_passed_pool)
                    link(pool.tensor_scalar(typ2[:], type_tab[:, k, :], cur_m[:, 4 + k:5 + k], None, ALU.mult))
                    ins = pool.tensor_tensor(typ[:], typ[:], typ2[:], ALU.add)
                    if k == 1:
                        link(ins)
                ins.then_inc(s_typ, 1)
                pool.wait_ge(s_typ, b + 1)

            def first_layers(b, t):
                if t == 0:
                    pool.wait_ge(s_loadp, (b + 1) * LOADP * 16)
                    pool.tensor_tensor(y_sb[:], x_sb[:], bc(bu_sb[:], T), ALU.add).then_inc(s_xbu, 1)
                    pool.wait_ge(s_xbu, 2 * b + 1)
                    pool.tensor_tensor(x_sb[:], x_sb[:], bc(be0_sb[:], T), ALU.add).then_inc(s_xbu, 1)
                    pool.wait_ge(s_xbu, 2 * b + 2)
                    types_for(b)
                if t == 2:
                    pool.wait_ge(s_var, b + 1)
                    newton(mv[:, :, 1], rstd, newt, s_rstd, b)
                    pool.wait_ge(s_yc, (b + 1) * T)
                    link(pool.tensor_tensor(y_sb[:], y_sb[:], bc(g0_sb[:], T), ALU.mult))
                    after(pool, s_pool, 2 * b)
                    after(pool, s_x2, T * b)
                    pool.tensor_tensor(x1[:], y_sb[:], x_sb[:], ALU.add).then_inc(s_x1, 1)
                    pool.wait_ge(s_x1, b + 1)
                if t in (11, 12):
                    o = t - 11
                    i = b * C + o + 1
                    pool.wait_ge(s_hi, i)
                    pool.tensor_tensor(qk[:, o::C], qk[:, o::C], parts[:, 0, o::C], ALU.subtract).then_inc(s_rest, 1)
                    pool.wait_ge(s_mid, i)
                    pool.tensor_tensor(parts[:, 2, o::C], qk[:, o::C], parts[:, 1, o::C], ALU.subtract).then_inc(s_lo, 1)
                    pool.wait_ge(s_lo, i)

            def split_max(b, g):
                pool.wait_ge(s_negm, b * G + g + 1)
                after(pool, s_mrow, (b * G + g) * 48)
                a = nm[0:4 * T, :]
                alone(pool, s_passed_pool)
                link(pool.tensor_copy(nm_parts[:, 0, :], a))
                link(pool.tensor_tensor(a, a, nm_parts[:, 0, :], ALU.subtract))
                alone(pool, s_passed_pool)
                link(pool.tensor_copy(nm_parts[:, 1, :], a))
                pool.tensor_tensor(nm_parts[:, 2, :], a, nm_parts[:, 1, :], ALU.subtract).then_inc(s_nsplit, 1)
                pool.wait_ge(s_nsplit, b * G + g + 1)

            def v_copy(b, g):
                if g == 0:
                    pool.wait_ge(s_vc, b + 1)
                after(pool, s_pv, b * H + 4 * g + 4 - H)
                src = v_next[:, :, g * 4 * DH:(g + 1) * 4 * DH].rearrange("p t (h r) -> p t h r", h=4)
                alone(pool, s_passed_pool)
                pool.tensor_copy(V[:, :, 4 * g:4 * g + 4, 0:DH], src).then_inc(s_vcopy, 1)
                pool.wait_ge(s_vcopy, b * G + g + 1)

            def last_layer(b, t):
                if t == 9:
                    pool.wait_ge(s_loadf, (b + 1) * LOADF * 16)
                    pool.tensor_tensor(x3[:], x3[:], bc(bo_sb[:], T), ALU.add).then_inc(s_x3in, 1)
                if t == 11:
                    pool.wait_ge(s_x3, 2 * b + 2)
                    after(pool, s_out, 16 * b)
                    pool.tensor_tensor(y3[:], x3[:], bc(lb2_sb[:], T), ALU.add).then_inc(s_x3b, 1)
                    pool.wait_ge(s_x3b, b + 1)
                if t == 12:
                    pool.wait_ge(s_fT, 2 * C * (b + 1))
                    link(pool.tensor_tensor(x3[:], x3[:], bc(lb_sb[:], T), ALU.add))
                if t == 14:
                    pool.wait_ge(s_var3, b + 1)
                    newton(mv3[:, :, 1], rstd3, newt3, s_rstd3, b)
                    pool.wait_ge(s_y3c, (b + 1) * T)
                    link(pool.tensor_tensor(y3[:], y3[:], bc(lg_sb[:], T), ALU.mult))
                    pool.tensor_tensor(y3[:], y3[:], x3[:], ALU.add).then_inc(s_out_sb, 1)
                    pool.wait_ge(s_out_sb, b + 1)

            def iteration(b, is_p, is_a, is_f):
                for t in range(16):
                    if t == 0 and is_f:
                        split_max(b - 1, 3)
                    if t in (4, 8, 12) and is_a:
                        split_max(b, t // 4 - 1)
                    if t == 1 and is_a:
                        v_copy(b, 0)
                        v_copy(b, 1)
                    if t in (4, 8) and is_a:
                        v_copy(b, 1 + t // 4)
                    if is_f:
                        last_layer(b - 1, t)
                    if is_p:
                        first_layers(b + 1, t)

            link(pool.memset(ident[:], 0.0))
            pool.affine_select(out=ident[:], in_=ident[:], compare_op=ALU.not_equal, fill=1.0, base=0,
                               pattern=[[-1, P]], channel_multiplier=1).then_inc(s_ident, 1)
            pool.memset(ones[:], 1.0).then_inc(s_ident, 1)
            link(pool.memset(type_tab[:], 0.0))
            for k, (op, sign, off) in enumerate(((ALU.is_ge, 1, 0), (ALU.is_ge, -1, 0), (ALU.not_equal, 1, 0))):
                link(pool.affine_select(out=type_tab[:, k, 0:P], in_=type_tab[:, k, 0:P], compare_op=op, fill=NEG,
                                        base=0, pattern=[[-sign, P]], channel_multiplier=sign))
                m = type_tab[:, k, P:P + T * T].rearrange("p (a b) -> p a b", a=T)
                link(pool.affine_select(out=m, in_=m, compare_op=op, fill=NEG, base=0 if k == 2 else -1,
                                        pattern=[[sign, T], [-sign, T]], channel_multiplier=0))
            for k, (base, step) in enumerate(((1, 1), (S, -1))):
                link(pool.iota(type_tab[:, k, P + T * T:TW], [[step * P, T]], base=base, channel_multiplier=step,
                               allow_small_or_imprecise_dtypes=True))
            link(pool.memset(type_tab[:, 2, P + T * T:TW], float(S - 1)))
            pool.wait_ge(s_iota, 1)
            pool.iota(iota_f, [[1, S]], base=0, channel_multiplier=0,
                      allow_small_or_imprecise_dtypes=True).then_inc(s_iota, 1)
            pool.wait_ge(s_types, 1)
            for t in range(16):
                first_layers(0, t)
            iteration(0, True, True, False)
            start = seq.n
            with pool.Fori(FIRST, LAST) as b:
                seq.enter(b, FIRST, SEQ)
                iteration(b, True, True, True)
            seq.leave(LAST - FIRST, start)
            iteration(LAST, False, True, True)
            iteration(B, False, False, True)


_INS = ['x', 'xt', 'profile', 'prompt', 'indices', 'u_prev', 'language', 'blocked', 'blocked_t', 'index_ok',
        'wd', 'bd', 'wu', 'bu', 'ln0_g', 'ln0_b', 'w1', 'b1', 'v', 'wq_t', 'bq', 'wk_t', 'bk', 'wv_t', 'bv', 'wo_t', 'bo',
        'lw1', 'lb1', 'lw2', 'lb2', 'lg', 'lb']


def kernel(x, itok_B_0_6, itok_B_0_2, itok_Sx32_0_1023, condB_uprev, itok_B_0_8, mask_SxS_bk0, mask_Sx32_bk1,
           L0_cond_down_w, L0_cond_down_b, L0_cond_up_w, L0_cond_up_b, L0_cond_ln_g, L0_cond_ln_b,
           L1_cond_W1, L1_cond_b1, L1_cond_v, L2_cond_Wq, L2_cond_bq, L2_cond_Wk, L2_cond_bk, L2_cond_Wv, L2_cond_bv,
           L2_cond_Wo, L2_cond_bo, L3_cond_W1, L3_cond_b1, L3_cond_W2, L3_cond_b2, L3_cond_gamma, L3_cond_beta):
    import numpy as np
    import concourse.bacc as bacc
    from concourse import mybir as mb
    from concourse.bass_utils import run_bass_kernel_spmd as run

    x = np.asarray(x)
    mask = np.asarray(mask_SxS_bk0)
    data = dict(zip(_INS, [
        x, x.transpose(0, 2, 1), itok_B_0_6, itok_B_0_2, itok_Sx32_0_1023, condB_uprev, itok_B_0_8,
        mask, mask.T, mask_Sx32_bk1,
        L0_cond_down_w, L0_cond_down_b, L0_cond_up_w, L0_cond_up_b, L0_cond_ln_g, L0_cond_ln_b,
        L1_cond_W1, L1_cond_b1, L1_cond_v, np.asarray(L2_cond_Wq).T, np.asarray(L2_cond_bq).reshape(-1, P).T, np.asarray(L2_cond_Wk).T,
        np.asarray(L2_cond_bk).reshape(-1, P).T,
        np.asarray(L2_cond_Wv).T, L2_cond_bv, np.asarray(L2_cond_Wo).T, L2_cond_bo,
        L3_cond_W1, L3_cond_b1, L3_cond_W2, L3_cond_b2, L3_cond_gamma, L3_cond_beta]))
    nc = bacc.Bacc("TRN2", target_bir_lowering=False, num_devices=1)
    arrays, args = {}, []
    for name in _INS:
        a = np.ascontiguousarray(data[name])
        arrays[f"in_{name}"] = a
        args.append(nc.dram_tensor(f"in_{name}", a.shape, mb.dt.from_np(a.dtype), kind="ExternalInput").ap())
    o = nc.dram_tensor("out_0", x.shape, mb.dt.from_np(x.dtype), kind="ExternalOutput").ap()
    cond_resid(nc, *args, o)
    r = run(nc, [arrays], core_ids=[0])
    return r.results[0]["out_0"]
```

```python
from contextlib import ExitStack

import concourse.bass as bass
from concourse import mybir

ALU = mybir.AluOpType
ACT = mybir.ActivationFunctionType
AX_X = mybir.AxisListType.X
F32 = mybir.dt.float32
BF16 = mybir.dt.bfloat16
F16 = mybir.dt.float16
I32 = mybir.dt.int32
U8 = mybir.dt.uint8

P = 128
NEG = -1.0e30
EPS = 1.0e-5


def alone(eng, sem):
    eng.sem_inc(sem, 1)


TAIL = 9


class Count:

    def __init__(self):
        self.base, self.n, self.per = 0, 0, 0

    def enter(self, b, first, per):
        self.base, self.n, self.per = self.n + (b - first) * per, 0, per

    def leave(self, trips, start):
        assert self.n == self.per, (self.n, self.per)
        self.base, self.n = 0, start + trips * self.per

    @property
    def value(self):
        return self.base + self.n


def either(eng, live, counts, body):
    start = [c.n for c in counts]
    with eng.If(live > 0):
        body(True)
    end = [c.n for c in counts]
    for c, n in zip(counts, start):
        c.n = n
    with eng.Else():
        body(False)
    assert [c.n for c in counts] == end


def in_slots(eng, live, b, is_a, is_f, counts, slots):
    def reg(i):
        return eng.value_load(live[0:1, i:i + 1] if isinstance(i, int) else live[0:1, bass.ds(i, 1)],
                              min_val=0, max_val=1)
    if is_a and is_f:
        new, old = reg(b), reg(b - 1)
        either(eng, old, counts, lambda o: either(eng, new, counts, lambda n: slots(range(0, TAIL), n, o)))
        either(eng, new, counts, lambda n: slots(range(TAIL, 16), n, n))
    elif is_a:
        either(eng, reg(b), counts, lambda n: slots(range(16), n, n))
    else:
        either(eng, reg(b - 1), counts, lambda o: slots(range(0, TAIL), o, o))
        slots(range(TAIL, 16), False, False)


def after(eng, sem, count):
    if not isinstance(count, int) or count > 0:
        eng.wait_ge(sem, count)


def cond_resid(nc, x, xt, profile, prompt, indices, u_prev, language, blocked, blocked_t, index_ok,
               wd, bd, wu, bu, ln0_g, ln0_b, w1, b1, v, wq_t, bq, wk_t, bk, wv_t, bv, wo_t, bo,
               lw1, lb1, lw2, lb2, lg, lb, out):
    B, S, D = x.shape
    T = S // P
    C = D // P
    TN, SN = T // 2, S // 2
    H = 16
    DH = D // H
    NI = indices.shape[1]
    HP = 32
    G = H // 4
    PAIRS = [(0, 0), (0, 1), (1, 0), (0, 2), (2, 0), (1, 1)]
    NS = len(PAIRS)
    KR = NS * DH
    LAG_T, LAG_W, LAG_V = 7, 8, 9
    RING = 4
    A1 = w1.shape[1]
    A3 = lw1.shape[2]
    CHUNK = 16

    with ExitStack() as ctx:
        def sb(name, shape, dt=F32):
            return ctx.enter_context(nc.sbuf_tensor(name, shape, dt))

        def ps(name):
            return ctx.enter_context(nc.psum_tensor(name, [P, 512], F32))

        def sem(name):
            return ctx.enter_context(nc.semaphore(name))

        psS = [ps("psS0"), ps("psS1")]
        psT = [ps("psT0"), ps("psT1")]
        psO = ps("psO")
        psP = [ps("psP0"), ps("psP1")]
        psF = ps("psF")

        ident = sb("ident", [P, P])
        identb = sb("identb", [P, P], BF16)
        ones = sb("ones", [P, P])
        TW = P + T * T + T
        type_tab = sb("type_tab", [P, 3, TW])
        wq_sb, wk_sb, wv_sb, wo_sb = (sb(n, [P, C, D]) for n in ("wq_sb", "wk_sb", "wv_sb", "wo_sb"))
        bq_sb, bk_sb = sb("bq_sb", [P, C]), sb("bk_sb", [P, C])
        bqs = sb("bqs", [P, C])
        bv_sb, bo_sb = sb("bv_sb", [P, D]), sb("bo_sb", [P, D])
        w1_sb, b1_sb, v_sb, vbc = sb("w1_sb", [P, C, A1]), sb("b1_sb", [A1, 1]), sb("v_sb", [A1, 1]), sb("vbc", [A1, P])
        ids = sb("ids", [1, 2, B], I32)
        u_sb, ty_i = sb("u_sb", [P, B]), sb("ty_i", [P, B], I32)
        live_i = sb("live_i", [1, B], I32)
        far = sb("far", [P, 1])
        table = sb("table", [P, B, 8])
        tmp8 = sb("tmp8", [P, 3, B])
        idx_i, idx_ok = sb("idx_i", [P, T, NI], I32), sb("idx_ok", [P, T, NI], U8)
        idx_f, idx_m = sb("idx_f", [P, T, NI]), sb("idx_m", [P, T, NI])
        prob = sb("prob", [P, RING, T, S])
        hot = prob[:, 0].rearrange("p k s -> p (k s)").bitcast(BF16).rearrange("p (r s) -> p r s", s=S)
        blk8 = prob[:, 1, 0].bitcast(U8).rearrange("p (t s) -> p t s", t=T)
        blkt8 = prob[:, 1, 1].bitcast(U8).rearrange("p (t s) -> p t s", t=T)
        count_sb = prob[:, 2, 0:2].rearrange("p k s -> p (k s)").bitcast(BF16).rearrange("p (t s) -> p t s", t=T)
        iota_f = prob[:, 3, 0]
        iota_h = prob[:, 3, 1].bitcast(F16)[:, 0:S]
        unprior = sb("unprior", [P, T, S], BF16)
        unprior_t = sb("unprior_t", [P, T, S], BF16)
        unlisted = sb("unlisted", [P, T, S], BF16)
        count_t = sb("count_t", [P, T, S], BF16)

        x_sb = sb("x_sb", [P, T, D])
        xT = sb("xT", [P, C, S])
        wd_sb, bd_sb, wu_sb = sb("wd_sb", [P, C, P]), sb("bd_sb", [P, 1]), sb("wu_sb", [P, D])
        bu_sb, g0_sb, be0_sb = sb("bu_sb", [P, D]), sb("g0_sb", [P, D]), sb("be0_sb", [P, D])
        z_sb = sb("z_sb", [P, S])
        y_sb = sb("y_sb", [P, T, D])
        stats, mv, rstd = sb("stats", [P, T, 6]), sb("mv", [P, T, 2]), sb("rstd", [P, T])
        x1 = sb("x1", [P, T, D])
        h1 = sb("h1", [A1, S])
        typ = sb("typ", [P, TW])
        typ2 = sb("typ2", [P, TW])
        cur_m = sb("cur_m", [P, 8])
        col = sb("col", [P, T])
        bmax = sb("bmax", [P, T])
        masked = sb("masked", [P, T, P])
        m_in, m_neg = sb("m_in", [P, T]), sb("m_neg", [P, T])
        oth = sb("oth", [P, T, T])
        m_oth = sb("m_oth", [P, T])
        w_oth = sb("w_oth", [P, T, T])
        e_arg = sb("e_arg", [P, T])
        e_diag = sb("e_diag", [P, T, T])
        pin = sb("pin", [P, T, P])
        sum_in = sb("sum_in", [P, T])
        pinT = sb("pinT", [P, T, P])
        w_othT = sb("w_othT", [T, T, P])
        u_blk = sb("u_blk", [T, D])
        e_sum = sb("e_sum", [P, T])
        rec = sb("rec", [P, T])
        x2 = sb("x2", [P, T, D])
        qk = sb("qk", [P, 2 * C, S])
        parts = sb("parts", [P, 3, 2 * C, S], BF16)

        Qs = sb("Qs", [KR + 3, H, S], BF16)
        Ks = sb("Ks", [KR + 3, H, S], BF16)
        v_next = sb("v_next", [P, T, D])
        V = sb("V", [P, T, H, HP])
        cur_a, cur_w = sb("cur_a", [P, 4]), sb("cur_w", [P, 4])
        mask_a = sb("mask_a", [P, T, S], BF16)
        wgt = sb("wgt", [P, T, S])
        mx = sb("mx", [P, 2, 4, T])
        nm = sb("nm", [P, P])
        nm_parts = sb("nm_parts", [16, 3, P], BF16)
        oT_sb = sb("oT_sb", [P, S])
        orec = sb("orec", [P, T, 4])
        o_sb = sb("o_sb", [P, T, D])

        fT = sb("fT", [P, C, S])
        x3 = sb("x3", [P, T, D])
        y3 = sb("y3", [P, T, D])
        lw1_sb, lb1_sb, lw2_sb = sb("lw1_sb", [P, C, A3]), sb("lb1_sb", [A3, 1]), sb("lw2_sb", [A3, D])
        lb2_sb, lg_sb, lb_sb = sb("lb2_sb", [P, D]), sb("lg_sb", [P, D]), sb("lb_sb", [P, D])
        newt, newt3 = sb("newt", [P, T]), sb("newt3", [P, T])
        h3 = sb("h3", [A3, S])
        stats3, mv3, rstd3 = sb("stats3", [P, T, 6]), sb("mv3", [P, T, 2]), sb("rstd3", [P, T])

        x2_dram = nc.dram_tensor("x2_spill", (B, S, D), F32, kind="Internal").ap()
        st_dram = nc.dram_tensor("stacks", (2, H, NS, DH, S), BF16, kind="Internal").ap()

        s_early, s_pooling, s_const, s_ids = sem("s_early"), sem("s_pooling"), sem("s_const"), sem("s_ids")
        s_far, s_far_row, s_live = sem("s_far"), sem("s_far_row"), sem("s_live")
        s_passed, s_passed_pool = sem("s_passed"), sem("s_passed_pool")
        s_ident, s_identb, s_types, s_iota = sem("s_ident"), sem("s_identb"), sem("s_types"), sem("s_iota")
        s_vbc, s_bqs = sem("s_vbc"), sem("s_bqs")
        s_e1, s_e2 = sem("s_e1"), sem("s_e2")
        s_hot, s_hot_used, s_cnt, s_cnt_read, s_ct, s_ct_read = (sem(n) for n in (
            "s_hot", "s_hot_used", "s_cnt", "s_cnt_read", "s_ct", "s_ct_read"))
        s_loadp, s_loadxt, s_loadf = sem("s_loadp"), sem("s_loadxt"), sem("s_loadf")
        s_p_read = [sem("s_p0_read"), sem("s_p1_read")]
        s_f_read = sem("s_f_read")
        s_z, s_zc, s_y, s_x1, s_x1T, s_x1Tc, s_h, s_hc = (sem(n) for n in (
            "s_z", "s_zc", "s_y", "s_x1", "s_x1T", "s_x1Tc", "s_h", "s_hc"))
        s_xbu, s_typ, s_pinT = sem("s_xbu"), sem("s_typ"), sem("s_pinT")
        s_row, s_colf, s_colc, s_arg, s_exp1 = (sem(n) for n in ("s_row", "s_colf", "s_colc", "s_arg", "s_exp1"))
        s_pT, s_pTc, s_u, s_uc, s_pool, s_x2 = (sem(n) for n in ("s_pT", "s_pTc", "s_u", "s_uc", "s_pool", "s_x2"))
        s_x2T, s_x2Tc, s_qk, s_qkc, s_v, s_vc = (sem(n) for n in ("s_x2T", "s_x2Tc", "s_qk", "s_qkc", "s_v", "s_vc"))
        s_hi, s_rest, s_mid, s_lo = (sem(n) for n in ("s_hi", "s_rest", "s_mid", "s_lo"))
        s_stored = [sem(f"s_stored{c}") for c in range(C)]
        s_stack = [sem(f"s_stack{g}") for g in range(G)]
        s_spill = sem("s_spill")
        s_scores, s_max, s_mT, s_negm, s_nsplit, s_mrow = (sem(n) for n in (
            "s_scores", "s_max", "s_mT", "s_negm", "s_nsplit", "s_mrow"))
        s_st, s_exp, s_wmul, s_vcopy, s_pv, s_oc, s_oT, s_o = (sem(n) for n in (
            "s_st", "s_exp", "s_wmul", "s_vcopy", "s_pv", "s_oc", "s_oT", "s_o"))
        s_fT, s_fTc, s_x3p, s_x3, s_x3in, s_x3b, s_h3, s_h3c, s_y3, s_out_sb, s_out = (sem(n) for n in (
            "s_fT", "s_fTc", "s_x3p", "s_x3", "s_x3in", "s_x3b", "s_h3", "s_h3c", "s_y3", "s_out_sb", "s_out"))
        s_x3lb = sem("s_x3lb")
        s_dve, s_pool_seq, s_vz = sem("s_dve"), sem("s_pool_seq"), sem("s_vz")

        def bc(ap, n):
            return ap.unsqueeze(1).to_broadcast([P, n, ap.shape[1]])

        def scores_at(t, wide):
            return psS[t % 2][:] if wide else psS[t // 2][:, t % 2 * SN:(t % 2 + 1) * SN]

        EARLY = [
            (idx_i[:], indices.rearrange("(t p) i -> p t i", p=P)), (idx_ok[:], index_ok.rearrange("(t p) i -> p t i", p=P)),
            (u_sb[:], u_prev.unsqueeze(0).to_broadcast([P, B])), (ty_i[:], prompt.unsqueeze(0).to_broadcast([P, B]))]
        POOLING = [
            (w1_sb[:], w1.rearrange("(c p) a -> p c a", p=P)), (b1_sb[:], b1.unsqueeze(1)), (v_sb[:], v.unsqueeze(1))]
        CONST = [
            (wq_sb[:], wq_t.rearrange("(c p) n -> p c n", p=P)), (wk_sb[:], wk_t.rearrange("(c p) n -> p c n", p=P)),
            (bq_sb[:], bq), (bk_sb[:], bk), (wv_sb[:], wv_t.rearrange("(c p) n -> p c n", p=P)),
            (bv_sb[:], bv.unsqueeze(0).to_broadcast([P, D])),
            (blk8, blocked.rearrange("(t p) k -> p t k", p=P)), (blkt8, blocked_t.rearrange("(t p) k -> p t k", p=P)),
            (wo_sb[:], wo_t.rearrange("(c p) n -> p c n", p=P)), (bo_sb[:], bo.unsqueeze(0).to_broadcast([P, D]))]

        block = ctx.enter_context(nc.Block())

        LOADP, LOADF = 7, 7
        FIRST, LAST = 1, B - 1

        @block.sync
        def _(sp):
            ra, rb, rm = sp.alloc_register("ra"), sp.alloc_register("rb"), sp.alloc_register("rm")

            def times(reg, b, per, c):
                if isinstance(b, int):
                    return b * per + c
                if c >= 0:
                    sp.reg_mul(rm, b, per)
                    sp.reg_add(reg, rm, c)
                else:
                    sp.reg_add(rm, b, -1)
                    sp.reg_mul(rm, rm, per)
                    sp.reg_add(reg, rm, per + c)
                return sp.snap(reg)

            def at(ap, i):
                return ap[i] if isinstance(i, int) else ap[bass.ds(i, 1)].squeeze(0)

            sp.dma_start(ids[0:1, 0, :], profile.unsqueeze(0)).then_inc(s_ids, 16)
            sp.dma_start(ids[0:1, 1, :], language.unsqueeze(0)).then_inc(s_ids, 16)
            sp.wait_ge(s_ids, 32)

            def load_xt(b):
                src = at(xt, b).rearrange("(c p) s -> p c s", p=P)
                w = times(ra, b, 2 * C, 0)
                after(sp, s_v, w)
                sp.dma_start(xT[:], src).then_inc(s_loadxt, 16)

            def load_p(b):
                i = sp.value_load(ids[0:1, 0, b:b + 1] if isinstance(b, int) else ids[0:1, 0, bass.ds(b, 1)],
                                  min_val=0, max_val=wd.shape[0] - 1)
                src = [at(x, b).rearrange("(t p) d -> p t d", p=P),
                       at(wd, i).rearrange("(c p) k -> p c k", p=P), at(bd, i).unsqueeze(1), at(wu, i),
                       at(bu, i).unsqueeze(0).to_broadcast([P, D]), at(ln0_g, i).unsqueeze(0).to_broadcast([P, D]),
                       at(ln0_b, i).unsqueeze(0).to_broadcast([P, D])]
                dst = [x_sb[:], wd_sb[:], bd_sb[:], wu_sb[:], bu_sb[:], g0_sb[:], be0_sb[:]]
                w = times(ra, b, 1, 0)
                after(sp, s_x1, w)
                for d_, s_ in zip(dst, src):
                    sp.dma_start(d_, s_).then_inc(s_loadp, 16)

            def load_f(b):
                i = sp.value_load(ids[0:1, 1, b:b + 1] if isinstance(b, int) else ids[0:1, 1, bass.ds(b, 1)],
                                  min_val=0, max_val=lw1.shape[0] - 1)
                src = [at(lw1, i).rearrange("(c p) k -> p c k", p=P), at(lb1, i).unsqueeze(1), at(lw2, i),
                       at(lb2, i).unsqueeze(0).to_broadcast([P, D]), at(lg, i).unsqueeze(0).to_broadcast([P, D]),
                       at(lb, i).unsqueeze(0).to_broadcast([P, D])]
                dst = [lw1_sb[:], lb1_sb[:], lw2_sb[:], lb2_sb[:], lg_sb[:], lb_sb[:]]
                w = times(ra, b, 1, 0)
                after(sp, s_out_sb, w)
                for d_, s_ in zip(dst, src):
                    sp.dma_start(d_, s_).then_inc(s_loadf, 16)

            def unspill(b):
                w = times(ra, b, 16, 16)
                sp.wait_ge(s_spill, w)
                sp.dma_start(x3[:], at(x2_dram, b).rearrange("(t p) d -> p t d", p=P)).then_inc(s_loadf, 16)

            def spill(b):
                w = times(ra, b, T, T)
                sp.wait_ge(s_x2, w)
                sp.dma_start(at(x2_dram, b).rearrange("(t p) d -> p t d", p=P), x2[:]).then_inc(s_spill, 16)

            def store_stacks(b, c, part):
                made, per, n = ((s_hi, C, c + 1), (s_mid, C, c + 1), (s_lo, C, c + 1))[part]
                w = times(ra, b, per, n)
                sp.wait_ge(made, w)
                if part == 0 and c == 0:
                    w2 = times(rb, b, 32, 0)
                    for g in range(G):
                        after(sp, s_stack[g], w2)
                for side in range(2):
                    for j, pair in enumerate(PAIRS):
                        if pair[side] == part:
                            sp.dma_start(st_dram[side, c * H // C:(c + 1) * H // C, j],
                                         parts[:, part, side * C + c, :]).then_inc(s_stored[c], 16)

            def load_stack(b, g):
                w = times(ra, b, 2 * NS * 16, 2 * NS * 16)
                w2 = times(rb, b, H * T, (4 * g + 4 - H) * T)
                sp.wait_ge(s_stored[g * C // G], w)
                after(sp, s_st, w2)
                for side, dst in enumerate((Qs, Ks)):
                    sp.dma_start(dst[0:KR, 4 * g:4 * g + 4, :],
                                 st_dram[side, 4 * g:4 * g + 4].rearrange("h j d s -> (j d) h s")).then_inc(s_stack[g], 16)

            def store_out(b):
                dst = at(out, b).rearrange("(t p) d -> p t d", p=P)
                w = times(ra, b, 1, 1)
                sp.wait_ge(s_out_sb, w)
                sp.dma_start(dst, y3[:]).then_inc(s_out, 16)

            def iteration(b, is_p, is_a, is_f, more=True):
                for t in range(16):
                    if t == 0 and is_f:
                        if not isinstance(b, int) or b > 1:
                            store_out(b - 2)
                        load_f(b - 1)
                        unspill(b - 1)
                    if t == 2 and is_a and is_f:
                        store_stacks(b, 1, 1)
                        store_stacks(b, 1, 2)
                        load_stack(b, 2)
                    if t == 5 and is_p and more:
                        load_p(b + 2)
                    if t == 6 and is_a and is_f:
                        load_stack(b, 3)
                    if t == 9 and is_p:
                        spill(b + 1)
                    if t == 10 and is_p:
                        store_stacks(b + 1, 0, 0)
                        store_stacks(b + 1, 0, 1)
                        store_stacks(b + 1, 0, 2)
                    if t == 11 and is_p:
                        load_stack(b + 1, 0)
                    if t == 14 and is_p:
                        load_stack(b + 1, 1)
                        if more:
                            load_xt(b + 2)
                        store_stacks(b + 1, 1, 0)

            load_xt(0)
            load_p(0)
            for sem_, loads in (
                (s_early, EARLY), (s_pooling, POOLING), (s_const, CONST),
            ):
                for d_, s_ in loads:
                    sp.dma_start(d_, s_).then_inc(sem_, 16)
            load_p(1)
            spill(0)
            for c in range(C):
                for part in range(3):
                    store_stacks(0, c, part)
                for g in range(c * G // C, (c + 1) * G // C):
                    load_stack(0, g)
                if c == 0:
                    load_xt(1)
            iteration(0, True, True, False)
            iteration(1, True, True, True)
            with sp.Fori(2, LAST - 1) as b:
                iteration(b, True, True, True)
            iteration(LAST - 1, True, True, True, more=False)
            iteration(LAST, False, True, True)
            iteration(B, False, False, True)
            store_out(B - 1)
            sp.wait_ge(s_out, 16 * B)

        @block.tensor
        def _(pe):
            P_USES = (11, 10)
            F_USES = 17
            p_used = [Count(), Count()]
            f_used = Count()

            def bank(k, b):
                after(pe, s_p_read[k], b * P_USES[k] + p_used[k].n)
                p_used[k].n += 1
                return psP[k]

            def fbank():
                after(pe, s_f_read, f_used.value)
                f_used.n += 1
                return psF

            def counts(t, first):
                for i in range(first, first + CHUNK):
                    n = t * NI + i
                    pe.wait_ge(s_hot, n + 1)
                    if i == 0 and t >= 2:
                        pe.wait_ge(s_cnt_read, t - 1)
                    mm = pe.matmul(psS[t % 2][:], identb[:], hot[:, n % 8, :], start=(i == 0), stop=(i == NI - 1))
                    if i < NI - 1:
                        mm.then_inc(s_hot_used, 1)
                    else:
                        mm.then_inc(s_cnt, 1)

            def counts_t():
                for k in range(T):
                    pe.wait_ge(s_cnt_read, T)
                    if k >= 2:
                        pe.wait_ge(s_ct_read, k - 1)
                    dst = psT[k % 2][:].bitcast(BF16)
                    for t in range(T):
                        mm = pe.transpose(dst[:, t * P:(t + 1) * P], count_sb[:, t, k * P:(k + 1) * P], identb[:])
                    mm.then_inc(s_ct, 1)

            def turned(src, dst, c, sem_):
                for t in range(T):
                    mm = pe.transpose(dst[:, t * P:(t + 1) * P], src[:, t, c * P:(c + 1) * P], ident[:])
                mm.then_inc(sem_, 1)

            def first_layers(b, t):
                if t == 0:
                    p_used[0].n = p_used[1].n = 0
                    pe.wait_ge(s_loadp, (b + 1) * LOADP * 16)
                    pe.wait_ge(s_loadxt, (b + 1) * 16)
                    dst = bank(0, b)
                    for c in range(C):
                        mm = pe.matmul(dst[:], wd_sb[:, c, :], xT[:, c, :], start=(c == 0), stop=(c == C - 1))
                    mm.then_inc(s_z, 1)
                if t == 0.5:
                    pe.wait_ge(s_zc, b + 1)
                    for k in range(2):
                        dst = bank(1 - k, b)
                        for i in range(2):
                            mm = pe.matmul(dst[:, i * D:(i + 1) * D], z_sb[:, (2 * k + i) * P:(2 * k + i + 1) * P], wu_sb[:],
                                           start=True, stop=True)
                        mm.then_inc(s_y, 1)
                if t == 2.5:
                    pe.wait_ge(s_x1, b + 1)
                    for c in range(C):
                        turned(x1, bank(1 - c, b), c, s_x1T)
                if t == 3:
                    pe.wait_ge(s_x1Tc, (b + 1) * C)
                    dst = bank(1, b)
                    for c in range(C):
                        mm = pe.matmul(dst[0:A1, :], w1_sb[:, c, :], xT[:, c, :], start=(c == 0), stop=(c == C - 1))
                    mm.then_inc(s_h, 1)
                if t == 3.5:
                    pe.wait_ge(s_hc, b + 1)
                    dst = bank(0, b)
                    pe.matmul(dst[:], vbc[:], h1[:], start=True, stop=True).then_inc(s_row, 1)
                    dst = bank(1, b)
                    for i in range(T):
                        mm = pe.matmul(dst[:, i:i + 1], h1[:, i * P:(i + 1) * P], v_sb[:], start=True, stop=True)
                    mm.then_inc(s_colf, 1)
                if t == 5.5:
                    pe.wait_ge(s_exp1, (b + 1) * (T + 2))
                    dst = bank(0, b)
                    for i in range(T):
                        pe.matmul(dst[:, D:D + T], ones[:], e_diag[:, i, :], start=(i == 0), stop=(i == T - 1))
                    for i in range(T):
                        mm = pe.matmul(dst[0:T, 0:D], e_diag[:, i, :], x1[:, i, :], start=(i == 0), stop=(i == T - 1))
                    mm.then_inc(s_u, 1)
                    dst = bank(1, b)
                    for i in range(T):
                        mm = pe.transpose(dst[:, i * P:(i + 1) * P], pin[:, i, :], ident[:])
                    mm.then_inc(s_pT, 1)
                    dst = bank(0, b)
                    for i in range(T):
                        mm = pe.transpose(dst[0:T, i * P:(i + 1) * P], w_oth[:, i, :], ident[:])
                    mm.then_inc(s_pT, 1)
                if t in (6.5, 7):
                    k = int(t > 6.5)
                    if k == 0:
                        pe.wait_ge(s_pinT, b + 1)
                        pe.wait_ge(s_pTc, b + 1)
                        pe.wait_ge(s_uc, 2 * b + 2)
                    dst = bank(1 - k, b)
                    for i in range(2):
                        j = 2 * k + i
                        pe.matmul(dst[:, i * D:(i + 1) * D], pinT[:, j, :], x1[:, j, :], start=True, stop=False)
                        mm = pe.matmul(dst[:, i * D:(i + 1) * D], w_othT[:, j, :], u_blk[:], start=False, stop=True)
                    mm.then_inc(s_pool, 1)
                if t == 9:
                    pe.wait_ge(s_x2, (b + 1) * T)
                    for c in range(C):
                        turned(x2, bank(1 - c, b), c, s_x2T)
                if t in (9.5, 10, 13, 13.5):
                    o, side = int(t > 10), int(t in (10, 13.5))
                    if t == 9.5:
                        pe.wait_ge(s_x2Tc, (b + 1) * C)
                    w_sb = (wq_sb, wk_sb)[side]
                    dst = bank(1 - side, b)
                    for c in range(C):
                        mm = pe.matmul(dst[:], w_sb[:, c, o * P:(o + 1) * P], xT[:, c, :], start=(c == 0), stop=(c == C - 1))
                    mm.then_inc(s_qk, 1)
                if t == 14.5:
                    for k in range(2):
                        dst = bank(1 - k, b)
                        for i in range(2):
                            j = 2 * k + i
                            for c in range(C):
                                mm = pe.matmul(dst[:, i * D:(i + 1) * D], xT[:, c, j * P:(j + 1) * P], wv_sb[:, c, :],
                                               start=(c == 0), stop=(c == C - 1))
                            mm.then_inc(s_v, 1)
                    assert (p_used[0].n, p_used[1].n) == P_USES, p_used

            def scores(b, h, t, wide):
                if h % 4 == 0 and t == 0:
                    pe.wait_ge(s_stack[h // 4], (b + 1) * 32)
                i = b * (H * T) + h * T + t
                if wide or t % 2 == 0:
                    after(pe, s_max, i - 1 if wide or h + t == 0 else i - 2)
                n = S if wide else SN
                pe.matmul(scores_at(t, wide), Qs[0:KR, h, t * P:(t + 1) * P], Ks[0:KR, h, 0:n], start=True, stop=True)\
                    .then_inc(s_scores, 1)

            def scores_t(b, h, k, wide):
                if h % 4 == 0 and k == 0:
                    pe.wait_ge(s_mrow, (b * G + h // 4 + 1) * 48)
                i = b * (H * T) + h * T + k
                after(pe, s_exp, i - 1)
                pe.matmul(psT[k % 2][:], Ks[:, h, k * P:(k + 1) * P], Qs[:, h, :], start=True, stop=True)\
                    .then_inc(s_st, 1 if wide else 2)

            def output(b, h, k, wide):
                n = T if wide else TN
                if k in (0, n // 2):
                    pe.wait_ge(s_wmul, 2 * (b * H + h) + (1 if k == 0 else 2))
                if h % 4 == 0 and k == 0:
                    pe.wait_ge(s_vcopy, b * G + h // 4 + 1)
                    after(pe, s_oc, b * G + h // 4)
                r = HP * (h % 4)
                mm = pe.matmul(psO[r:r + HP, :], V[:, k, h, :], prob[:, h % RING, k, :], start=(k == 0), stop=(k == n - 1))
                if k == n - 1:
                    mm.then_inc(s_pv, 1)

            def max_turned(b, g):
                pe.wait_ge(s_max, b * (H * T) + (g + 1) * 4 * T)
                dst = fbank()
                pe.transpose(dst[0:4 * T, 0:P], mx[:, g % 2].rearrange("p h t -> p (h t)"), ident[:]).then_inc(s_mT, 1)

            def output_turned(b, g):
                pe.wait_ge(s_oc, b * G + g + 1)
                dst = fbank()
                for t in range(T):
                    mm = pe.transpose(dst[:, t * P:(t + 1) * P], oT_sb[:, t * P:(t + 1) * P], ident[:])
                mm.then_inc(s_oT, 1)

            def last_layer(b, t):
                if t == 10:
                    pe.wait_ge(s_o, (b + 1) * G)
                    for c in range(C):
                        turned(o_sb, fbank(), c, s_fT)
                if t in (10.5, 11):
                    k = int(t > 10.5)
                    if k == 0:
                        pe.wait_ge(s_fTc, 2 * C * b + C)
                    dst = fbank()
                    for i in range(2):
                        j = 2 * k + i
                        for c in range(C):
                            mm = pe.matmul(dst[:, i * D:(i + 1) * D], fT[:, c, j * P:(j + 1) * P], wo_sb[:, c, :],
                                           start=(c == 0), stop=(c == C - 1))
                    mm.then_inc(s_x3p, 1)
                if t == 11.5:
                    pe.wait_ge(s_x3, 2 * b + 2)
                    for c in range(C):
                        turned(x3, fbank(), c, s_fT)
                if t == 12:
                    pe.wait_ge(s_fTc, 2 * C * (b + 1))
                    pe.wait_ge(s_loadf, (b + 1) * LOADF * 16)
                    dst = fbank()
                    for c in range(C):
                        mm = pe.matmul(dst[0:A3, :], lw1_sb[:, c, :], fT[:, c, :], start=(c == 0), stop=(c == C - 1))
                    mm.then_inc(s_h3, 1)
                if t in (12.5, 13):
                    k = int(t > 12.5)
                    if k == 0:
                        pe.wait_ge(s_h3c, b + 1)
                    dst = fbank()
                    for i in range(2):
                        j = 2 * k + i
                        mm = pe.matmul(dst[:, i * D:(i + 1) * D], h3[:, j * P:(j + 1) * P], lw2_sb[:], start=True, stop=True)
                    mm.then_inc(s_y3, 1)

            STEPS = "T0 T1 V0 S2 T2 V1 S3 T3 V2 V3".split()

            def slots(b, is_p, is_a, is_f, span, new, old):
                for t in span:
                    if t == 0 and is_a:
                        for k in range(T // 2 if new else T):
                            scores(b, 0, k, new)
                    for step in STEPS:
                        stage, k = step[0], int(step[1])
                        if stage == "S":
                            if is_a and new:
                                scores(b, t, k, new)
                            continue
                        lag, run = {"T": (LAG_T, scores_t), "V": (LAG_V, output)}[stage]
                        if t >= lag and is_a and (new or k < TN):
                            run(b, t - lag, k, new)
                        if t < lag and is_f and (old or k < TN):
                            run(b - 1, t - lag + H, k, old)
                    if t == 0 and is_f:
                        max_turned(b - 1, 3)
                    if t in (4, 8, 12) and is_a:
                        max_turned(b, t // 4 - 1)
                    if is_f:
                        last_layer(b - 1, t - 0.5)
                    if is_p:
                        first_layers(b + 1, t - 0.5)
                    if t < 15 and is_a:
                        for k in range(T // 2 if new else T):
                            scores(b, t + 1, k, new)
                    if t in (1, 5, 9) and is_f:
                        output_turned(b - 1, t // 4 + 1)
                    if t == 13 and is_a:
                        output_turned(b, 0)
                    if is_p:
                        first_layers(b + 1, t)
                    if is_f:
                        last_layer(b - 1, t)

            def iteration(b, is_p, is_a, is_f):
                in_slots(pe, live_i, b, is_a, is_f, [*p_used, f_used],
                         lambda span, new, old: slots(b, is_p, is_a, is_f, span, new, old))

            for t in range(16):
                if t == 1:
                    pe.wait_ge(s_identb, 1)
                if t == 3:
                    pe.wait_ge(s_pooling, 16 * len(POOLING))
                if t == 4:
                    pe.wait_ge(s_vbc, 1)
                if t == 9:
                    pe.wait_ge(s_const, 16 * len(CONST))
                first_layers(0, t - 0.5)
                first_layers(0, t)
                if 1 <= t <= T * NI // CHUNK:
                    n = (t - 1) * CHUNK
                    counts(n // NI, n % NI)
            counts_t()
            pe.wait_ge(s_far, 1)
            pe.matmul(psO[0:1, 0:P], far[:], ident[:], start=True, stop=True).then_inc(s_far_row, 1)
            pe.wait_ge(s_ct_read, T)
            pe.wait_ge(s_live, 1)
            iteration(0, True, True, False)
            start = f_used.n
            with pe.Fori(FIRST, LAST) as b:
                f_used.enter(b, FIRST, F_USES)
                iteration(b, True, True, True)
            f_used.leave(LAST - FIRST, start)
            iteration(LAST, False, True, True)
            iteration(B, False, False, True)

        @block.scalar
        def _(act):
            def exps(b, h, wide):
                after(act, s_pv, b * H + h + 1 - RING)
                each = 1 if wide else 2
                for k in range(T // each):
                    act.wait_ge(s_st, b * (H * T) + h * T + each * (k + 1))
                    act.activation(prob[:, h % RING, k, :], psT[k % 2][:], ACT.Exp).then_inc(s_exp, each)

            def load_mrow(b, g):
                act.wait_ge(s_nsplit, b * G + g + 1)
                for k in range(3):
                    dst = Qs[KR + k:KR + k + 1, 4 * g:4 * g + 4, :].rearrange("o h s -> o (h s)")
                    act.dma_start(dst, nm_parts[:, k, :]).then_inc(s_mrow, 16)

            def out_copy(b, g):
                act.wait_ge(s_pv, b * H + 4 * g + 4)
                after(act, s_oT, b * G + g)
                act.copy(oT_sb[:], psO[:]).then_inc(s_oc, 1)

            def first_layers(b, t):
                if t == 0:
                    act.wait_ge(s_z, b + 1)
                    after(act, s_y, 2 * b)
                    act.activation(z_sb[:], psP[0][:], ACT.Relu, bias=bd_sb[:]).then_inc(s_zc, 1)
                    act.wait_ge(s_zc, b + 1)
                    act.sem_inc(s_p_read[0], 1)
                if t == 2.5:
                    for c in range(C):
                        act.wait_ge(s_x1T, b * C + c + 1)
                        act.copy(xT[:, c, :], psP[1 - c][:]).then_inc(s_x1Tc, 1)
                        act.wait_ge(s_x1Tc, b * C + c + 1)
                        act.sem_inc(s_p_read[1 - c], 1)
                if t == 3:
                    act.wait_ge(s_h, b + 1)
                    after(act, s_colf, b)
                    act.activation(h1[:], psP[1][0:A1, :], ACT.Tanh, bias=b1_sb[:]).then_inc(s_hc, 1)
                    act.wait_ge(s_hc, b + 1)
                    act.sem_inc(s_p_read[1], 1)
                if t == 3.5:
                    act.wait_ge(s_colf, b + 1)
                    after(act, s_arg, b)
                    act.copy(col[:], psP[1][:, 0:T]).then_inc(s_colc, 1)
                    act.wait_ge(s_colc, b + 1)
                    act.sem_inc(s_p_read[1], 1)
                if t == 5:
                    act.wait_ge(s_arg, b + 1)
                    after(act, s_pT, 2 * b)
                    after(act, s_u, b)
                    for i in range(T):
                        act.activation(pin[:, i, :], masked[:, i, :], ACT.Exp, bias=m_neg[:, i:i + 1],
                                       accum_out=sum_in[:, i:i + 1]).then_inc(s_exp1, 1)
                    act.activation(w_oth[:], oth[:], ACT.Exp).then_inc(s_exp1, 1)
                    act.activation(e_diag[:].rearrange("p a b -> p (a b)")[:, 0:T * T:T + 1], e_arg[:], ACT.Exp)\
                       .then_inc(s_exp1, 1)
                if t == 5.5:
                    act.wait_ge(s_u, b + 1)
                    after(act, s_pool, 2 * b)
                    after(act, s_x2, T * b)
                    act.copy(u_blk[:], psP[0][0:T, 0:D]).then_inc(s_uc, 1)
                    act.copy(e_sum[:], psP[0][:, D:D + T]).then_inc(s_uc, 1)
                    act.wait_ge(s_uc, 2 * b + 2)
                    act.sem_inc(s_p_read[0], 1)
                    act.wait_ge(s_pT, 2 * b + 1)
                    act.copy(pinT[:].rearrange("p a b -> p (a b)"), psP[1][:]).then_inc(s_pinT, 1)
                    act.wait_ge(s_pinT, b + 1)
                    act.sem_inc(s_p_read[1], 1)
                    act.wait_ge(s_pT, 2 * b + 2)
                    act.copy(w_othT[:].rearrange("p a b -> p (a b)"), psP[0][0:T, :]).then_inc(s_pTc, 1)
                    act.wait_ge(s_pTc, b + 1)
                    act.sem_inc(s_p_read[0], 1)
                if t == 9:
                    for c in range(C):
                        act.wait_ge(s_x2T, b * C + c + 1)
                        act.copy(xT[:, c, :], psP[1 - c][:]).then_inc(s_x2Tc, 1)
                        act.wait_ge(s_x2Tc, b * C + c + 1)
                        act.sem_inc(s_p_read[1 - c], 1)
                if t in (9.5, 10, 13, 13.5):
                    o, side = int(t > 10), int(t in (10, 13.5))
                    if side == 0:
                        after(act, s_lo, b * C)
                        after(act, s_stored[o], b * 2 * NS * 16)
                    bias, scale = ((bqs, DH ** -0.5), (bk_sb, 1.0))[side]
                    i, n = side * C + o, b * 2 * C + 2 * o + side + 1
                    act.wait_ge(s_qk, n)
                    act.activation(qk[:, i, :], psP[1 - side][:], ACT.Identity, bias=bias[:, o:o + 1], scale=scale)\
                       .then_inc(s_qkc, 1)
                    act.activation(parts[:, 0, i, :], psP[1 - side][:], ACT.Identity, bias=bias[:, o:o + 1],
                                   scale=scale).then_inc(s_qkc, 1)
                    act.wait_ge(s_qkc, 2 * n)
                    act.sem_inc(s_p_read[1 - side], 1)
                    if side == 1:
                        act.sem_inc(s_hi, 1)

                if t == 14.5:
                    after(act, s_vcopy, b * G)
                    for k in range(2):
                        act.wait_ge(s_v, 2 * C * b + 2 * k + 2)
                        act.copy(v_next[:, 2 * k:2 * k + 2, :].rearrange("p t d -> p (t d)"), psP[1 - k][:]).then_inc(s_vc, 1)
                        act.wait_ge(s_vc, 2 * b + k + 1)
                        act.sem_inc(s_p_read[1 - k], 1)

            def neg_max(b, g):
                act.wait_ge(s_mT, b * G + g + 1)
                after(act, s_nsplit, b * G + g)
                act.mul(nm[0:4 * T, :], psF[0:4 * T, 0:P], -1.0).then_inc(s_negm, 1)
                act.wait_ge(s_negm, b * G + g + 1)
                act.sem_inc(s_f_read, 1)

            def last_layer(b, t):
                if t in (10, 11.5):
                    for c in range(C):
                        i = b * 2 * C + (C if t > 10 else 0) + c + 1
                        act.wait_ge(s_fT, i)
                        if t == 10 and c == 0:
                            after(act, s_h3, b)
                        if t > 10 and c == 0:
                            act.wait_ge(s_x3p, 2 * b + 2)
                        act.copy(fT[:, c, :], psF[:]).then_inc(s_fTc, 1)
                        act.wait_ge(s_fTc, i)
                        act.sem_inc(s_f_read, 1)
                if t == 12:
                    act.wait_ge(s_h3, b + 1)
                    after(act, s_y3, 2 * b)
                    act.activation(h3[:], psF[0:A3, :], ACT.Relu, bias=lb1_sb[:]).then_inc(s_h3c, 1)
                    act.wait_ge(s_h3c, b + 1)
                    act.sem_inc(s_f_read, 1)

            def slots(b, is_p, is_a, is_f, span, new, old):
                for t in span:
                    if t >= LAG_T and is_a:
                        exps(b, t - LAG_T, new)
                    if t < LAG_T and is_f:
                        exps(b - 1, t - LAG_T + H, old)
                    if t == 1 and is_f:
                        load_mrow(b - 1, 3)
                    if t in (5, 9, 13) and is_a:
                        load_mrow(b, t // 4 - 1)
                    if t == 0 and is_f:
                        neg_max(b - 1, 3)
                    if t in (4, 8, 12) and is_a:
                        neg_max(b, t // 4 - 1)
                    if is_f:
                        last_layer(b - 1, t - 0.5)
                    if is_p:
                        first_layers(b + 1, t - 0.5)
                    if t == 12 and is_a:
                        out_copy(b, 0)
                    if t in (0, 4, 8) and is_f:
                        out_copy(b - 1, 1 + t // 4)
                    if is_p:
                        first_layers(b + 1, t)
                    if is_f:
                        last_layer(b - 1, t)

            def iteration(b, is_p, is_a, is_f):
                in_slots(act, live_i, b, is_a, is_f, [],
                         lambda span, new, old: slots(b, is_p, is_a, is_f, span, new, old))

            act.wait_ge(s_loadp, LOADP * 16)
            act.wait_ge(s_early, 16 * len(EARLY))
            act.activation(tmp8[:, 0, :], u_sb[:], ACT.Exp, scale=-5.0).then_inc(s_e1, 1)
            act.wait_ge(s_e2, 1)
            act.activation(tmp8[:, 2, :], tmp8[:, 1, :], ACT.Exp, scale=-1.0).then_inc(s_e1, 1)
            for t in range(16):
                if t == 5:
                    act.wait_ge(s_vz, 2)
                if t == 3:
                    act.wait_ge(s_pooling, 16 * len(POOLING))
                if t == 9:
                    act.wait_ge(s_bqs, 1)
                first_layers(0, t - 0.5)
                first_layers(0, t)
            for k in range(T):
                act.wait_ge(s_ct, k + 1)
                act.copy(count_t[:, k, :], psT[k % 2][:].bitcast(BF16)[:, 0:S]).then_inc(s_ct_read, 1)
            act.wait_ge(s_live, 1)
            iteration(0, True, True, False)
            with act.Fori(FIRST, LAST) as b:
                iteration(b, True, True, True)
            iteration(LAST, False, True, True)
            iteration(B, False, False, True)

        @block.vector
        def _(dve):
            seq = Count()
            SEQ = 95

            def link(ins):
                ins.then_inc(s_dve, 1)
                seq.n += 1
                dve.wait_ge(s_dve, seq.value)

            def skip(n):
                dve.sem_inc(s_dve, n)
                seq.n += n

            def each_tile(op, end):
                for t in range(T):
                    ins = op(t)
                    if t < T - 1:
                        ins.then_inc(s_dve, 1)
                        seq.n += 1
                end(ins)

            def moments(y, st):
                each_tile(lambda t: dve.bn_stats(st[:, t, :], y[:, t, :]), link)

            def variances(st, m, r):
                alone(dve, s_passed)
                each_tile(lambda t: dve.bn_aggr(m[:, t, :], st[:, t, :]), link)
                link(dve.tensor_scalar(m[:, :, 1], m[:, :, 1], EPS, None, ALU.add))
                bits = r[:].bitcast(I32)
                link(dve.tensor_scalar(bits, m[:, :, 1].bitcast(I32), 1, None, ALU.logical_shift_right))
                link(dve.tensor_scalar(bits, bits, -1.0, float(0x5F3759DF), ALU.mult, ALU.add))

            def newton(m, r, new, n):
                for _ in range(n):
                    link(dve.tensor_tensor(new[:], r[:], r[:], ALU.mult))
                    link(dve.scalar_tensor_tensor(out=new[:], in0=new[:], scalar=-0.5, in1=m[:, :, 1], op0=ALU.mult, op1=ALU.mult))
                    link(dve.scalar_tensor_tensor(out=r[:], in0=new[:], scalar=1.5, in1=r[:], op0=ALU.add, op1=ALU.mult))

            def maxima(b, h, tiles, wide):
                n, mask = (S, mask_a) if wide else (SN, unlisted)
                for t in tiles:
                    i = b * (H * T) + h * T + t
                    if wide or t % 2 == 0:
                        dve.wait_ge(s_scores, i + 1 if wide else i + 2)
                    if h % 4 == 0 and t == 0:
                        after(dve, s_mT, b * G + h // 4 - 1)
                    alone(dve, s_passed)
                    s = scores_at(t, wide)
                    dve.tensor_tensor_reduce(s, s, mask[:, t, 0:n], 1.0, NEG, ALU.add, ALU.max,
                                             mx[:, (h // 4) % 2, h % 4, t:t + 1]).then_inc(s_max, 1)

            def weight(b, h, half, wide):
                n = (T if wide else TN) // 2
                if half == 0:
                    dve.wait_ge(s_exp, b * (H * T) + (h + 1) * T)
                k = slice(half * n, (half + 1) * n)
                p = prob[:, h % RING, k].rearrange("p k s -> p (k s)")
                by = (wgt if wide else count_t)[:, k].rearrange("p k s -> p (k s)")
                dve.scalar_tensor_tensor(out=p, in0=p, scalar=-NEG, in1=by, op0=ALU.min, op1=ALU.mult).then_inc(s_wmul, 1)

            def mask_for(b):
                after(dve, s_max, b * (H * T))
                src = table[:, b, 0:4] if isinstance(b, int) else table[:, bass.ds(b, 1), 0:4].squeeze(1)
                alone(dve, s_passed)
                link(dve.tensor_copy(cur_a[:], src))
                link(dve.tensor_scalar(mask_a[:], unprior[:], cur_a[:, 1:2], None, ALU.mult))
                link(dve.scalar_tensor_tensor(out=mask_a[:], in0=unlisted[:], scalar=cur_a[:, 0:1], in1=mask_a[:],
                                              op0=ALU.mult, op1=ALU.add))

            def weights_for(b):
                after(dve, s_wmul, 2 * b * H)
                src = table[:, b, 0:4] if isinstance(b, int) else table[:, bass.ds(b, 1), 0:4].squeeze(1)
                alone(dve, s_passed)
                link(dve.tensor_copy(cur_w[:], src))
                link(dve.tensor_scalar(wgt[:], unprior_t[:], cur_w[:, 3:4], cur_w[:, 2:3], ALU.mult, ALU.add))
                link(dve.scalar_tensor_tensor(out=wgt[:], in0=count_t[:], scalar=cur_w[:, 0:1], in1=wgt[:],
                                              op0=ALU.mult, op1=ALU.add))

            def normalize(b, g):
                dve.wait_ge(s_oT, b * G + g + 1)
                if g == 0:
                    after(dve, s_fT, 2 * C * b - C)
                src = psF[:].rearrange("p (t h r) -> p t h r", t=T, h=4)
                link(dve.reciprocal(orec[:], src[:, :, :, DH]))
                dst = o_sb[:, :, g * 4 * DH:(g + 1) * 4 * DH].rearrange("p t (h r) -> p t h r", h=4)
                for t in range(T):
                    ins = dve.tensor_tensor(dst[:, t], src[:, t, :, 0:DH],
                                            orec[:, t].unsqueeze(2).to_broadcast([P, 4, DH]), ALU.mult)
                    if t < T - 1:
                        ins.then_inc(s_dve, 1)
                        seq.n += 1
                ins.then_inc(s_o, 1)
                dve.wait_ge(s_o, b * G + g + 1)
                dve.sem_inc(s_f_read, 1)

            def first_layers(b, t):
                if t == 0.5:
                    dve.wait_ge(s_xbu, 2 * b + 1)
                    for k in range(2):
                        dve.wait_ge(s_y, 2 * b + k + 1)
                        y = y_sb[:, 2 * k:2 * k + 2, :].rearrange("p t d -> p (t d)")
                        link(dve.tensor_tensor(y, psP[1 - k][:], y, ALU.add))
                        dve.sem_inc(s_p_read[1 - k], 1)
                    moments(y_sb, stats)
                    variances(stats, mv, rstd)
                if t == 1:
                    newton(mv, rstd, newt, 2)
                if t == 1.5:
                    newton(mv, rstd, newt, 1)
                    after(dve, s_pool, 2 * b)
                    each_tile(lambda t: dve.scalar_tensor_tensor(
                        out=y_sb[:, t, :], in0=y_sb[:, t, :], scalar=mv[:, t, 0:1], in1=g0_sb[:], op0=ALU.subtract, op1=ALU.mult), link)
                    dve.wait_ge(s_xbu, 2 * b + 2)
                    each_tile(lambda t: dve.scalar_tensor_tensor(
                        out=x1[:, t, :], in0=y_sb[:, t, :], scalar=rstd[:, t:t + 1], in1=x_sb[:, t, :], op0=ALU.mult, op1=ALU.add),
                        lambda ins: ins.then_inc(s_x1, 1))
                if t == 3.5:
                    dve.wait_ge(s_typ, b + 1)
                    dve.wait_ge(s_row, b + 1)
                    after(dve, s_exp1, b * (T + 2))
                    row = psP[0][:].rearrange("p (t l) -> p t l", t=T)
                    link(dve.tensor_reduce(bmax[:], row, AX_X, ALU.max))
                    alone(dve, s_passed)
                    for i in range(T):
                        ins = dve.tensor_tensor_reduce(masked[:, i, :], row[:, i, :], typ[:, 0:P], 1.0, NEG,
                                                       ALU.add, ALU.max, m_in[:, i:i + 1])
                        if i < T - 1:
                            ins.then_inc(s_dve, 1)
                            seq.n += 1
                    link(ins)
                    dve.sem_inc(s_p_read[0], 1)
                if t == 4:
                    dve.wait_ge(s_colc, b + 1)
                    link(dve.tensor_tensor(oth[:], bmax[:].unsqueeze(1).to_broadcast([P, T, T]),
                                           typ[:, P:P + T * T].rearrange("p (a b) -> p a b", a=T), ALU.add))
                    link(dve.tensor_reduce(m_oth[:], oth[:], AX_X, ALU.max))
                    link(dve.tensor_tensor(m_in[:], m_in[:], m_oth[:], ALU.max))
                    link(dve.tensor_scalar(m_neg[:], m_in[:], -1.0, None, ALU.mult))
                    link(dve.tensor_tensor(oth[:], oth[:], m_in[:].unsqueeze(2).to_broadcast([P, T, T]), ALU.subtract))
                    dve.tensor_tensor(e_arg[:], col[:], bmax[:], ALU.subtract).then_inc(s_arg, 1)
                if t == 6:
                    dve.wait_ge(s_uc, 2 * b + 2)
                    link(dve.tensor_tensor(oth[:], w_oth[:], e_sum[:].unsqueeze(1).to_broadcast([P, T, T]), ALU.mult))
                    link(dve.tensor_reduce(m_oth[:], oth[:], AX_X, ALU.add))
                    link(dve.tensor_tensor(m_oth[:], m_oth[:], sum_in[:], ALU.add))
                    link(dve.tensor_tensor(m_oth[:], m_oth[:], typ[:, P + T * T:TW], ALU.mult))
                    link(dve.reciprocal(rec[:], m_oth[:]))
                if t in (6.5, 7):
                    k = int(t > 6.5)
                    if k == 0:
                        after(dve, s_x2T, C * b)
                        after(dve, s_spill, 16 * b)
                    dve.wait_ge(s_pool, 2 * b + k + 1)
                    for j in (2 * k, 2 * k + 1):
                        dve.scalar_tensor_tensor(out=x2[:, j, :], in0=psP[1 - k][:, (j % 2) * D:(j % 2 + 1) * D],
                                                 scalar=rec[:, j:j + 1], in1=x1[:, j, :], op0=ALU.mult, op1=ALU.add)\
                           .then_inc(s_x2, 1)
                    dve.wait_ge(s_x2, b * T + 2 * k + 2)
                    dve.sem_inc(s_p_read[1 - k], 1)

            def last_layer(b, t):
                if t in (10.5, 11):
                    k = int(t > 10.5)
                    dve.wait_ge(s_x3in, b + 1)
                    dve.wait_ge(s_x3p, 2 * b + k + 1)
                    r = x3[:, 2 * k:2 * k + 2, :].rearrange("p t d -> p (t d)")
                    dve.tensor_tensor(r, psF[:], r, ALU.add).then_inc(s_x3, 1)
                    dve.wait_ge(s_x3, 2 * b + k + 1)
                    dve.sem_inc(s_f_read, 1)
                if t in (12.5, 13):
                    k = int(t > 12.5)
                    dve.wait_ge(s_x3b, b + 1)
                    dve.wait_ge(s_y3, 2 * b + k + 1)
                    y = y3[:, 2 * k:2 * k + 2, :].rearrange("p t d -> p (t d)")
                    link(dve.tensor_tensor(y, psF[:], y, ALU.add))
                    dve.sem_inc(s_f_read, 1)
                    if k:
                        moments(y3, stats3)
                if t == 13.5:
                    variances(stats3, mv3, rstd3)
                    newton(mv3, rstd3, newt3, 1)
                if t == 14:
                    newton(mv3, rstd3, newt3, 2)
                    each_tile(lambda t: dve.scalar_tensor_tensor(
                        out=y3[:, t, :], in0=y3[:, t, :], scalar=mv3[:, t, 0:1], in1=lg_sb[:], op0=ALU.subtract, op1=ALU.mult), link)
                if t == 14.5:
                    dve.wait_ge(s_x3lb, b + 1)
                    each_tile(lambda t: dve.scalar_tensor_tensor(
                        out=y3[:, t, :], in0=y3[:, t, :], scalar=rstd3[:, t:t + 1], in1=x3[:, t, :], op0=ALU.mult, op1=ALU.add),
                        lambda ins: ins.then_inc(s_out_sb, 1))

            def slots(b, is_p, is_a, is_f, span, new, old):
                for t in span:
                    if is_a and t == 0:
                        if new:
                            mask_for(b)
                        else:
                            skip(3)
                    for half in range(2):
                        if is_a:
                            if new:
                                maxima(b, t, range(2 * half, 2 * half + 2), new)
                            elif half == 0:
                                maxima(b, t, range(T), new)
                        if t >= LAG_W and is_a:
                            weight(b, t - LAG_W, half, new)
                        if t < LAG_W and is_f:
                            weight(b - 1, t - LAG_W + H, half, old)
                        if half == 0:
                            if t in (2, 6, 10) and is_f:
                                normalize(b - 1, t // 4 + 1)
                            if t == 14 and is_a:
                                normalize(b, 0)
                            if is_p:
                                first_layers(b + 1, t - 1)
                            if is_f:
                                last_layer(b - 1, t - 1)
                        else:
                            if is_p:
                                first_layers(b + 1, t - 0.5)
                            if is_f:
                                last_layer(b - 1, t - 0.5)
                    if t == LAG_W - 1 and is_a:
                        if new:
                            weights_for(b)
                        else:
                            skip(3)
                alone(dve, s_passed)

            def iteration(b, is_p, is_a, is_f):
                in_slots(dve, live_i, b, is_a, is_f, [seq],
                         lambda span, new, old: slots(b, is_p, is_a, is_f, span, new, old))

            def hots(t, first):
                for i in range(first, first + CHUNK):
                    n = t * NI + i
                    m = n - 8
                    if m >= 0:
                        if m % NI == NI - 1:
                            dve.wait_ge(s_cnt, m // NI + 1)
                        else:
                            dve.wait_ge(s_hot_used, (m // NI) * (NI - 1) + m % NI + 1)
                    dve.tensor_scalar(hot[:, n % 8, :], iota_h, idx_f[:, t, i:i + 1], None, ALU.is_equal).then_inc(s_hot, 1)
                if first + CHUNK < NI:
                    return
                dve.wait_ge(s_cnt, t + 1)
                link(dve.tensor_scalar(unlisted[:, t, :], psS[t % 2][:], 0.5, NEG, ALU.is_lt, ALU.mult))
                dve.tensor_copy(count_sb[:, t, :], psS[t % 2][:]).then_inc(s_cnt_read, 1)

            link(dve.memset(V[:], 0.0))
            dve.memset(V[:, :, :, DH:DH + 1], 1.0).then_inc(s_vz, 1)
            dve.wait_ge(s_vz, 1)
            link(dve.memset(e_diag[:], 0.0))
            dve.sem_inc(s_vz, 1)
            dve.wait_ge(s_early, 16 * len(EARLY))
            link(dve.tensor_copy(idx_f[:], idx_i[:]))
            link(dve.tensor_copy(idx_m[:], idx_ok[:]))
            link(dve.tensor_scalar(iota_f[:, 0:T * NI], idx_f[:].rearrange("p t i -> p (t i)"), 0.0, float(S), ALU.is_lt, ALU.mult))
            link(dve.tensor_tensor(idx_f[:].rearrange("p t i -> p (t i)"), idx_f[:].rearrange("p t i -> p (t i)"),
                                   iota_f[:, 0:T * NI], ALU.add))
            link(dve.tensor_scalar(idx_f[:], idx_f[:], 0.0, float(S - 1), ALU.max, ALU.min))
            link(dve.scalar_tensor_tensor(out=idx_f[:], in0=idx_f[:], scalar=1.0, in1=idx_m[:], op0=ALU.add, op1=ALU.mult))
            link(dve.tensor_scalar(idx_f[:], idx_f[:], -1.0, None, ALU.add))
            dve.sem_inc(s_iota, 1)
            dve.tensor_reduce(far[:], idx_f[:].rearrange("p t i -> p (t i)"), AX_X, ALU.max).then_inc(s_far, 1)
            dve.wait_ge(s_iota, 2)
            link(dve.tensor_copy(iota_h, iota_f))
            dve.wait_ge(s_ident, 2)
            link(dve.tensor_copy(identb[:], ident[:]))
            dve.sem_inc(s_identb, 1)
            dve.wait_ge(s_e1, 1)
            link(dve.tensor_scalar(tmp8[:, 0, :], tmp8[:, 0, :], 10.0, None, ALU.mult))
            link(dve.tensor_scalar(table[:, :, 0], tmp8[:, 0, :], 1.0, None, ALU.is_ge))
            dve.tensor_scalar(tmp8[:, 1, :], tmp8[:, 0, :], 1.0, None, ALU.min).then_inc(s_e2, 1)
            dve.wait_ge(s_e1, 2)
            dve.wait_ge(s_e2, 1)
            link(dve.tensor_scalar(table[:, :, 2], table[:, :, 0], -1.0, 1.0, ALU.mult, ALU.add))
            link(dve.scalar_tensor_tensor(out=table[:, :, 1], in0=tmp8[:, 1, :], scalar=-1.0, in1=table[:, :, 2],
                                          op0=ALU.mult, op1=ALU.mult))
            link(dve.scalar_tensor_tensor(out=table[:, :, 3], in0=tmp8[:, 2, :], scalar=-1.0, in1=table[:, :, 2],
                                          op0=ALU.add, op1=ALU.mult))
            link(dve.tensor_copy(tmp8[:, 0, :], ty_i[:]))
            link(dve.tensor_scalar(table[:, :, 4], tmp8[:, 0, :], 0.0, None, ALU.is_equal))
            link(dve.tensor_scalar(table[:, :, 5], tmp8[:, 0, :], 1.0, None, ALU.is_equal))
            link(dve.tensor_tensor(tmp8[:, 1, :], table[:, :, 4], table[:, :, 5], ALU.add))
            link(dve.tensor_scalar(table[:, :, 6], tmp8[:, 1, :], -1.0, 1.0, ALU.mult, ALU.add))
            dve.sem_inc(s_types, 1)
            for t in range(16):
                first_layers(0, t - 0.5)
                first_layers(0, t)
                if 1 <= t <= T * NI // CHUNK:
                    n = (t - 1) * CHUNK
                    hots(n // NI, n % NI)
                if t == 3:
                    dve.wait_ge(s_pooling, 16 * len(POOLING))
                    link(dve.tensor_scalar(vbc[:], ones[0:A1, :], v_sb[:], None, ALU.mult))
                    dve.sem_inc(s_vbc, 1)
                if t == 8:
                    dve.wait_ge(s_const, 16 * len(CONST))
                    link(dve.tensor_scalar(bqs[:], bq_sb[:], DH ** -0.5, None, ALU.mult))
                    dve.sem_inc(s_bqs, 1)
                if t == 10:
                    link(dve.tensor_copy(unprior[:], blk8))
                    link(dve.tensor_scalar(unprior[:], unprior[:], -1.0, 1.0, ALU.mult, ALU.add))
                    link(dve.tensor_copy(unprior_t[:], blkt8))
                    link(dve.tensor_scalar(unprior_t[:], unprior_t[:], -1.0, 1.0, ALU.mult, ALU.add))
            link(dve.memset(Ks[KR:KR + 3, :, :], 1.0))
            dve.wait_ge(s_far_row, 1)
            link(dve.tensor_reduce(far[0:1, :], psO[0:1, 0:P], AX_X, ALU.max))
            link(dve.tensor_scalar(far[0:1, :], far[0:1, :], float(SN), None, ALU.is_ge))
            link(dve.tensor_scalar(live_i[:], table[0:1, :, 2], far[0:1, :], None, ALU.max))
            dve.sem_inc(s_live, 1)
            dve.wait_ge(s_ct_read, T)
            iteration(0, True, True, False)
            start = seq.n
            with dve.Fori(FIRST, LAST) as b:
                seq.enter(b, FIRST, SEQ)
                iteration(b, True, True, True)
            seq.leave(LAST - FIRST, start)
            iteration(LAST, False, True, True)
            iteration(B, False, False, True)

        @block.gpsimd
        def _(pool):
            seq = Count()
            SEQ = 29

            def link(ins):
                ins.then_inc(s_pool_seq, 1)
                seq.n += 1
                pool.wait_ge(s_pool_seq, seq.value)

            def biased(b):
                pool.wait_ge(s_loadp, (b + 1) * LOADP * 16)
                pool.tensor_tensor(y_sb[:], x_sb[:], bc(bu_sb[:], T), ALU.add).then_inc(s_xbu, 1)
                pool.wait_ge(s_xbu, 2 * b + 1)
                pool.tensor_tensor(x_sb[:], x_sb[:], bc(be0_sb[:], T), ALU.add).then_inc(s_xbu, 1)
                pool.wait_ge(s_xbu, 2 * b + 2)

            def types_for(b):
                after(pool, s_exp1, b * (T + 2))
                after(pool, s_x2, b * T)
                src = table[:, b, 4:7] if isinstance(b, int) else table[:, bass.ds(b, 1), 4:7].squeeze(1)
                alone(pool, s_passed_pool)
                link(pool.tensor_copy(cur_m[:, 4:7], src))
                alone(pool, s_passed_pool)
                link(pool.tensor_scalar(typ[:], type_tab[:, 0, :], cur_m[:, 4:5], None, ALU.mult))
                for k in (1, 2):
                    alone(pool, s_passed_pool)
                    link(pool.tensor_scalar(typ2[:], type_tab[:, k, :], cur_m[:, 4 + k:5 + k], None, ALU.mult))
                    ins = pool.tensor_tensor(typ[:], typ[:], typ2[:], ALU.add)
                    if k == 1:
                        link(ins)
                ins.then_inc(s_typ, 1)
                pool.wait_ge(s_typ, b + 1)

            def first_layers(b, t):
                if t == 0:
                    types_for(b)
                if t in (10, 14):
                    o = (t - 10) // 4
                    i = b * C + o + 1
                    pool.wait_ge(s_hi, i)
                    pool.tensor_tensor(qk[:, o::C], qk[:, o::C], parts[:, 0, o::C], ALU.subtract).then_inc(s_rest, 1)
                    pool.wait_ge(s_rest, i)
                    alone(pool, s_passed_pool)
                    pool.tensor_copy(parts[:, 1, o::C], qk[:, o::C]).then_inc(s_mid, 1)
                    pool.wait_ge(s_mid, i)
                    pool.tensor_tensor(parts[:, 2, o::C], qk[:, o::C], parts[:, 1, o::C], ALU.subtract).then_inc(s_lo, 1)
                    pool.wait_ge(s_lo, i)

            def split_max(b, g):
                pool.wait_ge(s_negm, b * G + g + 1)
                after(pool, s_mrow, (b * G + g) * 48)
                a = nm[0:4 * T, :]
                alone(pool, s_passed_pool)
                link(pool.tensor_copy(nm_parts[:, 0, :], a))
                link(pool.tensor_tensor(a, a, nm_parts[:, 0, :], ALU.subtract))
                alone(pool, s_passed_pool)
                link(pool.tensor_copy(nm_parts[:, 1, :], a))
                pool.tensor_tensor(nm_parts[:, 2, :], a, nm_parts[:, 1, :], ALU.subtract).then_inc(s_nsplit, 1)
                pool.wait_ge(s_nsplit, b * G + g + 1)

            def v_copy(b, g):
                if g == 0:
                    pool.wait_ge(s_vc, 2 * b + 2)
                after(pool, s_pv, b * H + 4 * g + 4 - H)
                for t in range(T):
                    src, bias = (a[:, g * 4 * DH:(g + 1) * 4 * DH].rearrange("p (h r) -> p h r", h=4)
                                 for a in (v_next[:, t], bv_sb))
                    ins = pool.tensor_tensor(V[:, t, 4 * g:4 * g + 4, 0:DH], src, bias, ALU.add)
                    if t < T - 1:
                        ins.then_inc(s_pool_seq, 1)
                        seq.n += 1
                ins.then_inc(s_vcopy, 1)
                pool.wait_ge(s_vcopy, b * G + g + 1)

            def last_layer(b, t):
                if t == 8:
                    pool.wait_ge(s_loadf, (b + 1) * LOADF * 16)
                    pool.tensor_tensor(x3[:], x3[:], bc(bo_sb[:], T), ALU.add).then_inc(s_x3in, 1)
                if t == 11:
                    pool.wait_ge(s_x3, 2 * b + 2)
                    after(pool, s_out, 16 * b)
                    pool.tensor_tensor(y3[:], x3[:], bc(lb2_sb[:], T), ALU.add).then_inc(s_x3b, 1)
                    pool.wait_ge(s_x3b, b + 1)
                if t == 12:
                    pool.wait_ge(s_fT, 2 * C * (b + 1))
                    pool.tensor_tensor(x3[:], x3[:], bc(lb_sb[:], T), ALU.add).then_inc(s_x3lb, 1)

            def iteration(b, is_p, is_a, is_f, more=True):
                for t in range(16):
                    if t == 0 and is_f:
                        split_max(b - 1, 3)
                    if t in (4, 8, 12) and is_a:
                        split_max(b, t // 4 - 1)
                    if t == 5 and is_a:
                        v_copy(b, 0)
                        v_copy(b, 1)
                    if t in (7, 13) and is_a:
                        v_copy(b, 2 + t // 13)
                    if is_f:
                        last_layer(b - 1, t)
                    if is_p:
                        first_layers(b + 1, t)
                        if t == 8 and more:
                            biased(b + 2)

            link(pool.memset(ident[:], 0.0))
            pool.affine_select(out=ident[:], in_=ident[:], compare_op=ALU.not_equal, fill=1.0, base=0,
                               pattern=[[-1, P]], channel_multiplier=1).then_inc(s_ident, 1)
            pool.memset(ones[:], 1.0).then_inc(s_ident, 1)
            link(pool.memset(type_tab[:], 0.0))
            for k, (op, sign, off) in enumerate(((ALU.is_ge, 1, 0), (ALU.is_ge, -1, 0), (ALU.not_equal, 1, 0))):
                link(pool.affine_select(out=type_tab[:, k, 0:P], in_=type_tab[:, k, 0:P], compare_op=op, fill=NEG,
                                        base=0, pattern=[[-sign, P]], channel_multiplier=sign))
                m = type_tab[:, k, P:P + T * T].rearrange("p (a b) -> p a b", a=T)
                link(pool.affine_select(out=m, in_=m, compare_op=op, fill=NEG, base=0 if k == 2 else -1,
                                        pattern=[[sign, T], [-sign, T]], channel_multiplier=0))
            for k, (base, step) in enumerate(((1, 1), (S, -1))):
                link(pool.iota(type_tab[:, k, P + T * T:TW], [[step * P, T]], base=base, channel_multiplier=step,
                               allow_small_or_imprecise_dtypes=True))
            link(pool.memset(type_tab[:, 2, P + T * T:TW], float(S - 1)))
            pool.wait_ge(s_iota, 1)
            pool.iota(iota_f, [[1, S]], base=0, channel_multiplier=0,
                      allow_small_or_imprecise_dtypes=True).then_inc(s_iota, 1)
            biased(0)
            pool.wait_ge(s_types, 1)
            for t in range(16):
                first_layers(0, t)
                if t == 8:
                    biased(1)
            pool.wait_ge(s_const, 16 * len(CONST))
            iteration(0, True, True, False)
            start = seq.n
            with pool.Fori(FIRST, LAST - 1) as b:
                seq.enter(b, FIRST, SEQ)
                iteration(b, True, True, True)
            seq.leave(LAST - 1 - FIRST, start)
            iteration(LAST - 1, True, True, True, more=False)
            iteration(LAST, False, True, True)
            iteration(B, False, False, True)


_INS = ['x', 'xt', 'profile', 'prompt', 'indices', 'u_prev', 'language', 'blocked', 'blocked_t', 'index_ok',
        'wd', 'bd', 'wu', 'bu', 'ln0_g', 'ln0_b', 'w1', 'b1', 'v', 'wq_t', 'bq', 'wk_t', 'bk', 'wv_t', 'bv', 'wo_t', 'bo',
        'lw1', 'lb1', 'lw2', 'lb2', 'lg', 'lb']


def kernel(x, itok_B_0_6, itok_B_0_2, itok_Sx32_0_1023, condB_uprev, itok_B_0_8, mask_SxS_bk0, mask_Sx32_bk1,
           L0_cond_down_w, L0_cond_down_b, L0_cond_up_w, L0_cond_up_b, L0_cond_ln_g, L0_cond_ln_b,
           L1_cond_W1, L1_cond_b1, L1_cond_v, L2_cond_Wq, L2_cond_bq, L2_cond_Wk, L2_cond_bk, L2_cond_Wv, L2_cond_bv,
           L2_cond_Wo, L2_cond_bo, L3_cond_W1, L3_cond_b1, L3_cond_W2, L3_cond_b2, L3_cond_gamma, L3_cond_beta):
    import numpy as np
    import concourse.bacc as bacc
    from concourse import mybir as mb
    from concourse.bass_utils import run_bass_kernel_spmd as run

    x = np.asarray(x)
    mask = np.asarray(mask_SxS_bk0)
    data = dict(zip(_INS, [
        x, x.transpose(0, 2, 1), itok_B_0_6, itok_B_0_2, itok_Sx32_0_1023, condB_uprev, itok_B_0_8,
        mask, mask.T, mask_Sx32_bk1,
        L0_cond_down_w, L0_cond_down_b, L0_cond_up_w, L0_cond_up_b, L0_cond_ln_g, L0_cond_ln_b,
        L1_cond_W1, L1_cond_b1, L1_cond_v, np.asarray(L2_cond_Wq).T, np.asarray(L2_cond_bq).reshape(-1, P).T, np.asarray(L2_cond_Wk).T,
        np.asarray(L2_cond_bk).reshape(-1, P).T,
        np.asarray(L2_cond_Wv).T, L2_cond_bv, np.asarray(L2_cond_Wo).T, L2_cond_bo,
        L3_cond_W1, L3_cond_b1, L3_cond_W2, L3_cond_b2, L3_cond_gamma, L3_cond_beta]))
    nc = bacc.Bacc("TRN2", target_bir_lowering=False, num_devices=1)
    arrays, args = {}, []
    for name in _INS:
        a = np.ascontiguousarray(data[name])
        arrays[f"in_{name}"] = a
        args.append(nc.dram_tensor(f"in_{name}", a.shape, mb.dt.from_np(a.dtype), kind="ExternalInput").ap())
    o = nc.dram_tensor("out_0", x.shape, mb.dt.from_np(x.dtype), kind="ExternalOutput").ap()
    cond_resid(nc, *args, o)
    r = run(nc, [arrays], core_ids=[0])
    return r.results[0]["out_0"]
```
